# Optimizing a Trainium2 kernel written in Bass

```python
import numpy as np
import jax
import jax.numpy as jnp

def _softmax(x, axis=-1):
    return jax.nn.softmax(x, axis=axis)

def _gelu(x):
    return jax.nn.gelu(x, approximate=True)

def _silu(x):
    return jax.nn.silu(x)

def _sigmoid(x):
    return jax.nn.sigmoid(x)

def _layernorm(x, axis=-1, eps=1e-05):
    m = jnp.mean(x, axis=axis, keepdims=True)
    v = jnp.var(x, axis=axis, keepdims=True)
    return (x - m) / jnp.sqrt(v + eps)

def _scatter_add(tgt, idx, src, axis=0):
    return tgt.at[idx].add(src)

def _segment_sum(src, seg, n):
    return jax.ops.segment_sum(src, seg, n)
kernel_name = 'mk_vit_tower_postln_d2_tok_img768_r4_a0de96'

def setup_inputs(seed: int=0):
    np.random.seed(seed)
    _w = jnp.asarray

    def _rec_inputs():
        import jax
        import jax.numpy as jnp
        _rk = jax.random.key(seed)
        x = 7.57192e-06 + 1.00007 * jax.random.normal(jax.random.fold_in(_rk, 1), (64, 3, 96, 96), jnp.float32)
        return x
    x = _rec_inputs()

    def _L0_tok_setup():
        import jax, jax.numpy as jnp
        import numpy as np
        PATCH = 16

        def _shift2d(x, shift):
            l, r, t, b = shift
            H, W = (x.shape[2], x.shape[3])
            xp = jnp.pad(x, ((0, 0), (0, 0), (max(t, 0), max(b, 0)), (max(l, 0), max(r, 0))))
            h0 = max(-t, 0)
            w0 = max(-l, 0)
            return xp[:, :, h0:h0 + H, w0:w0 + W]
        key = jax.random.key(seed)
        k1, k2 = jax.random.split(key)
        B, C, H, W = (64, 3, 224, 224)
        dim = 192
        patch_dim = PATCH * PATCH * 5 * C
        x = jax.random.normal(k1, (B, C, H, W), dtype=jnp.float32)
        ln_weight = jnp.ones((patch_dim,), dtype=jnp.float32)
        ln_bias = jnp.zeros((patch_dim,), dtype=jnp.float32)
        proj_weight = jax.random.normal(k2, (dim, patch_dim), dtype=jnp.float32) * patch_dim ** (-0.5)
        proj_bias = jnp.zeros((dim,), dtype=jnp.float32)
        return {'x': x, 'ln_weight': ln_weight, 'ln_bias': ln_bias, 'proj_weight': proj_weight, 'proj_bias': proj_bias}
    _L0_tok_all = _L0_tok_setup()
    _L0_tok_in = {k: v for k, v in _L0_tok_all.items() if k in ('ln_weight', 'ln_bias', 'proj_weight', 'proj_bias')}
    del _L0_tok_all

    def _L0_attn_setup():
        import jax, jax.numpy as jnp
        import numpy as np
        B, L, D = (4, 512, 192)
        H, K = (12, 9)
        IPG = D // H
        PAD = (K - 1) // 2

        def _sdconv(query, dw_w, pw_w, pw_b, ak_w, ak_b, pt_w, pt_b):
            b, l, d = query.shape
            x = query.transpose(0, 2, 1)
            dw = jax.lax.conv_general_dilated(x, dw_w, window_strides=(1,), padding=[(PAD, PAD)], feature_group_count=d, dimension_numbers=('NCH', 'OIH', 'NCH'))
            dwg = dw.reshape(b, H, IPG, l)
            pw = jnp.einsum('bhil,hoi->bhol', dwg, pw_w).reshape(b, d, l) + pw_b[None, :, None]
            key_conv_attn = pw.transpose(0, 2, 1)
            conv_attn = key_conv_attn * query
            ca = conv_attn.reshape(b, l, H, IPG)
            kern = jnp.einsum('blhi,hki->blhk', ca, ak_w) + ak_b.reshape(H, K)
            w = jax.nn.softmax(kern, axis=-1)
            v = query @ pt_w.T + pt_b
            vp = jnp.pad(v, ((0, 0), (PAD, PAD), (0, 0)))
            idx = jnp.arange(l)[:, None] + jnp.arange(K)[None, :]
            win = vp[:, idx]
            winh = win.reshape(b, l, K, H, IPG)
            out = jnp.einsum('blkhd,blhk->blhd', winh, w).reshape(b, l, d)
            return out
        key = jax.random.key(seed)
        ks = jax.random.split(key, 8)
        s = lambda k, shape, scale: jax.random.normal(k, shape, dtype=jnp.float32) * scale
        return {'query': s(ks[0], (B, L, D), 1.0), 'dw_w': s(ks[1], (D, 1, K), 0.1), 'pw_w': s(ks[2], (H, IPG, IPG), 0.05), 'pw_b': s(ks[3], (D,), 0.02), 'ak_w': s(ks[4], (H, K, IPG), 0.05), 'ak_b': s(ks[5], (H * K,), 0.02), 'pt_w': s(ks[6], (D, D), 0.02), 'pt_b': s(ks[7], (D,), 0.02)}
    _L0_attn_all = _L0_attn_setup()
    _L0_attn_in = {k: v for k, v in _L0_attn_all.items() if k in ('dw_w', 'pw_w', 'pw_b', 'ak_w', 'ak_b', 'pt_w', 'pt_b')}
    del _L0_attn_all

    def _L0_ffn_setup():
        import jax, jax.numpy as jnp
        import numpy as np
        DIM = 192
        HID = 512
        E = 8
        TOP_K = 2

        def _ffn(t, a, b, c):
            return jax.nn.silu(t @ a.T) * (t @ c.T) @ b.T
        key = jax.random.key(seed)
        ks = jax.random.split(key, 9)
        s = 0.02
        return {'x': jax.random.normal(ks[0], (2, 256, DIM), dtype=jnp.float32), 'gate_w': jax.random.normal(ks[1], (E, DIM), dtype=jnp.float32) * s, 'w1': jax.random.normal(ks[2], (E, HID, DIM), dtype=jnp.float32) * s, 'w2': jax.random.normal(ks[3], (E, DIM, HID), dtype=jnp.float32) * s, 'w3': jax.random.normal(ks[4], (E, HID, DIM), dtype=jnp.float32) * s, 'ws1': jax.random.normal(ks[5], (HID, DIM), dtype=jnp.float32) * s, 'ws2': jax.random.normal(ks[6], (DIM, HID), dtype=jnp.float32) * s, 'ws3': jax.random.normal(ks[7], (HID, DIM), dtype=jnp.float32) * s}
    _L0_ffn_all = _L0_ffn_setup()
    _L0_ffn_in = {k: v for k, v in _L0_ffn_all.items() if k in ('gate_w', 'w1', 'w2', 'w3', 'ws1', 'ws2', 'ws3')}
    del _L0_ffn_all

    def _L1_attn_setup():
        import jax, jax.numpy as jnp
        import numpy as np
        DIM = 192
        HEADS = 12
        DIM_HEAD = 64
        INNER = HEADS * DIM_HEAD
        L = 64
        EPS = 1e-08
        key = jax.random.key(seed)
        k1, k2, k3, k4 = jax.random.split(key, 4)
        x = jax.random.normal(k1, (2, 1024, DIM), dtype=jnp.float32)
        w_qkv = jax.random.normal(k2, (3 * INNER, DIM), dtype=jnp.float32) * DIM ** (-0.5)
        w_out = jax.random.normal(k3, (DIM, INNER), dtype=jnp.float32) * INNER ** (-0.5)
        b_out = jax.random.normal(k4, (DIM,), dtype=jnp.float32) * 0.01
        scale = jnp.full((HEADS,), np.log2(L * L - L), dtype=jnp.float32)
        return {'x': x, 'w_qkv': w_qkv, 'w_out': w_out, 'b_out': b_out, 'scale': scale}
    _L1_attn_all = _L1_attn_setup()
    _L1_attn_in = {k: v for k, v in _L1_attn_all.items() if k in ('w_qkv', 'w_out', 'b_out', 'scale')}
    del _L1_attn_all

    def _L1_ffn_setup():
        import jax, jax.numpy as jnp
        import numpy as np
        D_MODEL, D_FF, N_EXPERTS, TOP_K = (192, 768, 8, 2)
        B, S = (2, 256)
        LN_EPS = 1e-05

        def _layernorm(x, gamma, beta):
            mu = jnp.mean(x, axis=-1, keepdims=True)
            var = jnp.mean(jnp.square(x - mu), axis=-1, keepdims=True)
            return (x - mu) * jax.lax.rsqrt(var + LN_EPS) * gamma + beta
        key = jax.random.key(seed)
        k1, k2, k3, k4 = jax.random.split(key, 4)
        return {'hidden_states': jax.random.normal(k1, (B, S, D_MODEL), dtype=jnp.float32), 'ln_gamma': jnp.ones((D_MODEL,), dtype=jnp.float32), 'ln_beta': jnp.zeros((D_MODEL,), dtype=jnp.float32), 'router_w': jax.random.normal(k2, (D_MODEL, N_EXPERTS), dtype=jnp.float32) * 0.02, 'w1': jax.random.normal(k3, (N_EXPERTS, D_MODEL, D_FF), dtype=jnp.float32) * 0.02, 'w2': jax.random.normal(k4, (N_EXPERTS, D_FF, D_MODEL), dtype=jnp.float32) * 0.02}
    _L1_ffn_all = _L1_ffn_setup()
    _L1_ffn_in = {k: v for k, v in _L1_ffn_all.items() if k in ('ln_gamma', 'ln_beta', 'router_w', 'w1', 'w2')}
    del _L1_ffn_all
    return {'x': x, 'L0_tok_ln_weight': _L0_tok_in['ln_weight'], 'L0_tok_ln_bias': _L0_tok_in['ln_bias'], 'L0_tok_proj_weight': _L0_tok_in['proj_weight'], 'L0_tok_proj_bias': _L0_tok_in['proj_bias'], 'L0_attn_dw_w': _L0_attn_in['dw_w'], 'L0_attn_pw_w': _L0_attn_in['pw_w'], 'L0_attn_pw_b': _L0_attn_in['pw_b'], 'L0_attn_ak_w': _L0_attn_in['ak_w'], 'L0_attn_ak_b': _L0_attn_in['ak_b'], 'L0_attn_pt_w': _L0_attn_in['pt_w'], 'L0_attn_pt_b': _L0_attn_in['pt_b'], 'L0_ffn_gate_w': _L0_ffn_in['gate_w'], 'L0_ffn_w1': _L0_ffn_in['w1'], 'L0_ffn_w2': _L0_ffn_in['w2'], 'L0_ffn_w3': _L0_ffn_in['w3'], 'L0_ffn_ws1': _L0_ffn_in['ws1'], 'L0_ffn_ws2': _L0_ffn_in['ws2'], 'L0_ffn_ws3': _L0_ffn_in['ws3'], 'L1_attn_w_qkv': _L1_attn_in['w_qkv'], 'L1_attn_w_out': _L1_attn_in['w_out'], 'L1_attn_b_out': _L1_attn_in['b_out'], 'L1_attn_scale': _L1_attn_in['scale'], 'L1_ffn_ln_gamma': _L1_ffn_in['ln_gamma'], 'L1_ffn_ln_beta': _L1_ffn_in['ln_beta'], 'L1_ffn_router_w': _L1_ffn_in['router_w'], 'L1_ffn_w1': _L1_ffn_in['w1'], 'L1_ffn_w2': _L1_ffn_in['w2']}

def reference(x, L0_tok_ln_weight, L0_tok_ln_bias, L0_tok_proj_weight, L0_tok_proj_bias, L0_attn_dw_w, L0_attn_pw_w, L0_attn_pw_b, L0_attn_ak_w, L0_attn_ak_b, L0_attn_pt_w, L0_attn_pt_b, L0_ffn_gate_w, L0_ffn_w1, L0_ffn_w2, L0_ffn_w3, L0_ffn_ws1, L0_ffn_ws2, L0_ffn_ws3, L1_attn_w_qkv, L1_attn_w_out, L1_attn_b_out, L1_attn_scale, L1_ffn_ln_gamma, L1_ffn_ln_beta, L1_ffn_router_w, L1_ffn_w1, L1_ffn_w2):
    import jax
    import jax.numpy as jnp

    def _L0_tok_ref(x, ln_weight, ln_bias, proj_weight, proj_bias):
        import jax, jax.numpy as jnp
        import numpy as np
        PATCH = 16

        def _shift2d(x, shift):
            l, r, t, b = shift
            H, W = (x.shape[2], x.shape[3])
            xp = jnp.pad(x, ((0, 0), (0, 0), (max(t, 0), max(b, 0)), (max(l, 0), max(r, 0))))
            h0 = max(-t, 0)
            w0 = max(-l, 0)
            return xp[:, :, h0:h0 + H, w0:w0 + W]
        shifts = ((1, -1, 0, 0), (-1, 1, 0, 0), (0, 0, 1, -1), (0, 0, -1, 1))
        xc = jnp.concatenate([x] + [_shift2d(x, s) for s in shifts], axis=1)
        B, C5, H, W = xc.shape
        p = PATCH
        h, w = (H // p, W // p)
        t = xc.reshape(B, C5, h, p, w, p)
        t = t.transpose(0, 2, 4, 3, 5, 1).reshape(B, h * w, p * p * C5)
        mu = jnp.mean(t, axis=-1, keepdims=True)
        var = jnp.mean(jnp.square(t - mu), axis=-1, keepdims=True)
        tn = (t - mu) * jax.lax.rsqrt(var + 1e-05) * ln_weight + ln_bias
        return jnp.einsum('bnk,dk->bnd', tn, proj_weight) + proj_bias

    def _L0_attn_ref(query, dw_w, pw_w, pw_b, ak_w, ak_b, pt_w, pt_b):
        import jax, jax.numpy as jnp
        import numpy as np
        B, L, D = (4, 512, 192)
        H, K = (12, 9)
        IPG = D // H
        PAD = (K - 1) // 2

        def _sdconv(query, dw_w, pw_w, pw_b, ak_w, ak_b, pt_w, pt_b):
            b, l, d = query.shape
            x = query.transpose(0, 2, 1)
            dw = jax.lax.conv_general_dilated(x, dw_w, window_strides=(1,), padding=[(PAD, PAD)], feature_group_count=d, dimension_numbers=('NCH', 'OIH', 'NCH'))
            dwg = dw.reshape(b, H, IPG, l)
            pw = jnp.einsum('bhil,hoi->bhol', dwg, pw_w).reshape(b, d, l) + pw_b[None, :, None]
            key_conv_attn = pw.transpose(0, 2, 1)
            conv_attn = key_conv_attn * query
            ca = conv_attn.reshape(b, l, H, IPG)
            kern = jnp.einsum('blhi,hki->blhk', ca, ak_w) + ak_b.reshape(H, K)
            w = jax.nn.softmax(kern, axis=-1)
            v = query @ pt_w.T + pt_b
            vp = jnp.pad(v, ((0, 0), (PAD, PAD), (0, 0)))
            idx = jnp.arange(l)[:, None] + jnp.arange(K)[None, :]
            win = vp[:, idx]
            winh = win.reshape(b, l, K, H, IPG)
            out = jnp.einsum('blkhd,blhk->blhd', winh, w).reshape(b, l, d)
            return out
        return _sdconv(query, dw_w, pw_w, pw_b, ak_w, ak_b, pt_w, pt_b)

    def _L0_ffn_ref(x, gate_w, w1, w2, w3, ws1, ws2, ws3):
        import jax, jax.numpy as jnp
        import numpy as np
        DIM = 192
        HID = 512
        E = 8
        TOP_K = 2

        def _ffn(t, a, b, c):
            return jax.nn.silu(t @ a.T) * (t @ c.T) @ b.T
        B, S, D = x.shape
        xf = x.reshape(-1, D)
        T = xf.shape[0]
        logits = xf @ gate_w.T
        scores = jax.nn.softmax(logits, axis=-1)
        topk_w, topk_idx = jax.lax.top_k(scores, TOP_K)
        topk_w = topk_w / (topk_w.sum(-1, keepdims=True) + 1e-20)
        cw = jnp.zeros((T, E), xf.dtype).at[jnp.arange(T)[:, None], topk_idx].add(topk_w)
        y = jnp.zeros_like(xf)
        for e in range(E):
            y = y + cw[:, e:e + 1] * _ffn(xf, w1[e], w2[e], w3[e])
        y = y + _ffn(xf, ws1, ws2, ws3)
        return y.reshape(B, S, D)

    def _L1_attn_ref(x, w_qkv, w_out, b_out, scale):
        import jax, jax.numpy as jnp
        import numpy as np
        DIM = 192
        HEADS = 12
        DIM_HEAD = 64
        INNER = HEADS * DIM_HEAD
        L = 64
        EPS = 1e-08
        b, n, d = x.shape
        h, dh = (HEADS, DIM_HEAD)
        qkv = x @ w_qkv.T
        q, k, v = jnp.split(qkv, 3, axis=-1)
        q, k, v = (t.reshape(b, n, h, dh).transpose(0, 2, 1, 3) for t in (q, k, v))
        q = q * jax.lax.rsqrt(jnp.linalg.norm(q, axis=1, keepdims=True) + EPS)
        k = k * jax.lax.rsqrt(jnp.linalg.norm(k, axis=1, keepdims=True) + EPS)
        dots = jnp.einsum('bhid,bhjd->bhij', q, k)
        scores = jax.nn.softmax(dots / scale[:, None, None], axis=-1)
        out = jnp.einsum('bhij,bhjd->bhid', scores, v)
        out = out.transpose(0, 2, 1, 3).reshape(b, n, h * dh)
        return out @ w_out.T + b_out

    def _L1_ffn_ref(hidden_states, ln_gamma, ln_beta, router_w, w1, w2):
        import jax, jax.numpy as jnp
        import numpy as np
        D_MODEL, D_FF, N_EXPERTS, TOP_K = (192, 768, 8, 2)
        B, S = (2, 256)
        LN_EPS = 1e-05

        def _layernorm(x, gamma, beta):
            mu = jnp.mean(x, axis=-1, keepdims=True)
            var = jnp.mean(jnp.square(x - mu), axis=-1, keepdims=True)
            return (x - mu) * jax.lax.rsqrt(var + LN_EPS) * gamma + beta
        Bz, Sz, D = hidden_states.shape
        residual = hidden_states
        x = _layernorm(hidden_states, ln_gamma, ln_beta)
        tokens = x.reshape(-1, D)
        T = tokens.shape[0]
        logits = tokens @ router_w
        probs = jax.nn.softmax(logits, axis=-1)
        topw, topi = jax.lax.top_k(probs, TOP_K)
        topw = topw / jnp.sum(topw, axis=-1, keepdims=True)
        gates = jnp.zeros((T, N_EXPERTS), dtype=tokens.dtype)
        gates = gates.at[jnp.arange(T)[:, None], topi].set(topw)
        h = jnp.einsum('td,edf->etf', tokens, w1)
        h = jax.nn.silu(h)
        y = jnp.einsum('etf,efd->etd', h, w2)
        out = jnp.einsum('te,etd->td', gates, y)
        return residual + out.reshape(Bz, Sz, D)
    h = _L0_tok_ref(x, L0_tok_ln_weight, L0_tok_ln_bias, L0_tok_proj_weight, L0_tok_proj_bias)
    h = _layernorm(h + _L0_attn_ref(h, L0_attn_dw_w, L0_attn_pw_w, L0_attn_pw_b, L0_attn_ak_w, L0_attn_ak_b, L0_attn_pt_w, L0_attn_pt_b), axis=-1)
    h = _layernorm(h + _L0_ffn_ref(h, L0_ffn_gate_w, L0_ffn_w1, L0_ffn_w2, L0_ffn_w3, L0_ffn_ws1, L0_ffn_ws2, L0_ffn_ws3), axis=-1)
    h = _layernorm(h + _L1_attn_ref(h, L1_attn_w_qkv, L1_attn_w_out, L1_attn_b_out, L1_attn_scale), axis=-1)
    h = _layernorm(h + _L1_ffn_ref(h, L1_ffn_ln_gamma, L1_ffn_ln_beta, L1_ffn_router_w, L1_ffn_w1, L1_ffn_w2), axis=-1)
    return h

_drawn_inputs = setup_inputs


def setup_inputs(seed=0):
    import zlib

    import numpy as np

    out = dict(_drawn_inputs(seed))
    spreads = {'L0_tok_ln_weight': (1.0, 0.2),
     'L0_tok_ln_bias': (0.0, 0.1),
     'L0_tok_proj_bias': (0.0, 0.1),
     'L1_attn_scale': (11.977279663085938, 0.6),
     'L1_ffn_ln_gamma': (1.0, 0.6),
     'L1_ffn_ln_beta': (0.0, 0.715)}
    factors = {'L0_attn_dw_w': 8.0,
     'L0_attn_pw_w': 8.0,
     'L0_attn_pw_b': 8.0,
     'L0_attn_ak_w': 8.0,
     'L0_attn_ak_b': 8.0,
     'L0_ffn_gate_w': 5.045,
     'L0_ffn_w1': 4.431,
     'L0_ffn_w2': 4.413,
     'L0_ffn_w3': 4.388,
     'L0_ffn_ws1': 3.169,
     'L0_ffn_ws2': 3.146,
     'L0_ffn_ws3': 3.15,
     'L1_attn_b_out': 5.871}
    for name, (base, spread) in spreads.items():
        noise = np.random.default_rng([zlib.crc32(name.encode()), seed]).standard_normal(out[name].shape)
        drawn = base * np.exp(spread * noise) if base else spread * noise
        out[name] = jnp.asarray(drawn.astype(out[name].dtype))
    for name, factor in factors.items():
        out[name] = (out[name] * factor).astype(out[name].dtype)
    return out
```

```python
import numpy as np
from contextlib import ExitStack

import concourse.bass as bass
from concourse import mybir

F32 = mybir.dt.float32
F16 = mybir.dt.float16
ALU = mybir.AluOpType
ACT = mybir.ActivationFunctionType
AX = mybir.AxisListType.X

P = 128
B, C, IMG, PATCH = 64, 3, 96, 16
GRID = IMG // PATCH
L = GRID * GRID
T = B * L
NT = T // P
D = 192
DB = D - P
WS = 256.0
SHIFTS = 5
PD = PATCH * PATCH * SHIFTS * C
CLASSES = ((5, 294), (5, 294), (4, 168), (3, 12), (1, 192))
KR = sum(n for _, n in CLASSES)
KC, NK = 120, KR // 120
EPS = 1e-5
H, K, IPG = 12, 9, 16
PAD = (K - 1) // 2
NTP = NT + 2 * PAD
HT = NT // 2
HTP = HT + 2 * PAD
HA = P // IPG
E = 8
HID0, HID1 = 512, 768
H1, DH = 12, 64
INNER = H1 * DH
NM = INNER // P
PAIR = 2 * L
PG = 32
NPG = P // PG
GP = PG // 4
NEG = -1e30
AHEAD = 2


class Chain:

    def __init__(self, eng, sem):
        self.eng, self.sem, self.n = eng, sem, 0

    def link(self, ins):
        self.n += 1
        ins.then_inc(self.sem, 1)
        self.eng.wait_ge(self.sem, self.n)


def rows(ap, n):
    return ap.rearrange("(a n) -> a n", a=1).to_broadcast([n, ap.shape[0]])


def five(nc, out, xh, xl, ah, al, b):
    nc.tensor.matmul(out, xh[:, 0], ah, start=True, stop=False)
    nc.tensor.matmul(out, xl[:, 0], ah, start=False, stop=False)
    nc.tensor.matmul(out, xh[:, 0], al, start=False, stop=False)
    nc.tensor.matmul(out, xh[:, 1], b, start=False, stop=False)
    return nc.tensor.matmul(out, xl[0:DB, 1], b[0:DB], start=False, stop=True)


def five_t(nc, out, ah, al, b, xh, xl):
    nc.tensor.matmul(out, ah, xh[:, 0], start=True, stop=False)
    nc.tensor.matmul(out, ah, xl[:, 0], start=False, stop=False)
    nc.tensor.matmul(out, al, xh[:, 0], start=False, stop=False)
    nc.tensor.matmul(out, b, xh[:, 1], start=False, stop=False)
    return nc.tensor.matmul(out, b[0:DB], xl[0:DB, 1], start=False, stop=True)


def skewed(eng, n, ahead, behind):
    ahead(0, 0, 0)
    with eng.Fori(0, (n - 2) // 2) as i:
        for u in range(2):
            ahead(2 * i + u + 1, 1 - u, i + u)
            behind(2 * i + u, u, i)
    ahead(n - 1, 1, n // 2 - 1)
    behind(n - 2, 0, n // 2 - 1)
    behind(n - 1, 1, n // 2 - 1)


def pairs(eng, n, step):
    with eng.Fori(0, n // 2) as i:
        for u in range(2):
            step(2 * i + u, u, i)


SPENT = []


def scope(nc, ctx, tag):
    sb = lambda n, s, d=F32: ctx.enter_context(nc.sbuf_tensor(tag + n, s, d))
    ps = lambda n, s, d=F32: ctx.enter_context(nc.psum_tensor(tag + n, s, d))

    def sem(n):
        SPENT.append(nc.alloc_semaphore(tag + n))
        return SPENT[-1]

    return sb, ps, sem


def patch_projection(nc, dr, h, ident):
    ctx = ExitStack()
    with ctx:
        sb, pst, sem = scope(nc, ctx, "pp_")
        x = [sb(f"x{u}", [P, KR]) for u in range(2)]
        xh, xl = sb("xh", [KC, 2, NK, P], F16), sb("xl", [KC, 2, NK, P], F16)
        wl = sb("wl", [KC, SHIFTS, NK, D])
        lnw, lnb = sb("lnw", [KC, SHIFTS * NK]), sb("lnb", [KC, SHIFTS * NK])
        negmult = sb("negmult", [KC, NK])
        wsum = sb("wsum", [KC, NK, D])
        wh, wlo = sb("wh", [KC, NK, D], F16), sb("wlo", [KC, NK, D], F16)
        bsum = sb("bsum", [KC, D])
        pbias = sb("pbias", [1, D])
        ones = sb("ones", [KC, P])
        colsum, bias = sb("colsum", [P, D]), sb("bias", [P, D])
        cw = sb("cw", [P, len(CLASSES) * 6])
        st = sb("st", [P, NT, len(CLASSES) * 6])
        mv = sb("mv", [P, NT, 2])
        rstd = sb("rstd", [P, NT])
        xt = [pst(f"xt{u}", [KC, NK * P]) for u in range(2)]
        acc = [pst(f"acc{u}", [P, 512]) for u in range(2)]
        ps, ps2 = pst("ps", [P, 512]), pst("ps2", [P, 512])
        w_in, small_in = sem("w_in"), sem("small_in")
        x_in = [sem(f"x_in{u}") for u in range(2)]
        link = sem("link")
        ones_set, wsum_done, sums_done, centred, w_hi, w_ready = (
            sem(n) for n in ("ones_set", "wsum_done", "sums_done", "centred", "w_hi", "w_ready"))
        x_transposed, x_counted, hi_done, lo_done, xs_free, mm_done, acc_free = (
            sem(n) for n in ("x_transposed", "x_counted", "hi_done", "lo_done", "xs_free", "mm_done", "acc_free"))
        var_done, std_done = sem("var_done"), sem("std_done")
        block = ctx.enter_context(nc.Block())

        @block.sync
        def _(sp):
            sp.dma_start(wl[:], dr["tok_w"]).then_inc(w_in, 16)
            for u in range(2):
                sp.dma_start(x[u][:], dr["x"][u]).then_inc(x_in[u], 16)

            def load(t, u, i):
                sp.wait_ge(x_transposed, t + 1)
                sp.wait_ge(x_counted, t + 1)
                sp.dma_start(x[u][:], dr["x"][t + 2]).then_inc(x_in[u], 16)

            pairs(sp, NT - 2, load)

        @block.gpsimd
        def _(pool):
            nc.gpsimd.memset(ones[:], 1.0).then_inc(ones_set, 1)

        @block.scalar
        def _(act):
            act.sem_inc(acc_free, AHEAD)
            for dst, name in ((lnw, "tok_lnw"), (lnb, "tok_lnb"), (negmult, "tok_negmult")):
                act.dma_start(dst[:], dr[name]).then_inc(small_in, 16)
            act.dma_start(pbias[:], dr["tok_b"].rearrange("(a n) -> a n", a=1)).then_inc(small_in, 16)
            act.dma_start(cw[:], rows(dr["tok_class"], P)).then_inc(small_in, 16)
            act.wait_ge(centred, 1)
            nc.scalar.activation(wh[:], wsum[:], ACT.Copy, scale=WS).then_inc(w_hi, 1)
            def split_hi(t, u, i):
                act.wait_ge(x_transposed, t + 1)
                act.wait_ge(mm_done, t + 1)
                nc.scalar.activation(xh[:, u], xt[u][:].rearrange("p (k q) -> p k q", k=NK), ACT.Copy).then_inc(hi_done, 1)

            def evacuate(t, u, i):
                act.wait_ge(mm_done, t + 1 + AHEAD)
                nc.scalar.activation(h[:, t, 0:D], acc[u][:, 0:D], ACT.Copy, scale=1.0 / WS).then_inc(acc_free, 1)

            skewed(act, NT, split_hi, evacuate)
            act.wait_ge(var_done, 1)
            nc.scalar.activation(rstd[:], rstd[:], ACT.Sqrt).then_inc(std_done, 1)

        @block.vector
        def _(dve):
            ch = Chain(dve, link)
            dve.sem_inc(lo_done, AHEAD)
            dve.wait_ge(w_in, 16)
            dve.wait_ge(small_in, 80)
            ch.link(nc.vector.memset(wsum[:], 0.0))
            ch.link(nc.vector.memset(bsum[:], 0.0))
            for s in range(SHIFTS):
                for k in range(NK):
                    j = s * NK + k
                    nc.vector.scalar_tensor_tensor(wsum[:, k, :], wl[:, s, k, :], lnw[:, j:j + 1], wsum[:, k, :],
                                                   ALU.mult, ALU.add)
                    ch.link(nc.vector.scalar_tensor_tensor(bsum[:], wl[:, s, k, :], lnb[:, j:j + 1], bsum[:],
                                                           ALU.mult, ALU.add))
            nc.vector.engine_nop().then_inc(wsum_done, 1)
            dve.wait_ge(sums_done, 1)
            ch.link(nc.vector.tensor_copy(colsum[:], ps[:, 0:D]))
            ch.link(nc.vector.tensor_copy(bias[:], ps2[:, 0:D]))
            for k in range(NK):
                ins = nc.vector.scalar_tensor_tensor(wsum[:, k, :], colsum[0:KC, :], negmult[:, k:k + 1],
                                                     wsum[:, k, :], ALU.mult, ALU.add)
            ins.then_inc(centred, 1)
            dve.wait_ge(w_hi, 1)
            nc.vector.scalar_tensor_tensor(wlo[:], wsum[:], WS, wh[:], ALU.mult, ALU.subtract).then_inc(w_ready, 1)

            def count(t, u, i):
                dve.wait_ge(x_in[u], 16 * (i + 1))
                at = 0
                for c, (_, n) in enumerate(CLASSES):
                    ins = nc.vector.bn_stats(st[:, t, 6 * c:6 * c + 6], x[u][:, at:at + n])
                    at += n
                ins.then_inc(x_counted, 1)
                dve.wait_ge(hi_done, t + 1)
                dve.wait_ge(mm_done, t + 1)
                nc.vector.tensor_tensor(xl[:, u], xt[u][:].rearrange("p (k q) -> p k q", k=NK), xh[:, u],
                                        ALU.subtract).then_inc(lo_done, 1)

            pairs(dve, NT, count)
            dve.wait_ge(lo_done, NT + AHEAD)
            ch.link(nc.vector.tensor_tensor(st[:], st[:], cw[:].rearrange("p (a n) -> p a n", a=1).to_broadcast([P, NT, len(CLASSES) * 6]), ALU.mult))
            for t in range(NT):
                ins = nc.vector.bn_aggr(mv[:, t, :], st[:, t, :])
            ch.link(ins)
            nc.vector.tensor_scalar(rstd[:], mv[:, :, 1], EPS, None, ALU.add).then_inc(var_done, 1)
            dve.wait_ge(std_done, 1)
            dve.wait_ge(acc_free, NT + AHEAD)
            ch.link(nc.vector.reciprocal(rstd[:], rstd[:]))
            for t in range(NT):
                nc.vector.scalar_tensor_tensor(h[:, t, 0:D], h[:, t, 0:D], rstd[:, t:t + 1], bias[:], ALU.mult, ALU.add)

        @block.tensor
        def _(pe):
            pe.sem_inc(mm_done, AHEAD)
            pe.wait_ge(ones_set, 1)
            pe.wait_ge(wsum_done, 1)
            for k in range(NK):
                nc.tensor.matmul(ps[:, 0:D], ones[:], wsum[:, k, :], start=(k == 0), stop=(k == NK - 1))
            nc.tensor.matmul(ps2[:, 0:D], ones[:], bsum[:], start=True, stop=False)
            nc.tensor.matmul(ps2[:, 0:D], ones[0:1, :], pbias[:], start=False, stop=True).then_inc(sums_done, 1)
            pe.wait_ge(w_ready, 1)

            def transpose(t, u, i):
                pe.wait_ge(x_in[u], 16 * (i + 1))
                pe.wait_ge(lo_done, t + 1)
                for k in range(NK):
                    ins = nc.tensor.transpose(xt[u][:, k * P:(k + 1) * P], x[u][:, k * KC:(k + 1) * KC], ident[:])
                ins.then_inc(x_transposed, 1)

            def project(t, u, i):
                pe.wait_ge(lo_done, t + 1 + AHEAD)
                pe.wait_ge(acc_free, t + 1)
                for a, b in ((xh, wh), (xl, wh), (xh, wlo)):
                    for k in range(NK):
                        ins = nc.tensor.matmul(acc[u][:, 0:D], a[:, u, k, :], b[:, k, :],
                                               start=(a is xh and b is wh and k == 0), stop=(b is wlo and k == NK - 1))
                ins.then_inc(mm_done, 1)

            skewed(pe, NT, transpose, project)


def normalise(nc, z, h, xh, xl, ident16, tag, affine=None):
    ctx = ExitStack()
    with ctx:
        sb, pst, sem = scope(nc, ctx, tag)
        st, mv, rstd = sb("st", [P, NT, 6]), sb("mv", [P, NT, 2]), sb("rstd", [P, NT])
        sh, sl = sb("sh", [P, NT, 2 * P], F16), sb("sl", [P, NT, 2 * P], F16)
        gb = sb("gb", [P, 2, D])
        ts = [pst(f"ts{u}", [P, 4, P], F16) for u in range(2)]
        link, var_done, std_done, h_done, hi_done, lo_done, t_done, t_used, gb_in = (
            sem(n) for n in ("link", "var_done", "std_done", "h_done", "hi_done", "lo_done", "t_done", "t_used", "gb_in"))
        halves = ((slice(0, P), slice(0, P)), (slice(P, P + DB), slice(P, D)), (slice(P + DB, 2 * P), slice(P, D)))
        block = ctx.enter_context(nc.Block())

        @block.vector
        def _(dve):
            ch = Chain(dve, link)
            if z is not None:
                for t in range(NT):
                    ins = nc.vector.bn_stats(st[:, t, :], z[:, t, :])
                ch.link(ins)
                for t in range(NT):
                    ins = nc.vector.bn_aggr(mv[:, t, :], st[:, t, :])
                ch.link(ins)
                nc.vector.tensor_scalar(rstd[:], mv[:, :, 1], EPS, None, ALU.add).then_inc(var_done, 1)
                dve.wait_ge(std_done, 1)
                ch.link(nc.vector.reciprocal(rstd[:], rstd[:]))
                for t in range(NT):
                    ins = nc.vector.tensor_scalar(h[:, t, :], z[:, t, :], mv[:, t, 0:1], rstd[:, t:t + 1], ALU.subtract, ALU.mult)
                ch.link(ins)
                if affine is not None:
                    dve.wait_ge(gb_in, 32)
                    for j, op in ((0, ALU.mult), (1, ALU.add)):
                        ch.link(nc.vector.tensor_tensor(h[:], h[:], gb[:, j:j + 1, :].to_broadcast([P, NT, D]), op))
            nc.vector.engine_nop().then_inc(h_done, 1)
            dve.wait_ge(hi_done, 1)
            for n, (a, b) in enumerate(halves):
                ins = nc.vector.tensor_tensor(sl[:, :, a], h[:, :, b], sh[:, :, a], ALU.subtract)
            ins.then_inc(lo_done, 1)

        @block.scalar
        def _(act):
            if affine is not None:
                for j in range(2):
                    act.dma_start(gb[:, j, :], rows(affine[j], P)).then_inc(gb_in, 16)
            if z is not None:
                act.wait_ge(var_done, 1)
                nc.scalar.activation(rstd[:], rstd[:], ACT.Sqrt).then_inc(std_done, 1)
            act.wait_ge(h_done, 1)
            for n, (a, b) in enumerate(halves):
                ins = nc.scalar.activation(sh[:, :, a], h[:, :, b], ACT.Copy)
            ins.then_inc(hi_done, 1)

            def unload(t, u, i):
                act.wait_ge(t_done, t + 1)
                nc.scalar.activation(xh[:, :, t, :], ts[u][:, 0:2, :], ACT.Copy)
                nc.scalar.activation(xl[:, :, t, :], ts[u][:, 2:4, :], ACT.Copy).then_inc(t_used, 1)

            act.sem_inc(t_used, AHEAD)
            pairs(act, NT, unload)

        @block.tensor
        def _(pe):
            pe.wait_ge(hi_done, 1)
            pe.wait_ge(lo_done, 1)

            def transpose(t, u, i):
                pe.wait_ge(t_used, t + 1)
                for n, s in enumerate((sh, sh, sl, sl)):
                    ins = nc.tensor.transpose(ts[u][:, n, :], s[:, t, (n % 2) * P:(n % 2 + 1) * P], ident16[:])
                ins.then_inc(t_done, 1)

            pairs(pe, NT, transpose)


def dynamic_convolution(nc, dr, h, xh, xl):
    ctx = ExitStack()
    with ctx:
        sb, pst, sem = scope(nc, ctx, "dc_")
        xa, xb = sb("xa", [P, NTP, P]), sb("xb", [P, HTP, P])
        ca, cb = sb("ca", [P, NT, P]), sb("cb", [P, HT, P])
        csh, csl = sb("csh", [P, NT + HT, P], F16), sb("csl", [P, NT + HT, P], F16)
        wdw, wpb = sb("wdw", [P, 2, K]), sb("wpb", [P, 2])
        wst = sb("wst", [P, 2 * P + 2 * HA * K + 2 * D])
        wh, wl = (sb(n, [P, 2 * P + 2 * HA * K + 2 * D], F16) for n in ("wh", "wl"))
        akb, ptb = sb("akb", [P, H * K]), sb("ptb", [P, D])
        kern = sb("kern", [P, NT, H * K])
        mx, rs = sb("mx", [P, NT * H]), sb("rs", [P, NT * H])
        v = sb("v", [P, NTP, D])
        prod = [sb(f"prod{u}", [P, NT, D]) for u in range(2)]
        pw = [pst(f"pw{u}", [P, 512]) for u in range(2)]
        pk = [pst(f"pk{u}", [P, 512]) for u in range(2)]
        pv = [pst(f"pv{u}", [P, 512]) for u in range(2)]
        w_in, bias_in, w_hi, w_ready, link, plink = (sem(n) for n in ("w_in", "bias_in", "w_hi", "w_ready", "link", "plink"))
        x_ready, edges, conv_done, pw_done, ca_done, c_hi, c_lo = (
            sem(n) for n in ("x_ready", "edges", "conv_done", "pw_done", "ca_done", "c_hi", "c_lo"))
        k_done, k_out, v_done, v_out, centred, exp_done, halo, prod_done, prod_used = (
            sem(n) for n in ("k_done", "k_out", "v_done", "v_out", "centred", "exp_done", "halo", "prod_done", "prod_used"))
        O_AK, O_PT = 2 * P, 2 * P + 2 * HA * K
        NAK = HA * K
        CH = [(0, 3 * c) for c in range(NT // 3)] + [(1, 3 * c) for c in range(HT // 3)]
        block = ctx.enter_context(nc.Block())

        @block.sync
        def _(sp):
            sp.dma_start(wst[:], dr["dc_w"]).then_inc(w_in, 16)
            sp.dma_start(wdw[:], dr["dc_dw"]).then_inc(bias_in, 16)
            sp.dma_start(wpb[:], dr["dc_pwb"]).then_inc(bias_in, 16)
            sp.dma_start(akb[:], rows(dr["dc_akb"], P)).then_inc(bias_in, 16)
            sp.dma_start(ptb[:], rows(dr["dc_ptb"], P)).then_inc(bias_in, 16)
            sp.wait_ge(v_out, NT + AHEAD)
            sp.wait_ge(edges, 1)
            with nc.allow_non_contiguous_dma(reason="rows of other partitions"):
                sp.dma_start(v[1:P:2, 0:PAD, :], v[0:P:2, NT:NT + PAD, :]).then_inc(halo, 16)
                sp.dma_start(v[0:P:2, NT + PAD:NTP, :], v[1:P:2, PAD:2 * PAD, :]).then_inc(halo, 16)

        @block.gpsimd
        def _(pool):
            ch = Chain(pool, plink)
            nc.gpsimd.memset(v[:, 0:PAD, :], 0.0)
            nc.gpsimd.memset(v[:, NT + PAD:NTP, :], 0.0).then_inc(edges, 1)
            nc.gpsimd.memset(xa[:, 0:PAD, :], 0.0)
            nc.gpsimd.memset(xa[:, NT + PAD:NTP, :], 0.0)
            nc.gpsimd.memset(xb[:, 0:PAD, :], 0.0)
            ch.link(nc.gpsimd.memset(xb[:, HT + PAD:HTP, :], 0.0))
            ch.link(nc.gpsimd.tensor_tensor(xa[:, PAD:PAD + NT, :], xh[:, 0], xl[:, 0], ALU.add))
            ch.link(nc.gpsimd.tensor_tensor(xb[0:DB, PAD:HTP, :], xh[0:DB, 1, 0:HT + PAD], xl[0:DB, 1, 0:HT + PAD], ALU.add))
            ch.link(nc.gpsimd.tensor_tensor(xb[DB:P, 0:HT + PAD, :], xh[DB:P, 1, HT - PAD:NT], xl[DB:P, 1, HT - PAD:NT], ALU.add))
            odd, even = slice(1, P, 2), slice(0, P, 2)
            ch.link(nc.gpsimd.tensor_copy(xa[:, 0:PAD, odd], xa[:, NT:NT + PAD, even]))
            ch.link(nc.gpsimd.tensor_copy(xa[:, NT + PAD:NTP, even], xa[:, PAD:2 * PAD, odd]))
            ch.link(nc.gpsimd.tensor_tensor(xb[0:DB, 0:PAD, odd], xh[0:DB, 1, NT - PAD:NT, even], xl[0:DB, 1, NT - PAD:NT, even], ALU.add))
            nc.gpsimd.tensor_tensor(xb[DB:P, HT + PAD:HTP, even], xh[DB:P, 1, 0:PAD, odd], xl[DB:P, 1, 0:PAD, odd], ALU.add).then_inc(x_ready, 1)
            pool.wait_ge(x_ready, 1)
            for n, (g, t0) in enumerate(CH):
                pool.wait_ge(c_hi, n + 1)
                c = (ca, cb)[g]
                o = NT * g + t0
                nc.gpsimd.tensor_tensor(csl[:, o:o + 3, :], c[:, t0:t0 + 3, :], csh[:, o:o + 3, :], ALU.subtract).then_inc(c_lo, 1)
            for k in range(K):
                pool.wait_ge(prod_done, k + 1)
                if k:
                    pool.wait_ge(prod_used, k)
                nc.gpsimd.tensor_tensor(h[:], h[:], prod[k % 2][:], ALU.add).then_inc(prod_used, 1)

        @block.scalar
        def _(act):
            act.sem_inc(v_out, AHEAD)
            act.wait_ge(w_in, 16)
            nc.scalar.activation(wh[:], wst[:], ACT.Copy, scale=WS).then_inc(w_hi, 1)
            for n, (g, t0) in enumerate(CH):
                act.wait_ge(ca_done, n + 1)
                c = (ca, cb)[g]
                o = NT * g + t0
                nc.scalar.activation(csh[:, o:o + 3, :], c[:, t0:t0 + 3, :], ACT.Copy).then_inc(c_hi, 1)
            act.wait_ge(centred, 1)
            nc.scalar.activation(kern[:], kern[:], ACT.Exp).then_inc(exp_done, 1)

        @block.vector
        def _(dve):
            ch = Chain(dve, link)
            dve.sem_inc(k_out, AHEAD)
            dve.wait_ge(bias_in, 64)
            dve.wait_ge(w_hi, 1)
            ch.link(nc.vector.scalar_tensor_tensor(wl[:], wst[:], WS, wh[:], ALU.mult, ALU.subtract))
            nc.vector.tensor_copy(wh[DB:P, O_PT + D:], wl[DB:P, O_PT + D:]).then_inc(w_ready, 1)

            def values(t, u, i):
                dve.wait_ge(v_done, t + 1)
                nc.vector.scalar_tensor_tensor(v[:, PAD + t, :], pv[u][:, 0:D], 1.0 / WS, ptb[:], ALU.mult, ALU.add).then_inc(v_out, 1)

            pairs(dve, NT, values)
            dve.wait_ge(x_ready, 1)
            for x, c, n, g in ((xa, ca, NT, 0), (xb, cb, HT, 1)):
                ch.link(nc.vector.tensor_scalar(c[:], x[:, 0:n, :], wdw[:, g, 0:1], None, ALU.mult))
                for k in range(1, K):
                    ch.link(nc.vector.scalar_tensor_tensor(c[:], x[:, k:k + n, :], wdw[:, g, k:k + 1], c[:], ALU.mult, ALU.add))
                nc.vector.engine_nop().then_inc(conv_done, 1)
            for n, (g, t0) in enumerate(CH):
                x, c = ((xa, ca), (xb, cb))[g]
                dve.wait_ge(pw_done, n + 1)
                ch.link(nc.vector.tensor_scalar(c[:, t0:t0 + 3, :], pw[n % 2][:, 0:3 * P].rearrange("p (t q) -> p t q", t=3), wpb[:, g:g + 1], None, ALU.add))
                nc.vector.tensor_tensor(c[:, t0:t0 + 3, :], c[:, t0:t0 + 3, :], x[:, PAD + t0:PAD + t0 + 3, :], ALU.mult).then_inc(ca_done, 1)
            with dve.Fori(0, HT) as t:
                dve.wait_ge(k_done, t + 1)
                nc.vector.scalar_tensor_tensor(kern[:, t, :], pk[0][:, 0:H * K], 1.0 / WS, akb[:], ALU.mult, ALU.add)
                nc.vector.scalar_tensor_tensor(kern[:, t + HT, :], pk[0][:, H * K:2 * H * K], 1.0 / WS, akb[:], ALU.mult, ALU.add).then_inc(k_out, 1)
            dve.wait_ge(k_out, HT + AHEAD)
            k3 = kern[:].rearrange("p t (h k) -> p (t h) k", k=K)
            wide = lambda a: a[:].rearrange("p (n a) -> p n a", a=1).to_broadcast([P, NT * H, K])
            ch.link(nc.vector.tensor_reduce(mx[:], k3, AX, ALU.max))
            nc.vector.tensor_tensor(k3, k3, wide(mx), ALU.subtract).then_inc(centred, 1)
            dve.wait_ge(exp_done, 1)
            ch.link(nc.vector.tensor_reduce(rs[:], k3, AX, ALU.add))
            ch.link(nc.vector.reciprocal(rs[:], rs[:]))
            ch.link(nc.vector.tensor_tensor(k3, k3, wide(rs), ALU.mult))
            dve.wait_ge(halo, 32)
            for k in range(K):
                if k >= 2:
                    dve.wait_ge(prod_used, k - 1)
                nc.vector.tensor_tensor(prod[k % 2][:].rearrange("p t (h d) -> p (t h) d", d=IPG),
                                        v[:, k:k + NT, :].rearrange("p t (h d) -> p (t h) d", d=IPG),
                                        k3[:, :, k:k + 1].to_broadcast([P, NT * H, IPG]), ALU.mult).then_inc(prod_done, 1)

        @block.tensor
        def _(pe):
            pe.wait_ge(w_ready, 1)

            def values(t, u, i):
                pe.wait_ge(v_out, t + 1)
                five(nc, pv[u][:, 0:D], xh[:, :, t, :], xl[:, :, t, :], wh[:, O_PT:O_PT + D], wl[:, O_PT:O_PT + D],
                     wh[:, O_PT + D:]).then_inc(v_done, 1)

            pairs(pe, NT, values)
            for n, (g, t0) in enumerate(CH):
                pe.wait_ge(conv_done, g + 1)
                if n >= 2:
                    pe.wait_ge(ca_done, n - 1)
                c = (ca, cb)[g]
                nc.tensor.matmul(pw[n % 2][:, 0:3 * P], wst[:, g * P:(g + 1) * P], c[:, t0:t0 + 3, :], start=True, stop=True).then_inc(pw_done, 1)
            pe.wait_ge(c_lo, len(CH))
            with pe.Fori(0, HT) as t:
                pe.wait_ge(k_out, t + 2)
                for j, (o, n) in enumerate(((t, 0), (t + HT, 0), (t + NT, 1))):
                    if n == 0:
                        out = pk[0][:, j * H * K:j * H * K + NAK]
                    else:
                        out = pk[0][:, 0:2 * H * K].rearrange("p (a k) -> p a k", a=2)[:, :, NAK:H * K]
                    w = slice(O_AK + n * NAK, O_AK + (n + 1) * NAK)
                    nc.tensor.matmul(out, csh[:, o, :], wh[:, w], start=True, stop=False)
                    nc.tensor.matmul(out, csl[:, o, :], wh[:, w], start=False, stop=False)
                    ins = nc.tensor.matmul(out, csh[:, o, :], wl[:, w], start=False, stop=True)
                ins.then_inc(k_done, 1)


def experts(nc, dr, h, xh, xl, ident, tag, hid, gated, shared):
    ne = E + shared
    nb = ne * NT
    nm = hid // P
    nw = 2 * hid if gated else hid
    npass = 2
    wcol = nw // npass
    n2 = nm * D
    stage_cols = 2 * nw + n2
    O_B, O_AL, O_2H, O_2L, COLS = nw, 2 * nw, 3 * nw, 3 * nw + n2, 3 * nw + 2 * n2
    ctx = ExitStack()
    with ctx:
        sb, pst, sem = scope(nc, ctx, tag)
        w = sb("w", [P, ne, COLS], F16)
        wst = [sb(f"wst{u}", [P, stage_cols]) for u in range(2)]
        rst, rh, rl = sb("rst", [P, 2, E]), sb("rh", [P, 2, E], F16), sb("rl", [P, 2, E], F16)
        lg, pr, sel1, sel2 = (sb(n, [P, NT, E]) for n in ("lg", "pr", "sel1", "sel2"))
        order = sb("order", [P, E])
        m, m1, m2, rd = (sb(n, [P, NT]) for n in ("m", "m1", "m2", "rd"))
        cw = sb("cw", [P, NT, ne])
        act_out = [sb(f"act{u}", [P, hid]) for u in range(2)]
        g = [sb(f"g{u}", [P, hid]) for u in range(2)]
        gh, gl = sb("gh", [P, 2, nm, P], F16), sb("gl", [P, 2, nm, P], F16)
        ph = [[pst(f"ph{u}{k}", [P, 512]) for k in range(2)] for u in range(2)]
        pt = [pst("pt0", [P, nm * P])]
        py = [pst(f"py{u}", [P, 512]) for u in range(8 - 4 - (nm * P + 511) // 512)]
        py = [py[0], py[-1]]
        w_in = [sem(f"w_in{u}") for u in range(2)]
        w_split, w_hi, r_in, r_hi, r_ready, l_done, l_out, link, order_in, centred, exp_done, cw_ready = (
            sem(n) for n in ("w_split", "w_hi", "r_in", "r_hi", "r_ready", "l_done", "l_out", "link", "order_in", "centred", "exp_done", "cw_ready"))
        h_done, silu_done, g_done, t_done, gh_done, gl_done, y_done, y_out = (
            sem(n) for n in ("h_done", "silu_done", "g_done", "t_done", "gh_done", "gl_done", "y_done", "y_out"))
        block = ctx.enter_context(nc.Block())

        @block.sync
        def _(sp):
            sp.dma_start(rst[:], dr[tag + "router"]).then_inc(r_in, 16)
            sp.dma_start(order[:], rows(dr["order"], P)).then_inc(order_in, 16)
            for e in range(ne):
                if e >= 2:
                    sp.wait_ge(w_split, e - 1)
                sp.dma_start(wst[e % 2][:], dr[tag + "w"][e]).then_inc(w_in[e % 2], 16)

        @block.scalar
        def _(act):
            act.sem_inc(gh_done, 1)
            act.wait_ge(r_in, 16)
            nc.scalar.activation(rh[:], rst[:], ACT.Copy, scale=WS).then_inc(r_hi, 1)
            for e in range(ne):
                act.wait_ge(w_in[e % 2], 16 * (e // 2 + 1))
                nc.scalar.activation(w[:, e, 0:2 * nw], wst[e % 2][:, 0:2 * nw], ACT.Copy, scale=WS)
                nc.scalar.activation(w[:, e, O_2H:O_2L], wst[e % 2][:, 2 * nw:], ACT.Copy, scale=WS).then_inc(w_hi, 1)
            act.wait_ge(centred, 1)
            nc.scalar.activation(pr[:], lg[:], ACT.Exp).then_inc(exp_done, 1)

            def silu(n, u, i):
                act.wait_ge(h_done, n + 1)
                act.wait_ge(g_done, n + 1)
                if gated:
                    nc.scalar.activation(act_out[u][:], ph[u][0][:, 0:hid], ACT.Silu, scale=1.0 / WS).then_inc(silu_done, 1)
                else:
                    nc.scalar.activation(g[u][:, 0:wcol], ph[u][0][:, 0:wcol], ACT.Silu, scale=1.0 / WS)
                    nc.scalar.activation(g[u][:, wcol:], ph[u][1][:, 0:wcol], ACT.Silu, scale=1.0 / WS).then_inc(g_done, 1)

            def split(n, u, i):
                act.wait_ge(t_done, n + 1 + AHEAD)
                act.wait_ge(y_done, n + 1)
                nc.scalar.activation(gh[:, u], pt[0][:].rearrange("p (m q) -> p m q", m=nm), ACT.Copy).then_inc(gh_done, 1)

            skewed(act, nb, silu, split)

        @block.vector
        def _(dve):
            ch = Chain(dve, link)
            dve.sem_inc(g_done, AHEAD)
            dve.sem_inc(l_out, AHEAD)
            dve.sem_inc(y_out, AHEAD)
            dve.sem_inc(gl_done, 1)
            if not shared:
                ch.link(nc.vector.tensor_scalar(h[:], h[:], 2.0, None, ALU.mult))
            dve.wait_ge(r_hi, 1)
            ch.link(nc.vector.scalar_tensor_tensor(rl[:], rst[:], WS, rh[:], ALU.mult, ALU.subtract))
            nc.vector.tensor_copy(rh[DB:P, 1, :], rl[DB:P, 1, :]).then_inc(r_ready, 1)
            for e in range(ne):
                dve.wait_ge(w_hi, e + 1)
                st = wst[e % 2]
                nc.vector.scalar_tensor_tensor(w[:, e, O_AL:O_2H], st[:, 0:nw], WS, w[:, e, 0:nw], ALU.mult, ALU.subtract)
                nc.vector.scalar_tensor_tensor(w[DB:P, e, O_B:O_AL], st[DB:P, nw:2 * nw], WS, w[DB:P, e, O_B:O_AL], ALU.mult, ALU.subtract)
                nc.vector.scalar_tensor_tensor(w[:, e, O_2L:COLS], st[:, 2 * nw:], WS, w[:, e, O_2H:O_2L], ALU.mult, ALU.subtract).then_inc(w_split, 1)

            def logits(t, u, i):
                dve.wait_ge(l_done, t + 1)
                nc.vector.tensor_scalar(lg[:, t, :], ph[u][0][:, 0:E], 1.0 / WS, None, ALU.mult).then_inc(l_out, 1)

            pairs(dve, NT, logits)
            dve.wait_ge(l_out, NT + AHEAD)
            wide = lambda a: a[:].rearrange("p (n a) -> p n a", a=1).to_broadcast([P, NT, E])
            TT, TR = nc.vector.tensor_tensor, nc.vector.tensor_reduce
            ch.link(TR(m[:], lg[:], AX, ALU.max))
            TT(lg[:], lg[:], wide(m), ALU.subtract).then_inc(centred, 1)
            dve.wait_ge(exp_done, 1)
            ch.link(TR(m[:], pr[:], AX, ALU.add))
            ch.link(nc.vector.reciprocal(m[:], m[:]))
            ch.link(TT(pr[:], pr[:], wide(m), ALU.mult))
            dve.wait_ge(order_in, 16)
            ord3 = order[:].rearrange("p (a e) -> p a e", a=1).to_broadcast([P, NT, E])
            for mk, sel in ((m1, sel1), (m2, sel2)):
                ch.link(TR(mk[:], pr[:], AX, ALU.max))
                ch.link(TT(sel[:], pr[:], wide(mk), ALU.is_ge))
                ch.link(TT(sel[:], sel[:], ord3, ALU.mult))
                ch.link(TR(m[:], sel[:], AX, ALU.max))
                ch.link(TT(sel[:], sel[:], wide(m), ALU.is_equal))
                if mk is m1:
                    ch.link(nc.vector.scalar_tensor_tensor(pr[:], sel[:], -2.0, pr[:], ALU.mult, ALU.add))
            ch.link(TT(rd[:], m1[:], m2[:], ALU.add))
            if shared:
                ch.link(nc.vector.tensor_scalar(rd[:], rd[:], 1e-20, None, ALU.add))
            ch.link(nc.vector.reciprocal(rd[:], rd[:]))
            for mk, sel in ((m1, sel1), (m2, sel2)):
                ch.link(nc.vector.scalar_tensor_tensor(mk[:], mk[:], 1.0 / WS, rd[:], ALU.mult, ALU.mult))
                ch.link(TT(sel[:], sel[:], wide(mk), ALU.mult))
            ch.link(TT(cw[:, :, 0:E], sel1[:], sel2[:], ALU.add))
            if shared:
                ch.link(nc.vector.memset(cw[:, :, E:ne], 1.0 / WS))

            def gate(n, u, i):
                if gated:
                    dve.wait_ge(silu_done, n + 1)
                    dve.wait_ge(t_done, n + 1)
                    nc.vector.scalar_tensor_tensor(g[u][:], ph[u][1][:, 0:hid], 1.0 / WS, act_out[u][:], ALU.mult, ALU.mult).then_inc(g_done, 1)

            def split(n, u, i):
                dve.wait_ge(gh_done, n + 2)
                nc.vector.tensor_tensor(gl[:, u], pt[0][:].rearrange("p (m q) -> p m q", m=nm), gh[:, u], ALU.subtract).then_inc(gl_done, 1)
                dve.wait_ge(y_done, n + 1 + AHEAD)
                e, t = i // (NT // 2), 2 * (i % (NT // 2)) + u
                nc.vector.scalar_tensor_tensor(h[:, t, :], py[u][:, 0:D], cw[:, t, bass.ds(e, 1)], h[:, t, :], ALU.mult, ALU.add).then_inc(y_out, 1)

            skewed(dve, nb, gate, split)

        @block.tensor
        def _(pe):
            pe.sem_inc(y_done, AHEAD)
            pe.sem_inc(t_done, AHEAD)
            pe.wait_ge(r_ready, 1)

            def logits(t, u, i):
                pe.wait_ge(l_out, t + 1)
                five(nc, ph[u][0][:, 0:E], xh[:, :, t, :], xl[:, :, t, :], rh[:, 0, :], rl[:, 0, :], rh[:, 1, :]).then_inc(l_done, 1)

            pairs(pe, NT, logits)
            pe.wait_ge(w_split, ne)
            pe.wait_ge(l_out, NT + AHEAD)

            def first(n, u, i):
                pe.wait_ge(g_done, n + 1)
                e, t = i // (NT // 2), 2 * (i % (NT // 2)) + u
                for k in range(npass):
                    c = k * wcol
                    ins = five(nc, ph[u][k][:, 0:wcol], xh[:, :, t, :], xl[:, :, t, :], w[:, e, c:c + wcol], w[:, e, O_AL + c:O_AL + c + wcol],
                               w[:, e, O_B + c:O_B + c + wcol])
                ins.then_inc(h_done, 1)

            def second(n, u, i):
                e = i // (NT // 2)
                pe.wait_ge(g_done, n + 1 + AHEAD)
                pe.wait_ge(gl_done, n + 1)
                for k in range(nm):
                    ins = nc.tensor.transpose(pt[0][:, k * P:(k + 1) * P], g[u][:, k * P:(k + 1) * P], ident[:])
                ins.then_inc(t_done, 1)
                pe.wait_ge(gl_done, n + 2)
                pe.wait_ge(y_out, n + 1)
                for n_, (a, o) in enumerate(((gh, O_2H), (gl, O_2H), (gh, O_2L))):
                    for k in range(nm):
                        ins = nc.tensor.matmul(py[u][:, 0:D], a[:, u, k, :], w[:, e, o + k * D:o + (k + 1) * D],
                                               start=(n_ == 0 and k == 0), stop=(n_ == 2 and k == nm - 1))
                ins.then_inc(y_done, 1)

            skewed(pe, nb, first, second)


def attention_weights(nc, dr, h, w, small):
    wqh, wql, wqb, woh, wol = w
    mask, isc, fold = small
    ctx = ExitStack()
    with ctx:
        sb, pst, sem = scope(nc, ctx, "aw_")
        wst, wost = sb("wst", [P, 2, 3 * INNER]), sb("wost", [P, NM * D])
        bout = sb("bout", [P, D])
        w_in, small_in, w_hi, link = (sem(n) for n in ("w_in", "small_in", "w_hi", "link"))
        block = ctx.enter_context(nc.Block())

        @block.sync
        def _(sp):
            sp.dma_start(bout[:], rows(dr["at_bout"], P)).then_inc(small_in, 16)
            sp.dma_start(mask[:], dr["at_mask"]).then_inc(small_in, 16)
            sp.dma_start(isc[:], dr["at_scale"]).then_inc(small_in, 16)
            sp.dma_start(fold[:], dr["at_fold"]).then_inc(small_in, 16)
            sp.dma_start(wst[:], dr["at_wqkv"]).then_inc(w_in, 16)
            sp.dma_start(wost[:], dr["at_wout"]).then_inc(w_in, 16)

        @block.scalar
        def _(act):
            act.wait_ge(w_in, 32)
            nc.scalar.activation(wqh[:], wst[:, 0], ACT.Copy, scale=WS)
            nc.scalar.activation(wqb[:], wst[:, 1], ACT.Copy, scale=WS)
            nc.scalar.activation(woh[:], wost[:], ACT.Copy, scale=WS).then_inc(w_hi, 1)

        @block.vector
        def _(dve):
            dve.wait_ge(small_in, 64)
            nc.vector.reciprocal(isc[:], isc[:])
            dve.wait_ge(w_hi, 1)
            nc.vector.scalar_tensor_tensor(wql[:], wst[:, 0], WS, wqh[:], ALU.mult, ALU.subtract)
            nc.vector.scalar_tensor_tensor(wqb[DB:P], wst[DB:P, 1], WS, wqb[DB:P], ALU.mult, ALU.subtract)
            nc.vector.scalar_tensor_tensor(wol[:], wost[:], WS, woh[:], ALU.mult, ALU.subtract)

        @block.gpsimd
        def _(pool):
            pool.wait_ge(small_in, 64)
            nc.gpsimd.tensor_tensor(h[:], h[:], bout[:].rearrange("p (a n) -> p a n", a=1).to_broadcast([P, NT, D]), ALU.add)


def attention(nc, dr, h, xh, xl, ident):
    ctx = ExitStack()
    with ctx:
        sb, pst, sem = scope(nc, ctx, "at_")
        GT = PG * NT
        HG = GT // 2
        NH = H1 // 2
        W6 = NH * PAIR
        wqh, wql, wqb = (sb(n, [P, 3 * INNER], F16) for n in ("wqh", "wql", "wqb"))
        woh, wol = sb("woh", [P, NM * D], F16), sb("wol", [P, NM * D], F16)
        mask, isc, fold = sb("mask", [PAIR, PAIR]), sb("isc", [P, NM]), sb("fold", [P, P])
        attention_weights(nc, dr, h, (wqh, wql, wqb, woh, wol), (mask, isc, fold))
        oh, ol = sb("oh", [P, NM, NT, P], F16), sb("ol", [P, NM, NT, P], F16)
        xgh, xgl = sb("xgh", [P, 2, GT], F16), sb("xgl", [P, 2, GT], F16)
        qk = sb("qk", [P, 2 * NM, GT])
        qkh, qkl = sb("qkh", [P, 2 * NM, GT], F16), sb("qkl", [P, 2 * NM, GT], F16)
        eps = sb("eps", [P, 1])
        sq = [sb(f"sq{u}", [P, HG]) for u in range(2)]
        ss = sb("ss", [P, 2, 2, HG])
        vh, vl = sb("vh", [PAIR, 2, INNER], F16), sb("vl", [PAIR, 2, INNER], F16)
        sm = [sb(f"sm{u}", [PAIR, 2, W6]) for u in range(2)]
        mx, rs = [[sb(f"{n}{u}", [PAIR, H1]) for u in range(2)] for n in ("mx", "rs")]
        ph, pl = sb("ph", [PAIR, 2, W6], F16), sb("pl", [PAIR, 2, W6], F16)
        pss = [pst(f"pss{u}", [P, 512]) for u in range(2)]
        pv = [pst(f"pv{u}", [P, 512]) for u in range(2)]
        pt = [pst(f"pt{u}", [P, 512]) for u in range(2)]
        po = [pst(f"po{u}", [P, 512]) for u in range(2)]
        (p_done, p_out, sq_done, sq_used, ss_done, fold_done, root_done, rn_done, scaled, qk_hi, qk_lo) = (sem(n) for n in (
            "p_done", "p_out", "sq_done", "sq_used", "ss_done", "fold_done", "root_done", "rn_done", "scaled", "qk_hi", "qk_lo"))
        (v_done, v_hi, v_lo, s_done, s_out, mx_done, centred, exp_done, rs_done, prob_done, t_done, t_hi, t_lo, o_done, o_hi, o_lo, rs_inv, rn_ready) = (
            sem(n) for n in ("v_done", "v_hi", "v_lo", "s_done", "s_out", "mx_done", "centred", "exp_done", "rs_done", "prob_done",
                             "t_done", "t_hi", "t_lo", "o_done", "o_hi", "o_lo", "rs_inv", "rn_ready"))
        eps_set, grouped = sem("eps_set"), sem("grouped")
        NP = 4 * NM
        block = ctx.enter_context(nc.Block())
        tiles = lambda x, c, lo, n, p, np_: x[:, c, lo:lo + n, bass.ds(p, np_)]
        head = lambda hd: ((hd % 2) * DH, hd // 2)

        @block.tensor
        def _(pe):
            with pe.Fori(0, NPG) as g:
                for n in range(NP):
                    m, hf = n // 2, n % 2
                    pe.wait_ge(p_out, g * NP + n + 1)
                    c = slice(m * P, (m + 1) * P)
                    if n == 0:
                        pe.wait_ge(grouped, g + 1)
                    xs = [x[:, :, hf * HG:(hf + 1) * HG] for x in (xgh, xgl)]
                    five_t(nc, pv[n % 2][:, 0:HG], wqh[:, c], wql[:, c], wqb[:, c], *xs).then_inc(p_done, 1)
                for n in range(4):
                    pe.wait_ge(ss_done, g * 4 + n + 1)
                    pe.wait_ge(root_done, g * 4 + n + 1)
                    nc.tensor.matmul(pt[n % 2][:, 0:HG], fold[:], ss[:, n // 2, n % 2, :], start=True, stop=True).then_inc(fold_done, 1)
                pe.wait_ge(qk_lo, g * 2 * NM + 2 * NM + 1)

                def scores(j):
                    pe.wait_ge(v_lo, g * GP + j + 1)
                    for half in range(2):
                        ins = None
                        xs = [x[:, :, j * PAIR:(j + 1) * PAIR] for x in (xgh, xgl)]
                        c = slice(2 * INNER + half * (INNER // 2), 2 * INNER + (half + 1) * (INNER // 2))
                        ins = five(nc, pv[half][0:PAIR, 0:INNER // 2], *xs, wqh[:, c], wql[:, c], wqb[:, c])
                    ins.then_inc(v_done, 1)
                    pe.wait_ge(s_out, g * GP + j + 1)
                    for hd in range(H1):
                        o, m = head(hd)
                        out = pss[hd % 2][0:PAIR, m * PAIR:(m + 1) * PAIR]
                        part = lambda t, mm: t[o:o + DH, mm, j * PAIR:(j + 1) * PAIR]
                        for k, (a, b) in enumerate(((qkh, qkh), (qkl, qkh), (qkh, qkl))):
                            ins = nc.tensor.matmul(out, part(a, m), part(b, NM + m), start=(k == 0), stop=(k == 2))
                    ins.then_inc(s_done, 1)

                def mix(j):
                    pe.wait_ge(prob_done, g * GP + j + 1)
                    pe.wait_ge(t_lo, g * GP + j + 1)
                    for hd in range(H1):
                        ins = nc.tensor.transpose(pt[hd % 2][0:PAIR, hd // 2 * PAIR:(hd // 2 + 1) * PAIR],
                                                  sm[j % 2][:, hd % 2, hd // 2 * PAIR:(hd // 2 + 1) * PAIR], ident[0:PAIR, 0:PAIR])
                    ins.then_inc(t_done, 1)
                    pe.wait_ge(t_lo, g * GP + j + 2)
                    pe.wait_ge(o_lo, g * GP + j + 1)
                    for hd in range(H1):
                        o, m = head(hd)
                        out = po[0][o:o + DH, m * PAIR:(m + 1) * PAIR]
                        for k, (a, b) in enumerate(((vh, ph), (vl, ph), (vh, pl))):
                            ins = nc.tensor.matmul(out, a[:, j % 2, hd * DH:(hd + 1) * DH], b[:, hd % 2, m * PAIR:(m + 1) * PAIR],
                                                   start=(k == 0), stop=(k == 2))
                    ins.then_inc(o_done, 1)

                scores(0)
                for j in range(GP):
                    if j + 1 < GP:
                        scores(j + 1)
                    mix(j)
            pe.wait_ge(o_hi, NPG * GP)
            pe.wait_ge(o_lo, NPG * GP + 1)

            def project(t, u, i):
                pe.wait_ge(p_out, NPG * NP + t + 1)
                for k, (a, b) in enumerate(((oh, woh), (ol, woh), (oh, wol))):
                    for m in range(NM):
                        ins = nc.tensor.matmul(pv[u][:, 0:D], a[:, m, t, :], b[:, m * D:(m + 1) * D], start=(k == m == 0), stop=(k == 2 and m == NM - 1))
                ins.then_inc(p_done, 1)

            pairs(pe, NT, project)

        @block.scalar
        def _(act):
            act.sem_inc(p_out, AHEAD)
            act.sem_inc(root_done, AHEAD)
            with act.Fori(0, NPG) as g:
                for n in range(NP):
                    m, hf = n // 2, n % 2
                    act.wait_ge(p_done, g * NP + n + 1)
                    act.wait_ge(sq_used, g * NP + n + 1)
                    if n == 0:
                        act.wait_ge(qk_lo, g * 2 * NM + 1)
                        act.wait_ge(scaled, g * 2 * NM + 1)
                    to = ss[:, m // NM, hf, :] if m % NM == 0 else sq[n % 2][:]
                    nc.scalar.activation(to, pv[n % 2][:, 0:HG], ACT.Square, scale=1.0 / WS).then_inc(sq_done, 1)
                    nc.scalar.activation(qk[:, m, hf * HG:(hf + 1) * HG], pv[n % 2][:, 0:HG], ACT.Copy, scale=1.0 / WS).then_inc(p_out, 1)
                for n in range(4):
                    act.wait_ge(fold_done, g * 4 + n + 1)
                    nc.scalar.activation(ss[:, n // 2, n % 2, :], pt[n % 2][:, 0:HG], ACT.Sqrt).then_inc(root_done, 1)
                act.wait_ge(root_done, g * 4 + 4 + AHEAD)
                act.wait_ge(eps_set, 1)
                nc.scalar.activation(ss[:], ss[:], ACT.Sqrt, bias=eps[:]).then_inc(rn_done, 1)
                for m in range(2 * NM):
                    act.wait_ge(scaled, g * 2 * NM + m + 2)
                    if m == 0:
                        act.wait_ge(s_done, g * GP + 1)
                    nc.scalar.activation(qkh[:, m, :], qk[:, m, :], ACT.Copy).then_inc(qk_hi, 1)

                def values(j):
                    n = g * GP + j
                    act.wait_ge(v_done, n + 2)
                    act.wait_ge(o_done, n + 1)
                    for half in range(2):
                        ins = nc.scalar.activation(vh[:, j % 2, half * (INNER // 2):(half + 1) * (INNER // 2)], pv[half][0:PAIR, 0:INNER // 2], ACT.Copy, scale=1.0 / WS)
                    ins.then_inc(v_hi, 1)

                def probabilities(j):
                    n = g * GP + j
                    act.wait_ge(centred, n + 1)
                    nc.scalar.activation(sm[j % 2][:], sm[j % 2][:], ACT.Exp).then_inc(exp_done, 1)

                def transposed(j):
                    n = g * GP + j
                    act.wait_ge(t_done, n + 1 + AHEAD)
                    act.wait_ge(o_done, n + AHEAD)
                    for par in range(2):
                        ins = nc.scalar.activation(ph[:, par, :], pt[par][0:PAIR, 0:W6], ACT.Copy)
                    ins.then_inc(t_hi, 1)
                    act.wait_ge(o_done, n + 1 + AHEAD)
                    nc.scalar.activation(oh[:, :, :, bass.ds(g * PG + 4 * j, 4)], po[0][:, 0:W6].rearrange("p (m t q) -> p m t q", m=NM, q=4), ACT.Copy).then_inc(o_hi, 1)

                values(0)
                probabilities(0)
                for j in range(GP):
                    if j + 1 < GP:
                        values(j + 1)
                        probabilities(j + 1)
                    transposed(j)

        @block.vector
        def _(dve):
            nc.vector.memset(eps[:], 1e-8).then_inc(eps_set, 1)
            with dve.Fori(0, NPG) as g:
                dve.wait_ge(v_done, g * GP + 1)
                for a, b in ((xgh, xh), (xgl, xl)):
                    for c in range(2):
                        ins = nc.vector.tensor_copy(a[:, c, :].rearrange("f (j t q) -> f j t q", t=NT, q=4),
                                                    b[:, c, :, bass.ds(g * PG, PG)].rearrange("f t (j q) -> f j t q", q=4))
                ins.then_inc(grouped, 1)
                dve.wait_ge(rn_done, g + 1)
                nc.vector.reciprocal(ss[:], ss[:]).then_inc(rn_ready, 1)
                dve.wait_ge(rn_ready, g + 1)
                for m in range(2 * NM):
                    w = qk[:, m, :].rearrange("p (a n) -> p a n", a=2)
                    if m < NM:
                        ins = nc.vector.scalar_tensor_tensor(w, w, isc[:, m:m + 1], ss[:, 0], ALU.mult, ALU.mult)
                    else:
                        ins = nc.vector.tensor_tensor(w, w, ss[:, 1], ALU.mult)
                    ins.then_inc(scaled, 1)

                def scores(j):
                    n = g * GP + j
                    s = sm[j % 2]
                    dve.wait_ge(v_hi, n + 1)
                    for half in range(2):
                        c = slice(half * (INNER // 2), (half + 1) * (INNER // 2))
                        ins = nc.vector.scalar_tensor_tensor(vl[:, j % 2, c], pv[half][0:PAIR, 0:INNER // 2], 1.0 / WS, vh[:, j % 2, c], ALU.mult, ALU.subtract)
                    ins.then_inc(v_lo, 1)
                    dve.wait_ge(s_done, n + 2)
                    dve.wait_ge(t_done, n + 1)
                    mk = mask[:].rearrange("p (a n) -> p a n", a=1).to_broadcast([PAIR, NH, PAIR])
                    for par in range(2):
                        ins = nc.vector.tensor_tensor(s[:, par, :].rearrange("p (m n) -> p m n", m=NH), pss[par][0:PAIR, 0:W6].rearrange("p (m n) -> p m n", m=NH), mk, ALU.add)
                    ins.then_inc(s_out, 1)
                    dve.wait_ge(s_out, n + 2)
                    nc.vector.tensor_reduce(mx[j % 2][:], s[:].rearrange("p a (m n) -> p (a m) n", n=PAIR), AX, ALU.max).then_inc(mx_done, 1)
                    dve.wait_ge(mx_done, n + 1)
                    s3 = s[:].rearrange("p a (m n) -> p (a m) n", n=PAIR)
                    nc.vector.tensor_tensor(s3, s3, mx[j % 2][:].rearrange("p (n a) -> p n a", a=1).to_broadcast([PAIR, H1, PAIR]), ALU.subtract).then_inc(centred, 1)

                def sums(j):
                    n = g * GP + j
                    dve.wait_ge(exp_done, n + 1)
                    nc.vector.tensor_reduce(rs[j % 2][:], sm[j % 2][:].rearrange("p a (m n) -> p (a m) n", n=PAIR), AX, ALU.add).then_inc(rs_done, 1)
                    dve.wait_ge(rs_done, n + 1)
                    nc.vector.reciprocal(rs[j % 2][:], rs[j % 2][:]).then_inc(rs_inv, 1)

                def transposed(j):
                    n = g * GP + j
                    dve.wait_ge(t_hi, n + 1)
                    for par in range(2):
                        ins = nc.vector.tensor_tensor(pl[:, par, :], pt[par][0:PAIR, 0:W6], ph[:, par, :], ALU.subtract)
                    ins.then_inc(t_lo, 1)
                    dve.wait_ge(o_hi, n + 1)
                    at = bass.ds(g * PG + 4 * j, 4)
                    nc.vector.tensor_tensor(ol[:, :, :, at], po[0][:, 0:W6].rearrange("p (m t q) -> p m t q", m=NM, q=4), oh[:, :, :, at], ALU.subtract).then_inc(o_lo, 1)

                scores(0)
                sums(0)
                for j in range(GP):
                    if j + 1 < GP:
                        scores(j + 1)
                        sums(j + 1)
                    transposed(j)

            def project(t, u, i):
                dve.wait_ge(p_done, NPG * NP + t + 1)
                nc.vector.scalar_tensor_tensor(h[:, t, :], pv[u][:, 0:D], 1.0 / WS, h[:, t, :], ALU.mult, ALU.add).then_inc(p_out, 1)

            pairs(dve, NT, project)

        @block.gpsimd
        def _(pool):
            pool.sem_inc(sq_used, AHEAD)
            pool.sem_inc(t_done, AHEAD)
            pool.sem_inc(o_done, AHEAD)
            for one in (v_lo, s_out, t_lo, o_lo, qk_lo, scaled, s_done, v_done):
                pool.sem_inc(one, 1)
            with pool.Fori(0, NPG) as g:
                for n in range(NP):
                    m, hf = n // 2, n % 2
                    to = ss[:, m // NM, hf, :]
                    pool.wait_ge(sq_done, g * NP + n + 1)
                    if m % NM == 0:
                        pool.sem_inc(sq_used, 1)
                        continue
                    nc.gpsimd.tensor_tensor(to, to, sq[n % 2][:], ALU.add).then_inc(sq_used, 1)
                    if m % NM == NM - 1:
                        pool.wait_ge(sq_used, g * NP + n + 1 + AHEAD)
                        pool.sem_inc(ss_done, 1)
                for m in range(2 * NM):
                    pool.wait_ge(qk_hi, g * 2 * NM + m + 1)
                    nc.gpsimd.tensor_tensor(qkl[:, m, :], qk[:, m, :], qkh[:, m, :], ALU.subtract).then_inc(qk_lo, 1)

                def scale(j):
                    pool.wait_ge(rs_inv, g * GP + j + 1)
                    s3 = sm[j % 2][:].rearrange("p a (m n) -> p (a m) n", n=PAIR)
                    nc.gpsimd.tensor_tensor(s3, s3, rs[j % 2][:].rearrange("p (n a) -> p n a", a=1).to_broadcast([PAIR, H1, PAIR]), ALU.mult).then_inc(prob_done, 1)

                for j in range(GP):
                    scale(j)


def identity(nc, ident, ident16):
    with nc.semaphore("id_set") as id_set, nc.Block() as block:
        @block.gpsimd
        def _(pool):
            nc.gpsimd.memset(ident[:], 0.0).then_inc(id_set, 1)
            nc.gpsimd.memset(ident16[:], 0.0).then_inc(id_set, 1)
            pool.wait_ge(id_set, 2)
            for m in (ident, ident16):
                nc.gpsimd.affine_select(out=m[:], in_=m[:], compare_op=ALU.not_equal, fill=1.0, base=0,
                                        pattern=[[-1, P]], channel_multiplier=1)


def recycle_semaphores(nc):
    nc.clear_and_free_semaphores(SPENT)
    SPENT.clear()
    nc.all_engine_barrier()


def build(nc, dr, out, stage):
    SPENT.clear()
    with (nc.sbuf_tensor("h", [P, NT, D], F32) as h, nc.sbuf_tensor("ident", [P, P], F32) as ident,
          nc.sbuf_tensor("ident16", [P, P], F16) as ident16, ExitStack() as stack):
        identity(nc, ident, ident16)
        xh = stack.enter_context(nc.sbuf_tensor("xh", [P, 2, NT, P], F16))
        xl = stack.enter_context(nc.sbuf_tensor("xl", [P, 2, NT, P], F16))
        patch_projection(nc, dr, h, ident)
        if stage >= 1:
            normalise(nc, None, h, xh, xl, ident16, "n0_")
            dynamic_convolution(nc, dr, h, xh, xl)
            normalise(nc, h, h, xh, xl, ident16, "n1_")
        if stage >= 2:
            experts(nc, dr, h, xh, xl, ident, "f0_", HID0, True, 1)
            normalise(nc, h, h, xh, xl, ident16, "n2_")
        if stage >= 3:
            attention(nc, dr, h, xh, xl, ident)
            h2 = stack.enter_context(nc.sbuf_tensor("h2", [P, NT, D], F32))
            normalise(nc, h, h, xh, xl, ident16, "n3_")
        if stage >= 4:
            recycle_semaphores(nc)
            normalise(nc, h, h2, xh, xl, ident16, "n4_", affine=(dr["f1_gamma"], dr["f1_beta"]))
            experts(nc, dr, h, xh, xl, ident, "f1_", HID1, False, 0)
            normalise(nc, h, h, xh, xl, ident16, "n5_")
        with nc.semaphore("out_done") as out_done, nc.Block() as block:
            @block.sync
            def _(sp):
                sp.dma_start(out, h[:]).then_inc(out_done, 16)
                sp.wait_ge(out_done, 16)


def pixel_rows():
    pix = []
    for c in range(C):
        for y in range(-1, PATCH + 1):
            for x in range(-1, PATCH + 1):
                if not (0 <= y < PATCH or 0 <= x < PATCH):
                    continue
                fs = []
                for s, (dy, dx) in enumerate(((0, 0), (0, 1), (0, -1), (1, 0), (-1, 0))):
                    py, px = y + dy, x + dx
                    inside = 0 <= py < PATCH and 0 <= px < PATCH
                    fs.append((py * PATCH + px) * SHIFTS * C + s * C + c if inside else PD)
                pix.append((sum(f < PD for f in fs), c, y, x, fs))
    pix.sort(key=lambda p: -p[0])
    return [p[1:4] for p in pix], np.array([p[4] for p in pix]).T, np.array([p[0] for p in pix])


def lay_out(inp):
    f = {k: np.asarray(v) for k, v in inp.items()}
    pix, feats, count = pixel_rows()
    assert [tuple(c) for c in CLASSES if c[0] < 5] == [(n, int((count == n).sum())) for n in (4, 3, 1)]
    xp = np.pad(f["x"], ((0, 0), (0, 0), (1, 1), (1, 1)))
    cols = np.empty((B, GRID, GRID, KR), np.float32)
    for r, (c, y, x) in enumerate(pix):
        cols[..., r] = xp[:, c, y + 1:y + 2 + IMG - PATCH:PATCH, x + 1:x + 2 + IMG - PATCH:PATCH]
    d = {"x": cols.reshape(P, NT, KR).transpose(1, 0, 2)}
    none = lambda a: np.concatenate([a, np.zeros(a.shape[:-1] + (1,), a.dtype)], -1)
    wt = none(f["L0_tok_proj_weight"])[:, feats]
    d["tok_w"] = wt.reshape(D, SHIFTS, NK, KC).transpose(3, 1, 2, 0)
    by_row = lambda a: none(a)[feats].reshape(SHIFTS * NK, KC).T
    d["tok_lnw"] = by_row(f["L0_tok_ln_weight"])
    d["tok_lnb"] = by_row(f["L0_tok_ln_bias"])
    d["tok_negmult"] = (-count / PD).astype(np.float32).reshape(NK, KC).T
    d["tok_class"] = np.array([[n, 1, n] * 2 for n, _ in CLASSES], np.float32).ravel()
    d["tok_b"] = f["L0_tok_proj_bias"]
    dw = f["L0_attn_dw_w"][:, 0]
    twice = lambda a: np.concatenate([a[P:], a[P:]])
    d["dc_dw"] = np.stack([dw[:P], twice(dw)], 1)
    d["dc_pwb"] = np.stack([f["L0_attn_pw_b"][:P], twice(f["L0_attn_pw_b"])], 1)
    d["dc_akb"], d["dc_ptb"] = f["L0_attn_ak_b"], f["L0_attn_pt_b"]
    pw, ak, pt = f["L0_attn_pw_w"], f["L0_attn_ak_w"], f["L0_attn_pt_w"].T
    w = np.zeros((P, 2 * P + 2 * HA * K + 2 * D), np.float32)
    heads_b = list(range(HA, H)) * 2
    for n in range(HA):
        r = slice(n * IPG, (n + 1) * IPG)
        for g, head in ((0, n), (1, heads_b[n])):
            w[r, g * P + n * IPG:g * P + (n + 1) * IPG] = pw[head].T
            w[r, 2 * P + (g * HA + n) * K:2 * P + (g * HA + n + 1) * K] = ak[head].T
    w[:, 2 * P + 2 * HA * K:2 * P + 2 * HA * K + D] = pt[:P]
    w[:, 2 * P + 2 * HA * K + D:] = np.concatenate([pt[P:], pt[P:]])
    d["dc_w"] = w
    wq = f["L1_attn_w_qkv"].T
    d["at_wqkv"] = np.stack([wq[:P], twice(wq)], 1)
    d["at_wout"] = f["L1_attn_w_out"].T.reshape(NM, P, D).transpose(1, 0, 2).reshape(P, NM * D)
    d["at_bout"] = f["L1_attn_b_out"]
    d["at_scale"] = np.repeat(f["L1_attn_scale"].reshape(NM, 2).T, DH, 0)
    d["at_fold"] = np.tile(np.eye(DH, dtype=np.float32), (2, 2))
    image = np.arange(PAIR) % 4 // 2
    d["at_mask"] = np.where(image[:, None] == image, 0, NEG).astype(np.float32)
    d["f1_gamma"], d["f1_beta"] = f["L1_ffn_ln_gamma"], f["L1_ffn_ln_beta"]
    d["order"] = np.arange(E, 0, -1).astype(np.float32)

    def router(r):
        return np.stack([r[:P], twice(r)], 1)

    def pack(first, second):
        return np.concatenate([first[:P], twice(first), second.reshape(-1, P, D).transpose(1, 0, 2).reshape(P, -1)], 1)

    d["f0_router"] = router(f["L0_ffn_gate_w"].T)
    d["f0_w"] = np.stack([pack(np.concatenate([a.T, c.T], 1), b.T) for a, b, c in
                          [(f["L0_ffn_w1"][e], f["L0_ffn_w2"][e], f["L0_ffn_w3"][e]) for e in range(E)]
                          + [(f["L0_ffn_ws1"], f["L0_ffn_ws2"], f["L0_ffn_ws3"])]])
    d["f1_router"] = router(f["L1_ffn_router_w"])
    d["f1_w"] = np.stack([pack(f["L1_ffn_w1"][e], f["L1_ffn_w2"][e]) for e in range(E)])
    return {k: np.ascontiguousarray(v) for k, v in d.items()}


STAGE = 9


def kernel(**inputs):
    import concourse.bacc as bacc
    from concourse.bass_utils import run_bass_kernel_spmd as run

    d = lay_out(inputs)
    nc = bacc.Bacc("TRN2", target_bir_lowering=False, num_devices=1)
    dr = {k: nc.dram_tensor("in_" + k, v.shape, mybir.dt.from_np(v.dtype), kind="ExternalInput").ap() for k, v in d.items()}
    out = nc.dram_tensor("out_h", [P, NT, D], F32, kind="ExternalOutput").ap()
    build(nc, dr, out, STAGE)
    r = run(nc, [{"in_" + k: v for k, v in d.items()}], core_ids=[0])
    return np.asarray(r.results[0]["out_h"]).reshape(B, L, D)
```

```python
import numpy as np
from contextlib import ExitStack

import concourse.bass as bass
from concourse import mybir

F32 = mybir.dt.float32
F16 = mybir.dt.float16
I32 = mybir.dt.int32
ALU = mybir.AluOpType
ACT = mybir.ActivationFunctionType
AX = mybir.AxisListType.X

P = 128
B, C, IMG, PATCH = 64, 3, 96, 16
GRID = IMG // PATCH
L = GRID * GRID
T = B * L
NT = T // P
D = 192
DB = D - P
WS = 256.0
SHIFTS = 5
PD = PATCH * PATCH * SHIFTS * C
CLASSES = ((5, 294), (5, 294), (4, 168), (3, 12), (1, 192))
KR = sum(n for _, n in CLASSES)
KC, NK = 120, KR // 120
EPS = 1e-5
H, K, IPG = 12, 9, 16
PAD = (K - 1) // 2
NTP = NT + 2 * PAD
HT = NT // 2
HTP = HT + 2 * PAD
HA = P // IPG
E = 8
HID0, HID1 = 512, 768
H1, DH = 12, 64
INNER = H1 * DH
NM = INNER // P
PAIR = 2 * L
PG = 32
NPG = P // PG
GP = PG // 4
NEG = -1e30
NB = 2 * T // P + E - 1
RING = 6
ROW = D + 2
AHEAD = 2


class Chain:

    def __init__(self, eng, sem):
        self.eng, self.sem, self.n = eng, sem, 0

    def link(self, ins):
        self.n += 1
        ins.then_inc(self.sem, 1)
        self.eng.wait_ge(self.sem, self.n)


def rows(ap, n):
    return ap.rearrange("(a n) -> a n", a=1).to_broadcast([n, ap.shape[0]])


def five(nc, out, xh, xl, ah, al, b):
    nc.tensor.matmul(out, xh[:, 0], ah, start=True, stop=False)
    nc.tensor.matmul(out, xl[:, 0], ah, start=False, stop=False)
    nc.tensor.matmul(out, xh[:, 0], al, start=False, stop=False)
    nc.tensor.matmul(out, xh[:, 1], b, start=False, stop=False)
    return nc.tensor.matmul(out, xl[0:DB, 1], b[0:DB], start=False, stop=True)


def five_t(nc, out, ah, al, b, xh, xl):
    nc.tensor.matmul(out, ah, xh[:, 0], start=True, stop=False)
    nc.tensor.matmul(out, ah, xl[:, 0], start=False, stop=False)
    nc.tensor.matmul(out, al, xh[:, 0], start=False, stop=False)
    nc.tensor.matmul(out, b, xh[:, 1], start=False, stop=False)
    return nc.tensor.matmul(out, b[0:DB], xl[0:DB, 1], start=False, stop=True)


def skewed(eng, n, ahead, behind):
    ahead(0, 0, 0)
    with eng.Fori(0, (n - 2) // 2) as i:
        for u in range(2):
            ahead(2 * i + u + 1, 1 - u, i + u)
            behind(2 * i + u, u, i)
    ahead(n - 1, 1, n // 2 - 1)
    behind(n - 2, 0, n // 2 - 1)
    behind(n - 1, 1, n // 2 - 1)


def pairs(eng, n, step):
    with eng.Fori(0, n // 2) as i:
        for u in range(2):
            step(2 * i + u, u, i)


SPENT = []


def pipelined(eng, n, r, *stages):
    lead = max(a for a, _ in stages)

    def peeled(i):
        for a, f in stages:
            if 0 <= i + a < n:
                f(i + a, (i + a) % r, (i + a) // r)

    for i in range(-lead, 0):
        peeled(i)
    with eng.Fori(0, (n - lead) // r) as q:
        for u in range(r):
            for a, f in stages:
                f(r * q + u + a, (u + a) % r, q + (u + a) // r)
    for i in range((n - lead) // r * r, n):
        peeled(i)


def scope(nc, ctx, tag):
    sb = lambda n, s, d=F32: ctx.enter_context(nc.sbuf_tensor(tag + n, s, d))
    ps = lambda n, s, d=F32: ctx.enter_context(nc.psum_tensor(tag + n, s, d))

    def sem(n):
        SPENT.append(nc.alloc_semaphore(tag + n))
        return SPENT[-1]

    return sb, ps, sem


def patch_projection(nc, dr, h, ident):
    ctx = ExitStack()
    with ctx:
        sb, pst, sem = scope(nc, ctx, "pp_")
        x = [sb(f"x{u}", [P, KR]) for u in range(2)]
        xh, xl = sb("xh", [KC, 2, NK, P], F16), sb("xl", [KC, 2, NK, P], F16)
        wl = sb("wl", [KC, SHIFTS, NK, D])
        lnw, lnb = sb("lnw", [KC, SHIFTS * NK]), sb("lnb", [KC, SHIFTS * NK])
        negmult = sb("negmult", [KC, NK])
        wsum = sb("wsum", [KC, NK, D])
        wh, wlo = sb("wh", [KC, NK, D], F16), sb("wlo", [KC, NK, D], F16)
        bsum = sb("bsum", [KC, D])
        pbias = sb("pbias", [1, D])
        ones = sb("ones", [KC, P])
        colsum, bias = sb("colsum", [P, D]), sb("bias", [P, D])
        cw = sb("cw", [P, len(CLASSES) * 6])
        st = sb("st", [P, NT, len(CLASSES) * 6])
        mv = sb("mv", [P, NT, 2])
        rstd = sb("rstd", [P, NT])
        xt = [pst(f"xt{u}", [KC, NK * P]) for u in range(2)]
        acc = [pst(f"acc{u}", [P, 512]) for u in range(2)]
        ps, ps2 = pst("ps", [P, 512]), pst("ps2", [P, 512])
        w_in, small_in = sem("w_in"), sem("small_in")
        x_in = [sem(f"x_in{u}") for u in range(2)]
        link = sem("link")
        ones_set, wsum_done, sums_done, centred, w_hi, w_ready = (
            sem(n) for n in ("ones_set", "wsum_done", "sums_done", "centred", "w_hi", "w_ready"))
        x_transposed, x_counted, hi_done, lo_done, xs_free, mm_done, acc_free = (
            sem(n) for n in ("x_transposed", "x_counted", "hi_done", "lo_done", "xs_free", "mm_done", "acc_free"))
        var_done, std_done = sem("var_done"), sem("std_done")
        block = ctx.enter_context(nc.Block())

        @block.sync
        def _(sp):
            sp.dma_start(wl[:], dr["tok_w"]).then_inc(w_in, 16)
            for u in range(2):
                sp.dma_start(x[u][:], dr["x"][u]).then_inc(x_in[u], 16)

            def load(t, u, i):
                sp.wait_ge(x_transposed, t + 1)
                sp.wait_ge(x_counted, t + 1)
                sp.dma_start(x[u][:], dr["x"][t + 2]).then_inc(x_in[u], 16)

            pairs(sp, NT - 2, load)

        @block.gpsimd
        def _(pool):
            nc.gpsimd.memset(ones[:], 1.0).then_inc(ones_set, 1)

        @block.scalar
        def _(act):
            act.sem_inc(acc_free, AHEAD)
            for dst, name in ((lnw, "tok_lnw"), (lnb, "tok_lnb"), (negmult, "tok_negmult")):
                act.dma_start(dst[:], dr[name]).then_inc(small_in, 16)
            act.dma_start(pbias[:], dr["tok_b"].rearrange("(a n) -> a n", a=1)).then_inc(small_in, 16)
            act.dma_start(cw[:], rows(dr["tok_class"], P)).then_inc(small_in, 16)
            act.wait_ge(centred, 1)
            nc.scalar.activation(wh[:], wsum[:], ACT.Copy, scale=WS).then_inc(w_hi, 1)
            def split_hi(t, u, i):
                act.wait_ge(x_transposed, t + 1)
                act.wait_ge(mm_done, t + 1)
                nc.scalar.activation(xh[:, u], xt[u][:].rearrange("p (k q) -> p k q", k=NK), ACT.Copy).then_inc(hi_done, 1)

            def evacuate(t, u, i):
                act.wait_ge(mm_done, t + 1 + AHEAD)
                nc.scalar.activation(h[:, t, 0:D], acc[u][:, 0:D], ACT.Copy, scale=1.0 / WS).then_inc(acc_free, 1)

            skewed(act, NT, split_hi, evacuate)
            act.wait_ge(var_done, 1)
            nc.scalar.activation(rstd[:], rstd[:], ACT.Sqrt).then_inc(std_done, 1)

        @block.vector
        def _(dve):
            ch = Chain(dve, link)
            dve.sem_inc(lo_done, AHEAD)
            dve.wait_ge(w_in, 16)
            dve.wait_ge(small_in, 80)
            ch.link(nc.vector.memset(wsum[:], 0.0))
            ch.link(nc.vector.memset(bsum[:], 0.0))
            for s in range(SHIFTS):
                for k in range(NK):
                    j = s * NK + k
                    nc.vector.scalar_tensor_tensor(wsum[:, k, :], wl[:, s, k, :], lnw[:, j:j + 1], wsum[:, k, :],
                                                   ALU.mult, ALU.add)
                    ch.link(nc.vector.scalar_tensor_tensor(bsum[:], wl[:, s, k, :], lnb[:, j:j + 1], bsum[:],
                                                           ALU.mult, ALU.add))
            nc.vector.engine_nop().then_inc(wsum_done, 1)
            dve.wait_ge(sums_done, 1)
            ch.link(nc.vector.tensor_copy(colsum[:], ps[:, 0:D]))
            ch.link(nc.vector.tensor_copy(bias[:], ps2[:, 0:D]))
            for k in range(NK):
                ins = nc.vector.scalar_tensor_tensor(wsum[:, k, :], colsum[0:KC, :], negmult[:, k:k + 1],
                                                     wsum[:, k, :], ALU.mult, ALU.add)
            ins.then_inc(centred, 1)
            dve.wait_ge(w_hi, 1)
            nc.vector.scalar_tensor_tensor(wlo[:], wsum[:], WS, wh[:], ALU.mult, ALU.subtract).then_inc(w_ready, 1)

            def count(t, u, i):
                dve.wait_ge(x_in[u], 16 * (i + 1))
                at = 0
                for c, (_, n) in enumerate(CLASSES):
                    ins = nc.vector.bn_stats(st[:, t, 6 * c:6 * c + 6], x[u][:, at:at + n])
                    at += n
                ins.then_inc(x_counted, 1)
                dve.wait_ge(hi_done, t + 1)
                dve.wait_ge(mm_done, t + 1)
                nc.vector.tensor_tensor(xl[:, u], xt[u][:].rearrange("p (k q) -> p k q", k=NK), xh[:, u],
                                        ALU.subtract).then_inc(lo_done, 1)

            pairs(dve, NT, count)
            dve.wait_ge(lo_done, NT + AHEAD)
            ch.link(nc.vector.tensor_tensor(st[:], st[:], cw[:].rearrange("p (a n) -> p a n", a=1).to_broadcast([P, NT, len(CLASSES) * 6]), ALU.mult))
            for t in range(NT):
                ins = nc.vector.bn_aggr(mv[:, t, :], st[:, t, :])
            ch.link(ins)
            nc.vector.tensor_scalar(rstd[:], mv[:, :, 1], EPS, None, ALU.add).then_inc(var_done, 1)
            dve.wait_ge(std_done, 1)
            dve.wait_ge(acc_free, NT + AHEAD)
            ch.link(nc.vector.reciprocal(rstd[:], rstd[:]))
            for t in range(NT):
                nc.vector.scalar_tensor_tensor(h[:, t, 0:D], h[:, t, 0:D], rstd[:, t:t + 1], bias[:], ALU.mult, ALU.add)

        @block.tensor
        def _(pe):
            pe.sem_inc(mm_done, AHEAD)
            pe.wait_ge(ones_set, 1)
            pe.wait_ge(wsum_done, 1)
            for k in range(NK):
                nc.tensor.matmul(ps[:, 0:D], ones[:], wsum[:, k, :], start=(k == 0), stop=(k == NK - 1))
            nc.tensor.matmul(ps2[:, 0:D], ones[:], bsum[:], start=True, stop=False)
            nc.tensor.matmul(ps2[:, 0:D], ones[0:1, :], pbias[:], start=False, stop=True).then_inc(sums_done, 1)
            pe.wait_ge(w_ready, 1)

            def transpose(t, u, i):
                pe.wait_ge(x_in[u], 16 * (i + 1))
                pe.wait_ge(lo_done, t + 1)
                for k in range(NK):
                    ins = nc.tensor.transpose(xt[u][:, k * P:(k + 1) * P], x[u][:, k * KC:(k + 1) * KC], ident[:])
                ins.then_inc(x_transposed, 1)

            def project(t, u, i):
                pe.wait_ge(lo_done, t + 1 + AHEAD)
                pe.wait_ge(acc_free, t + 1)
                for a, b in ((xh, wh), (xl, wh), (xh, wlo)):
                    for k in range(NK):
                        ins = nc.tensor.matmul(acc[u][:, 0:D], a[:, u, k, :], b[:, k, :],
                                               start=(a is xh and b is wh and k == 0), stop=(b is wlo and k == NK - 1))
                ins.then_inc(mm_done, 1)

            skewed(pe, NT, transpose, project)


def normalise(nc, z, h, xh, xl, ident16, tag, affine=None):
    ctx = ExitStack()
    with ctx:
        sb, pst, sem = scope(nc, ctx, tag)
        st, mv, rstd = sb("st", [P, NT, 6]), sb("mv", [P, NT, 2]), sb("rstd", [P, NT])
        sh, sl = sb("sh", [P, NT, 2 * P], F16), sb("sl", [P, NT, 2 * P], F16)
        gb = sb("gb", [P, 2, D])
        ts = [pst(f"ts{u}", [P, 4, P], F16) for u in range(2)]
        link, var_done, std_done, h_done, hi_done, lo_done, t_done, t_used, gb_in = (
            sem(n) for n in ("link", "var_done", "std_done", "h_done", "hi_done", "lo_done", "t_done", "t_used", "gb_in"))
        halves = ((slice(0, P), slice(0, P)), (slice(P, P + DB), slice(P, D)), (slice(P + DB, 2 * P), slice(P, D)))
        block = ctx.enter_context(nc.Block())

        @block.vector
        def _(dve):
            ch = Chain(dve, link)
            if z is not None:
                for t in range(NT):
                    ins = nc.vector.bn_stats(st[:, t, :], z[:, t, :])
                ch.link(ins)
                for t in range(NT):
                    ins = nc.vector.bn_aggr(mv[:, t, :], st[:, t, :])
                ch.link(ins)
                nc.vector.tensor_scalar(rstd[:], mv[:, :, 1], EPS, None, ALU.add).then_inc(var_done, 1)
                dve.wait_ge(std_done, 1)
                ch.link(nc.vector.reciprocal(rstd[:], rstd[:]))
                for t in range(NT):
                    ins = nc.vector.tensor_scalar(h[:, t, :], z[:, t, :], mv[:, t, 0:1], rstd[:, t:t + 1], ALU.subtract, ALU.mult)
                ch.link(ins)
                if affine is not None:
                    dve.wait_ge(gb_in, 32)
                    for j, op in ((0, ALU.mult), (1, ALU.add)):
                        ch.link(nc.vector.tensor_tensor(h[:], h[:], gb[:, j:j + 1, :].to_broadcast([P, NT, D]), op))
            nc.vector.engine_nop().then_inc(h_done, 1)
            dve.wait_ge(hi_done, 1)
            for n, (a, b) in enumerate(halves):
                ins = nc.vector.tensor_tensor(sl[:, :, a], h[:, :, b], sh[:, :, a], ALU.subtract)
            ins.then_inc(lo_done, 1)

        @block.scalar
        def _(act):
            if affine is not None:
                for j in range(2):
                    act.dma_start(gb[:, j, :], rows(affine[j], P)).then_inc(gb_in, 16)
            if z is not None:
                act.wait_ge(var_done, 1)
                nc.scalar.activation(rstd[:], rstd[:], ACT.Sqrt).then_inc(std_done, 1)
            act.wait_ge(h_done, 1)
            for n, (a, b) in enumerate(halves):
                ins = nc.scalar.activation(sh[:, :, a], h[:, :, b], ACT.Copy)
            ins.then_inc(hi_done, 1)

            def unload(t, u, i):
                act.wait_ge(t_done, t + 1)
                nc.scalar.activation(xh[:, :, t, :], ts[u][:, 0:2, :], ACT.Copy)
                nc.scalar.activation(xl[:, :, t, :], ts[u][:, 2:4, :], ACT.Copy).then_inc(t_used, 1)

            act.sem_inc(t_used, AHEAD)
            pairs(act, NT, unload)

        @block.tensor
        def _(pe):
            pe.wait_ge(hi_done, 1)
            pe.wait_ge(lo_done, 1)

            def transpose(t, u, i):
                pe.wait_ge(t_used, t + 1)
                for n, s in enumerate((sh, sh, sl, sl)):
                    ins = nc.tensor.transpose(ts[u][:, n, :], s[:, t, (n % 2) * P:(n % 2 + 1) * P], ident16[:])
                ins.then_inc(t_done, 1)

            pairs(pe, NT, transpose)


def dynamic_convolution(nc, dr, h, xh, xl):
    ctx = ExitStack()
    with ctx:
        sb, pst, sem = scope(nc, ctx, "dc_")
        xa, xb = sb("xa", [P, NTP, P]), sb("xb", [P, HTP, P])
        ca, cb = sb("ca", [P, NT, P]), sb("cb", [P, HT, P])
        csh, csl = sb("csh", [P, NT + HT, P], F16), sb("csl", [P, NT + HT, P], F16)
        wdw, wpb = sb("wdw", [P, 2, K]), sb("wpb", [P, 2])
        wst = sb("wst", [P, 2 * P + 2 * HA * K + 2 * D])
        wh, wl = (sb(n, [P, 2 * P + 2 * HA * K + 2 * D], F16) for n in ("wh", "wl"))
        akb, ptb = sb("akb", [P, H * K]), sb("ptb", [P, D])
        kern = sb("kern", [P, NT, H * K])
        mx, rs = sb("mx", [P, NT * H]), sb("rs", [P, NT * H])
        v = sb("v", [P, NTP, D])
        prod = [sb(f"prod{u}", [P, NT, D]) for u in range(2)]
        pw = [pst(f"pw{u}", [P, 512]) for u in range(2)]
        pk = [pst(f"pk{u}", [P, 512]) for u in range(2)]
        pv = [pst(f"pv{u}", [P, 512]) for u in range(2)]
        w_in, bias_in, w_hi, w_ready, link, plink = (sem(n) for n in ("w_in", "bias_in", "w_hi", "w_ready", "link", "plink"))
        x_ready, edges, conv_done, pw_done, ca_done, c_hi, c_lo = (
            sem(n) for n in ("x_ready", "edges", "conv_done", "pw_done", "ca_done", "c_hi", "c_lo"))
        k_done, k_out, v_done, v_out, centred, exp_done, halo, prod_done, prod_used = (
            sem(n) for n in ("k_done", "k_out", "v_done", "v_out", "centred", "exp_done", "halo", "prod_done", "prod_used"))
        O_AK, O_PT = 2 * P, 2 * P + 2 * HA * K
        NAK = HA * K
        CH = [(0, 3 * c) for c in range(NT // 3)] + [(1, 3 * c) for c in range(HT // 3)]
        block = ctx.enter_context(nc.Block())

        @block.sync
        def _(sp):
            sp.dma_start(wst[:], dr["dc_w"]).then_inc(w_in, 16)
            sp.dma_start(wdw[:], dr["dc_dw"]).then_inc(bias_in, 16)
            sp.dma_start(wpb[:], dr["dc_pwb"]).then_inc(bias_in, 16)
            sp.dma_start(akb[:], rows(dr["dc_akb"], P)).then_inc(bias_in, 16)
            sp.dma_start(ptb[:], rows(dr["dc_ptb"], P)).then_inc(bias_in, 16)
            sp.wait_ge(v_out, NT + AHEAD)
            sp.wait_ge(edges, 1)
            with nc.allow_non_contiguous_dma(reason="rows of other partitions"):
                sp.dma_start(v[1:P:2, 0:PAD, :], v[0:P:2, NT:NT + PAD, :]).then_inc(halo, 16)
                sp.dma_start(v[0:P:2, NT + PAD:NTP, :], v[1:P:2, PAD:2 * PAD, :]).then_inc(halo, 16)

        @block.gpsimd
        def _(pool):
            ch = Chain(pool, plink)
            nc.gpsimd.memset(v[:, 0:PAD, :], 0.0)
            nc.gpsimd.memset(v[:, NT + PAD:NTP, :], 0.0).then_inc(edges, 1)
            nc.gpsimd.memset(xa[:, 0:PAD, :], 0.0)
            nc.gpsimd.memset(xa[:, NT + PAD:NTP, :], 0.0)
            nc.gpsimd.memset(xb[:, 0:PAD, :], 0.0)
            ch.link(nc.gpsimd.memset(xb[:, HT + PAD:HTP, :], 0.0))
            ch.link(nc.gpsimd.tensor_tensor(xa[:, PAD:PAD + NT, :], xh[:, 0], xl[:, 0], ALU.add))
            ch.link(nc.gpsimd.tensor_tensor(xb[0:DB, PAD:HTP, :], xh[0:DB, 1, 0:HT + PAD], xl[0:DB, 1, 0:HT + PAD], ALU.add))
            ch.link(nc.gpsimd.tensor_tensor(xb[DB:P, 0:HT + PAD, :], xh[DB:P, 1, HT - PAD:NT], xl[DB:P, 1, HT - PAD:NT], ALU.add))
            odd, even = slice(1, P, 2), slice(0, P, 2)
            ch.link(nc.gpsimd.tensor_copy(xa[:, 0:PAD, odd], xa[:, NT:NT + PAD, even]))
            ch.link(nc.gpsimd.tensor_copy(xa[:, NT + PAD:NTP, even], xa[:, PAD:2 * PAD, odd]))
            ch.link(nc.gpsimd.tensor_tensor(xb[0:DB, 0:PAD, odd], xh[0:DB, 1, NT - PAD:NT, even], xl[0:DB, 1, NT - PAD:NT, even], ALU.add))
            nc.gpsimd.tensor_tensor(xb[DB:P, HT + PAD:HTP, even], xh[DB:P, 1, 0:PAD, odd], xl[DB:P, 1, 0:PAD, odd], ALU.add).then_inc(x_ready, 1)
            pool.wait_ge(x_ready, 1)
            for n, (g, t0) in enumerate(CH):
                pool.wait_ge(c_hi, n + 1)
                c = (ca, cb)[g]
                o = NT * g + t0
                nc.gpsimd.tensor_tensor(csl[:, o:o + 3, :], c[:, t0:t0 + 3, :], csh[:, o:o + 3, :], ALU.subtract).then_inc(c_lo, 1)
            for k in range(K):
                pool.wait_ge(prod_done, k + 1)
                if k:
                    pool.wait_ge(prod_used, k)
                nc.gpsimd.tensor_tensor(h[:], h[:], prod[k % 2][:], ALU.add).then_inc(prod_used, 1)

        @block.scalar
        def _(act):
            act.sem_inc(v_out, AHEAD)
            act.wait_ge(w_in, 16)
            nc.scalar.activation(wh[:], wst[:], ACT.Copy, scale=WS).then_inc(w_hi, 1)
            for n, (g, t0) in enumerate(CH):
                act.wait_ge(ca_done, n + 1)
                c = (ca, cb)[g]
                o = NT * g + t0
                nc.scalar.activation(csh[:, o:o + 3, :], c[:, t0:t0 + 3, :], ACT.Copy).then_inc(c_hi, 1)
            act.wait_ge(centred, 1)
            nc.scalar.activation(kern[:], kern[:], ACT.Exp).then_inc(exp_done, 1)

        @block.vector
        def _(dve):
            ch = Chain(dve, link)
            dve.sem_inc(k_out, AHEAD)
            dve.wait_ge(bias_in, 64)
            dve.wait_ge(w_hi, 1)
            ch.link(nc.vector.scalar_tensor_tensor(wl[:], wst[:], WS, wh[:], ALU.mult, ALU.subtract))
            nc.vector.tensor_copy(wh[DB:P, O_PT + D:], wl[DB:P, O_PT + D:]).then_inc(w_ready, 1)

            def values(t, u, i):
                dve.wait_ge(v_done, t + 1)
                nc.vector.scalar_tensor_tensor(v[:, PAD + t, :], pv[u][:, 0:D], 1.0 / WS, ptb[:], ALU.mult, ALU.add).then_inc(v_out, 1)

            pairs(dve, NT, values)
            dve.wait_ge(x_ready, 1)
            for x, c, n, g in ((xa, ca, NT, 0), (xb, cb, HT, 1)):
                ch.link(nc.vector.tensor_scalar(c[:], x[:, 0:n, :], wdw[:, g, 0:1], None, ALU.mult))
                for k in range(1, K):
                    ch.link(nc.vector.scalar_tensor_tensor(c[:], x[:, k:k + n, :], wdw[:, g, k:k + 1], c[:], ALU.mult, ALU.add))
                nc.vector.engine_nop().then_inc(conv_done, 1)
            for n, (g, t0) in enumerate(CH):
                x, c = ((xa, ca), (xb, cb))[g]
                dve.wait_ge(pw_done, n + 1)
                ch.link(nc.vector.tensor_scalar(c[:, t0:t0 + 3, :], pw[n % 2][:, 0:3 * P].rearrange("p (t q) -> p t q", t=3), wpb[:, g:g + 1], None, ALU.add))
                nc.vector.tensor_tensor(c[:, t0:t0 + 3, :], c[:, t0:t0 + 3, :], x[:, PAD + t0:PAD + t0 + 3, :], ALU.mult).then_inc(ca_done, 1)
            with dve.Fori(0, HT) as t:
                dve.wait_ge(k_done, t + 1)
                nc.vector.scalar_tensor_tensor(kern[:, t, :], pk[0][:, 0:H * K], 1.0 / WS, akb[:], ALU.mult, ALU.add)
                nc.vector.scalar_tensor_tensor(kern[:, t + HT, :], pk[0][:, H * K:2 * H * K], 1.0 / WS, akb[:], ALU.mult, ALU.add).then_inc(k_out, 1)
            dve.wait_ge(k_out, HT + AHEAD)
            k3 = kern[:].rearrange("p t (h k) -> p (t h) k", k=K)
            wide = lambda a: a[:].rearrange("p (n a) -> p n a", a=1).to_broadcast([P, NT * H, K])
            ch.link(nc.vector.tensor_reduce(mx[:], k3, AX, ALU.max))
            nc.vector.tensor_tensor(k3, k3, wide(mx), ALU.subtract).then_inc(centred, 1)
            dve.wait_ge(exp_done, 1)
            ch.link(nc.vector.tensor_reduce(rs[:], k3, AX, ALU.add))
            ch.link(nc.vector.reciprocal(rs[:], rs[:]))
            ch.link(nc.vector.tensor_tensor(k3, k3, wide(rs), ALU.mult))
            dve.wait_ge(halo, 32)
            for k in range(K):
                if k >= 2:
                    dve.wait_ge(prod_used, k - 1)
                nc.vector.tensor_tensor(prod[k % 2][:].rearrange("p t (h d) -> p (t h) d", d=IPG),
                                        v[:, k:k + NT, :].rearrange("p t (h d) -> p (t h) d", d=IPG),
                                        k3[:, :, k:k + 1].to_broadcast([P, NT * H, IPG]), ALU.mult).then_inc(prod_done, 1)

        @block.tensor
        def _(pe):
            pe.wait_ge(w_ready, 1)

            def values(t, u, i):
                pe.wait_ge(v_out, t + 1)
                five(nc, pv[u][:, 0:D], xh[:, :, t, :], xl[:, :, t, :], wh[:, O_PT:O_PT + D], wl[:, O_PT:O_PT + D],
                     wh[:, O_PT + D:]).then_inc(v_done, 1)

            pairs(pe, NT, values)
            for n, (g, t0) in enumerate(CH):
                pe.wait_ge(conv_done, g + 1)
                if n >= 2:
                    pe.wait_ge(ca_done, n - 1)
                c = (ca, cb)[g]
                nc.tensor.matmul(pw[n % 2][:, 0:3 * P], wst[:, g * P:(g + 1) * P], c[:, t0:t0 + 3, :], start=True, stop=True).then_inc(pw_done, 1)
            pe.wait_ge(c_lo, len(CH))
            with pe.Fori(0, HT) as t:
                pe.wait_ge(k_out, t + 2)
                for j, (o, n) in enumerate(((t, 0), (t + HT, 0), (t + NT, 1))):
                    if n == 0:
                        out = pk[0][:, j * H * K:j * H * K + NAK]
                    else:
                        out = pk[0][:, 0:2 * H * K].rearrange("p (a k) -> p a k", a=2)[:, :, NAK:H * K]
                    w = slice(O_AK + n * NAK, O_AK + (n + 1) * NAK)
                    nc.tensor.matmul(out, csh[:, o, :], wh[:, w], start=True, stop=False)
                    nc.tensor.matmul(out, csl[:, o, :], wh[:, w], start=False, stop=False)
                    ins = nc.tensor.matmul(out, csh[:, o, :], wl[:, w], start=False, stop=True)
                ins.then_inc(k_done, 1)


def experts(nc, dr, x, h, xh, xl, idents, slots, sums, tag, hid, gated, shared):
    ident, tri, ones16 = idents
    ne = E + shared
    nm = hid // P
    nw = 2 * hid if gated else hid
    wcol = nw // 2
    n2 = nm * D
    O_B, O_AL, O_2H, O_2L, COLS = nw, 2 * nw, 3 * nw, 3 * nw + n2, 3 * nw + 2 * n2
    NS = NT * shared
    R = RING
    ctx = ExitStack()
    with ctx:
        sb, pst, sem = scope(nc, ctx, tag)
        w = sb("w", [P, ne, COLS], F16)
        wst = [sb(f"wst{u}", [P, 2 * nw + n2]) for u in range(2)]
        rst, rh, rl = sb("rst", [P, 2, E]), sb("rh", [P, 2, E], F16), sb("rl", [P, 2, E], F16)
        lg, pr, sel1, sel2, tmp = (sb(n, [P, NT, E]) for n in ("lg", "pr", "sel1", "sel2", "tmp"))
        both = sb("both", [P, E, NT], F16)
        rank, tot, incl, ones = (sb(n, [P, E, NT]) for n in ("rank", "tot", "incl", "ones"))
        consts = sb("consts", [P, E + NT + NB])
        cnt, nblk, iblk, start = (sb(n, [P, E]) for n in ("cnt", "nblk", "iblk", "start"))
        m, m1, m2, rd = (sb(n, [P, NT]) for n in ("m", "m1", "m2", "rd"))
        pos = sb("pos", [P, 2, NT], I32)
        ebt, ebf, eb = sb("ebt", [1, NB, E]), sb("ebf", [1, NB]), sb("eb", [1, NB], I32)
        fill = sb("fill", [P, R, ROW])
        xr = sb("xr", [P, 2, NT, ROW])
        z = xr[:].rearrange("p a t c -> p (a t c)")[:, 0:2 * NT * D].rearrange("p (t a c) -> p t a c", a=2, c=D)
        xb = [sb(f"xb{u}", [P, ROW + DB]) for u in range(R)]
        xsh, xsl = sb("xsh", [P, 2, 2, P], F16), sb("xsl", [P, 2, 2, P], F16)
        act_out = [sb(f"act{u}", [P, hid]) for u in range(2)] if gated else None
        g = [sb(f"g{u}", [P, hid]) for u in range(2)]
        gh, gl = sb("gh", [P, 2, nm, P], F16), sb("gl", [P, 2, nm, P], F16)
        ys = [sb(f"ys{u}", [P, D]) for u in range(R)]
        ph = [[pst(f"ph{u}{k}", [P, 512]) for k in range(2)] for u in range(2)]
        px = pst("px", [P, 512])
        pt = pst("pt", [P, nm * P])
        py = pst("py", [P, 512])
        w_in = [sem(f"w_in{u}") for u in range(2)]
        (w_split, w_hi, r_in, r_hi, r_ready, l_done, l_out, link, centred, exp_done, both_done, rank_done, consts_in) = (
            sem(n) for n in ("w_split", "w_hi", "r_in", "r_hi", "r_ready", "l_done", "l_out", "link", "centred", "exp_done",
                             "both_done", "rank_done", "consts_in"))
        fill_set, filled, rows_copied, rows_marked, routed, scattered, sums_in, y_seen = (
            sem(n) for n in ("fill_set", "filled", "rows_copied", "rows_marked", "routed", "scattered", "sums_in", "y_seen"))
        h_done, g_done, t_done, y_done = (sem(n) for n in ("h_done", "g_done", "t_done", "y_done"))
        xl_done, gl_done, y_out = (sem(n) for n in ("xl_done", "gl_done", "y_out"))
        xt_done, xh_done, silu_done, gh_done = (sem(n) for n in ("xt_done", "xh_done", "silu_done", "gh_done"))
        x_in, y_sent = ([sem(f"{n}{u}") for u in range(R)] for n in ("x_in", "y_sent"))
        block = ctx.enter_context(nc.Block())

        @block.sync
        def _(sp):
            sp.dma_start(consts[:], rows(dr["consts"], P)).then_inc(consts_in, 16)
            sp.dma_start(rst[:], dr[tag + "router"]).then_inc(r_in, 16)
            sp.wait_ge(fill_set, 2)
            for u in range(R):
                sp.dma_start(slots.rearrange("(b p) c -> p b c", p=P)[:, u:NB:R, :],
                             fill[:, u:u + 1, :].to_broadcast([P, len(range(u, NB, R)), ROW])).then_inc(filled, 16)
            for e in range(ne):
                if e >= 2:
                    sp.wait_ge(w_split, e - 1)
                e_ = (e - shared) % ne
                sp.dma_start(wst[e % 2][:], dr[tag + "w"][e_]).then_inc(w_in[e % 2], 16)
            sp.wait_ge(scattered, 16 * 2 * NT)

            def load(n, u, q):
                at = bass.ds(n * P, P)
                sp.dma_start(xb[u][:, 0:D], slots[at, 0:D]).then_inc(x_in[u], 16)
                sp.dma_start(xb[u][:, D:D + ROW - P], slots[at, P:ROW]).then_inc(x_in[u], 16)

            for n in range(R):
                load(n, n, 0)

            def reload(n, u, q):
                sp.wait_ge(y_sent[u], 16 * (q + 1))
                load(n + R, u, q + 1)

            pipelined(sp, NB - R, R, (0, reload))
            for u in range(R):
                sp.wait_ge(y_sent[u], 16 * len(range(u, NB, R)))
            sp.dma_start(z, sums[0:2 * T, :].rearrange("(p t a) c -> p t a c", t=NT, a=2)).then_inc(sums_in, 16)

        @block.gpsimd
        def _(pool):
            nc.gpsimd.memset(fill[:, :, 0:ROW - 1], 0.0).then_inc(fill_set, 1)
            nc.gpsimd.iota(fill[:, :, ROW - 1:ROW].bitcast(I32), pattern=[[P, R]], base=2 * T, channel_multiplier=1).then_inc(fill_set, 1)
            nc.gpsimd.memset(ones[:], 1.0)
            for a in range(2):
                nc.gpsimd.iota(xr[:, a, :, ROW - 1:ROW].bitcast(I32), pattern=[[2, NT]], base=a, channel_multiplier=2 * NT)
            nc.gpsimd.tensor_copy(xr[:, 1, :, 0:D], x[:]).then_inc(rows_marked, 1)
            pool.wait_ge(rows_copied, 1)
            pool.wait_ge(rows_marked, 1)
            pool.wait_ge(filled, 16 * R)
            pool.wait_ge(routed, 1)
            for t in range(NT):
                for a in range(2):
                    nc.gpsimd.indirect_dma_start(out=slots, out_offset=bass.IndirectOffsetOnAxis(ap=pos[:, a, t:t + 1], axis=0),
                                                 in_=xr[:, a, t, :], in_offset=None).then_inc(scattered, 16)

            def send(n, u, q):
                pool.wait_ge(y_out, NS + n + 2)
                pool.sem_inc(y_seen, 1)
                nc.gpsimd.indirect_dma_start(out=sums, out_offset=bass.IndirectOffsetOnAxis(ap=xb[u][:, ROW + DB - 1:ROW + DB].bitcast(I32), axis=0),
                                             in_=ys[u][:], in_offset=None).then_inc(y_sent[u], 16)

            pipelined(pool, NB, R, (0, send))

        @block.scalar
        def _(act):
            act.wait_ge(r_in, 16)
            nc.scalar.activation(rh[:], rst[:], ACT.Copy, scale=WS).then_inc(r_hi, 1)

            act.wait_ge(centred, 1)
            nc.scalar.activation(pr[:], lg[:], ACT.Exp).then_inc(exp_done, 1)
            nc.scalar.activation(xr[:, 0, :, 0:D], x[:], ACT.Copy).then_inc(rows_copied, 1)

            def split_weights(v, i):
                e_ = E * shared if type(i) is int and v + 2 * i == 0 else v + 2 * i - shared
                act.wait_ge(w_in[v], 16 * (i + 1))
                nc.scalar.activation(w[:, e_, 0:2 * nw], wst[v][:, 0:2 * nw], ACT.Copy, scale=WS)
                nc.scalar.activation(w[:, e_, O_2H:O_2L], wst[v][:, 2 * nw:], ACT.Copy, scale=WS).then_inc(w_hi, 1)

            def more_weights(n, u, q):
                if u % 2 and not (type(q) is int and q > 0):
                    split_weights(*((1, q) if u == 1 else (0, q + 1)))

            split_weights(0, 0)
            if not shared:
                for e in range(1, ne):
                    split_weights(e % 2, e // 2)

            def rows_hi(n, u, q):
                act.wait_ge(xt_done, n + 1)
                act.wait_ge(h_done, NS + n + 1)
                nc.scalar.activation(xsh[:, u % 2], px[:, 0:2 * P].rearrange("p (c q) -> p c q", c=2), ACT.Copy).then_inc(xh_done, 1)

            def silu_of(base):
                def silu(n, u, q):
                    v = u % 2
                    act.wait_ge(h_done, base + n + 1 + AHEAD)
                    if gated:
                        act.wait_ge(g_done, base + n + 1)
                        nc.scalar.activation(act_out[v][:], ph[v][0][:, 0:hid], ACT.Silu, scale=1.0 / WS).then_inc(silu_done, 1)
                    else:
                        act.wait_ge(t_done, base + n + 1)
                        nc.scalar.activation(g[v][:, 0:wcol], ph[v][0][:, 0:wcol], ACT.Silu, scale=1.0 / WS)
                        nc.scalar.activation(g[v][:, wcol:], ph[v][1][:, 0:wcol], ACT.Silu, scale=1.0 / WS).then_inc(g_done, 1)
                return silu

            def hidden_hi_of(base):
                def hidden_hi(n, u, q):
                    act.wait_ge(t_done, base + n + 1 + AHEAD)
                    act.wait_ge(y_done, base + n + 1)
                    nc.scalar.activation(gh[:, u % 2], pt[:].rearrange("p (m q) -> p m q", m=nm), ACT.Copy).then_inc(gh_done, 1)
                return hidden_hi

            if shared:
                pipelined(act, NS, 4, (2, silu_of(0)), (1, hidden_hi_of(0)), (0, more_weights))
            pipelined(act, NB, R, (3, rows_hi), (2, silu_of(NS)), (1, hidden_hi_of(NS)))

        @block.vector
        def _(dve):
            ch = Chain(dve, link)
            dve.sem_inc(g_done, AHEAD)
            dve.sem_inc(l_out, AHEAD)
            for one in (y_out, gl_done, xl_done):
                dve.sem_inc(one, 1)
            if not shared:
                ch.link(nc.vector.tensor_scalar(h[:], h[:], 2.0, None, ALU.mult))
            dve.wait_ge(r_hi, 1)
            ch.link(nc.vector.scalar_tensor_tensor(rl[:], rst[:], WS, rh[:], ALU.mult, ALU.subtract))
            nc.vector.tensor_copy(rh[DB:P, 1, :], rl[DB:P, 1, :]).then_inc(r_ready, 1)

            def logits(t, u, i):
                dve.wait_ge(l_done, t + 1)
                nc.vector.tensor_scalar(lg[:, t, :], ph[u][0][:, 0:E], 1.0 / WS, None, ALU.mult).then_inc(l_out, 1)

            def split_weights(v, i):
                e_ = E * shared if type(i) is int and v + 2 * i == 0 else v + 2 * i - shared
                dve.wait_ge(w_hi, v + 2 * i + 1)
                st = wst[v]
                nc.vector.scalar_tensor_tensor(w[:, e_, O_AL:O_2H], st[:, 0:nw], WS, w[:, e_, 0:nw], ALU.mult, ALU.subtract)
                nc.vector.scalar_tensor_tensor(w[DB:P, e_, O_B:O_AL], st[DB:P, nw:2 * nw], WS, w[DB:P, e_, O_B:O_AL], ALU.mult, ALU.subtract)
                nc.vector.scalar_tensor_tensor(w[:, e_, O_2L:COLS], st[:, 2 * nw:], WS, w[:, e_, O_2H:O_2L], ALU.mult, ALU.subtract).then_inc(w_split, 1)

            def more_weights(n, u, q):
                if u % 2 and not (type(q) is int and q > 0):
                    split_weights(*((1, q) if u == 1 else (0, q + 1)))

            pairs(dve, NT, logits)
            dve.wait_ge(l_out, NT + AHEAD)
            over = lambda a, n: a.rearrange("p (n a) -> p n a", a=1).to_broadcast([a.shape[0], a.shape[1], n])
            each = lambda a, n: a.rearrange("p (a n) -> p a n", a=1).to_broadcast([a.shape[0], n, a.shape[1]])
            TT, TR = nc.vector.tensor_tensor, nc.vector.tensor_reduce
            ch.link(TR(m[:], lg[:], AX, ALU.max))
            TT(lg[:], lg[:], over(m[:], E), ALU.subtract).then_inc(centred, 1)
            dve.wait_ge(exp_done, 1)
            ch.link(TR(m[:], pr[:], AX, ALU.add))
            ch.link(nc.vector.reciprocal(m[:], m[:]))
            ch.link(TT(pr[:], pr[:], over(m[:], E), ALU.mult))
            dve.wait_ge(consts_in, 16)
            order, blocks_of, block_no = consts[:, 0:E], consts[:, E:E + NT], consts[:, E + NT:]
            for mk, sel in ((m1, sel1), (m2, sel2)):
                ch.link(TR(mk[:], pr[:], AX, ALU.max))
                ch.link(TT(sel[:], pr[:], over(mk[:], E), ALU.is_ge))
                ch.link(TT(sel[:], sel[:], each(order, NT), ALU.mult))
                ch.link(TR(m[:], sel[:], AX, ALU.max))
                ch.link(TT(sel[:], sel[:], over(m[:], E), ALU.is_equal))
                if mk is m1:
                    ch.link(nc.vector.scalar_tensor_tensor(pr[:], sel[:], -2.0, pr[:], ALU.mult, ALU.add))
            TT(both[:].rearrange("p e t -> p t e"), sel1[:], sel2[:], ALU.add).then_inc(both_done, 1)
            ch.link(TT(rd[:], m1[:], m2[:], ALU.add))
            if shared:
                ch.link(nc.vector.tensor_scalar(rd[:], rd[:], 1e-20, None, ALU.add))
            ch.link(nc.vector.reciprocal(rd[:], rd[:]))
            dve.wait_ge(rows_marked, 1)
            for a, mk in ((0, m1), (1, m2)):
                nc.vector.scalar_tensor_tensor(xr[:, a, :, D], mk[:], 1.0 / WS, rd[:], ALU.mult, ALU.mult)
            dve.wait_ge(rank_done, 1)
            flat = lambda a: a[:].rearrange("p e t -> p (e t)")
            ch.link(nc.vector.tensor_copy(flat(tot), ph[0][1][:, 0:E * NT]))
            ch.link(nc.vector.tensor_tensor_scan(flat(incl), flat(ones), flat(tot), 0.0, ALU.mult, ALU.add))
            ch.link(TT(tot[:], incl[:], tot[:], ALU.subtract))
            ch.link(TT(cnt[:], incl[:, :, NT - 1], tot[:, :, 0], ALU.subtract))
            ch.link(TT(incl[:], over(cnt[:], NT), each(blocks_of, E), ALU.is_gt))
            ch.link(TR(nblk[:], incl[:], AX, ALU.add))
            ch.link(nc.vector.tensor_tensor_scan(iblk[:], ones[:, 0, 0:E], nblk[:], 0.0, ALU.mult, ALU.add))
            ch.link(TT(start[:], iblk[:], nblk[:], ALU.subtract))
            ch.link(nc.vector.scalar_tensor_tensor(start[:], start[:], float(P), tot[:, :, 0], ALU.mult, ALU.subtract))
            ch.link(TT(flat(rank), ph[0][0][:, 0:E * NT], flat(tot), ALU.add))
            ch.link(TT(rank[:], rank[:], over(start[:], NT), ALU.add))
            for a, sel in ((0, sel1), (1, sel2)):
                ch.link(TT(tmp[:], sel[:], rank[:].rearrange("p e t -> p t e"), ALU.mult))
                ch.link(TR(m[:], tmp[:], AX, ALU.add))
                ch.link(nc.vector.tensor_copy(pos[:, a, :], m[:]))
            ch.link(TT(ebt[:], over(block_no[0:1], E), each(iblk[0:1, :], NB), ALU.is_ge))
            ch.link(TR(ebf[:], ebt[:], AX, ALU.add))
            ch.link(nc.vector.tensor_scalar(ebf[:], ebf[:], float(E - 1), None, ALU.min))
            nc.vector.tensor_copy(eb[:], ebf[:]).then_inc(routed, 1)
            dve.wait_ge(rows_copied, 1)
            split_weights(0, 0)
            if not shared:
                for e in range(1, ne):
                    split_weights(e % 2, e // 2)

            def rows_lo(n, u, q):
                dve.wait_ge(xh_done, n + 1)
                dve.wait_ge(h_done, NS + n + 1)
                TT(xsl[:, u % 2], px[:, 0:2 * P].rearrange("p (c q) -> p c q", c=2), xsh[:, u % 2], ALU.subtract).then_inc(xl_done, 1)

            def gate_of(base):
                def gate(n, u, q):
                    v = u % 2
                    if gated:
                        dve.wait_ge(silu_done, base + n + 1)
                        dve.wait_ge(t_done, base + n + 1)
                        nc.vector.scalar_tensor_tensor(g[v][:], ph[v][1][:, 0:hid], 1.0 / WS, act_out[v][:], ALU.mult, ALU.mult).then_inc(g_done, 1)
                return gate

            def hidden_lo_of(base):
                def hidden_lo(n, u, q):
                    dve.wait_ge(gh_done, base + n + 1)
                    TT(gl[:, u % 2], pt[:].rearrange("p (m q) -> p m q", m=nm), gh[:, u % 2], ALU.subtract).then_inc(gl_done, 1)
                return hidden_lo

            def add_shared(n, u, q):
                dve.wait_ge(y_done, n + 1 + AHEAD)
                nc.vector.scalar_tensor_tensor(h[:, n, :], py[:, 0:D], 1.0 / WS, h[:, n, :], ALU.mult, ALU.add).then_inc(y_out, 1)

            def share(n, u, q):
                dve.wait_ge(y_done, NS + n + 1 + AHEAD)
                nc.vector.tensor_scalar(ys[u][:], py[:, 0:D], xb[u][:, ROW + DB - 2:ROW + DB - 1], None, ALU.mult).then_inc(y_out, 1)

            if shared:
                pipelined(dve, NS, 4, (2, gate_of(0)), (1, hidden_lo_of(0)), (0, add_shared), (0, more_weights))
            pipelined(dve, NB, R, (3, rows_lo), (2, gate_of(NS)), (1, hidden_lo_of(NS)), (0, share))
            dve.wait_ge(sums_in, 16)
            for a in range(2):
                ch.link(TT(h[:], h[:], z[:, :, a, :], ALU.add))

        @block.tensor
        def _(pe):
            for two in (h_done, t_done, y_done):
                pe.sem_inc(two, AHEAD)
            pe.wait_ge(r_ready, 1)

            def logits(t, u, i):
                pe.wait_ge(l_out, t + 1)
                five(nc, ph[u][0][:, 0:E], xh[:, :, t, :], xl[:, :, t, :], rh[:, 0, :], rl[:, 0, :], rh[:, 1, :]).then_inc(l_done, 1)

            pairs(pe, NT, logits)
            pe.wait_ge(both_done, 1)
            cols = both[:].rearrange("p e t -> p (e t)")
            nc.tensor.matmul(ph[0][0][:, 0:E * NT], tri[:], cols, start=True, stop=True)
            nc.tensor.matmul(ph[0][1][:, 0:E * NT], ones16[:], cols, start=True, stop=True).then_inc(rank_done, 1)
            pe.wait_ge(routed, 1)

            sorted_rows = lambda n, v: (xsh[:, v], xsl[:, v])

            def first_of(base, parts, expert):
                def first(n, u, q):
                    v = u % 2
                    e = expert(n)
                    if parts is sorted_rows:
                        pe.wait_ge(xl_done, n + 2)
                    pe.wait_ge(g_done, base + n + 1)
                    for k in range(2):
                        c = k * wcol
                        ins = five(nc, ph[v][k][:, 0:wcol], *parts(n, v), w[:, e, c:c + wcol],
                                   w[:, e, O_AL + c:O_AL + c + wcol], w[:, e, O_B + c:O_B + c + wcol])
                    ins.then_inc(h_done, 1)
                return first

            def second_of(base, expert):
                def second(n, u, q):
                    v = u % 2
                    e = expert(n)
                    pe.wait_ge(gl_done, base + n + 2)
                    pe.wait_ge(y_out, base + n + 1)
                    for j, (a, o) in enumerate(((gh, O_2H), (gl, O_2H), (gh, O_2L))):
                        for k in range(nm):
                            ins = nc.tensor.matmul(py[:, 0:D], a[:, v, k, :], w[:, e, o + k * D:o + (k + 1) * D],
                                                   start=(j == 0 and k == 0), stop=(j == 2 and k == nm - 1))
                    ins.then_inc(y_done, 1)
                return second

            def turn_of(base):
                def turn(n, u, q):
                    v = u % 2
                    pe.wait_ge(g_done, base + n + 1 + AHEAD)
                    pe.wait_ge(gl_done, base + n + 1)
                    for k in range(nm):
                        ins = nc.tensor.transpose(pt[:, k * P:(k + 1) * P], g[v][:, k * P:(k + 1) * P], ident[:])
                    ins.then_inc(t_done, 1)
                return turn

            def rows_in(n, u, q):
                pe.wait_ge(x_in[u], 32 * (q + 1))
                pe.wait_ge(xl_done, n + 1)
                nc.tensor.transpose(px[:, 0:P], xb[u][:, 0:P], ident[:])
                nc.tensor.transpose(px[:, P:2 * P], xb[u][:, P:2 * P], ident[:]).then_inc(xt_done, 1)

            if shared:
                pe.wait_ge(w_split, 1)
                own = lambda n: E
                pipelined(pe, NS, 4, (2, first_of(0, lambda n, v: (xh[:, :, n, :], xl[:, :, n, :]), own)), (1, turn_of(0)), (0, second_of(0, own)))
            pe.wait_ge(w_split, ne)
            by_block = lambda n: pe.value_load(eb[0:1, bass.ds(n, 1)], min_val=0, max_val=E - 1)
            pipelined(pe, NB, R, (3, rows_in), (2, first_of(NS, sorted_rows, by_block)), (1, turn_of(NS)), (0, second_of(NS, by_block)))


def attention_weights(nc, dr, h, w, small):
    wqh, wql, wqb, woh, wol = w
    mask, isc, fold = small
    ctx = ExitStack()
    with ctx:
        sb, pst, sem = scope(nc, ctx, "aw_")
        wst, wost = sb("wst", [P, 2, 3 * INNER]), sb("wost", [P, NM * D])
        bout = sb("bout", [P, D])
        w_in, small_in, w_hi, link = (sem(n) for n in ("w_in", "small_in", "w_hi", "link"))
        block = ctx.enter_context(nc.Block())

        @block.sync
        def _(sp):
            sp.dma_start(bout[:], rows(dr["at_bout"], P)).then_inc(small_in, 16)
            sp.dma_start(mask[:], dr["at_mask"]).then_inc(small_in, 16)
            sp.dma_start(isc[:], dr["at_scale"]).then_inc(small_in, 16)
            sp.dma_start(fold[:], dr["at_fold"]).then_inc(small_in, 16)
            sp.dma_start(wst[:], dr["at_wqkv"]).then_inc(w_in, 16)
            sp.dma_start(wost[:], dr["at_wout"]).then_inc(w_in, 16)

        @block.scalar
        def _(act):
            act.wait_ge(w_in, 32)
            nc.scalar.activation(wqh[:], wst[:, 0], ACT.Copy, scale=WS)
            nc.scalar.activation(wqb[:], wst[:, 1], ACT.Copy, scale=WS)
            nc.scalar.activation(woh[:], wost[:], ACT.Copy, scale=WS).then_inc(w_hi, 1)

        @block.vector
        def _(dve):
            dve.wait_ge(small_in, 64)
            nc.vector.reciprocal(isc[:], isc[:])
            dve.wait_ge(w_hi, 1)
            nc.vector.scalar_tensor_tensor(wql[:], wst[:, 0], WS, wqh[:], ALU.mult, ALU.subtract)
            nc.vector.scalar_tensor_tensor(wqb[DB:P], wst[DB:P, 1], WS, wqb[DB:P], ALU.mult, ALU.subtract)
            nc.vector.scalar_tensor_tensor(wol[:], wost[:], WS, woh[:], ALU.mult, ALU.subtract)

        @block.gpsimd
        def _(pool):
            pool.wait_ge(small_in, 64)
            nc.gpsimd.tensor_tensor(h[:], h[:], bout[:].rearrange("p (a n) -> p a n", a=1).to_broadcast([P, NT, D]), ALU.add)


def attention(nc, dr, h, xh, xl, ident):
    ctx = ExitStack()
    with ctx:
        sb, pst, sem = scope(nc, ctx, "at_")
        GT = PG * NT
        HG = GT // 2
        NH = H1 // 2
        W6 = NH * PAIR
        wqh, wql, wqb = (sb(n, [P, 3 * INNER], F16) for n in ("wqh", "wql", "wqb"))
        woh, wol = sb("woh", [P, NM * D], F16), sb("wol", [P, NM * D], F16)
        mask, isc, fold = sb("mask", [PAIR, PAIR]), sb("isc", [P, NM]), sb("fold", [P, P])
        attention_weights(nc, dr, h, (wqh, wql, wqb, woh, wol), (mask, isc, fold))
        oh, ol = sb("oh", [P, NM, NT, P], F16), sb("ol", [P, NM, NT, P], F16)
        xgh, xgl = sb("xgh", [P, 2, GT], F16), sb("xgl", [P, 2, GT], F16)
        qk = sb("qk", [P, 2 * NM, GT])
        qkh, qkl = sb("qkh", [P, 2 * NM, GT], F16), sb("qkl", [P, 2 * NM, GT], F16)
        eps = sb("eps", [P, 1])
        sq = [sb(f"sq{u}", [P, HG]) for u in range(2)]
        ss = sb("ss", [P, 2, 2, HG])
        vh, vl = sb("vh", [PAIR, 2, INNER], F16), sb("vl", [PAIR, 2, INNER], F16)
        sm = [sb(f"sm{u}", [PAIR, 2, W6]) for u in range(2)]
        mx, rs = [[sb(f"{n}{u}", [PAIR, H1]) for u in range(2)] for n in ("mx", "rs")]
        ph, pl = sb("ph", [PAIR, 2, W6], F16), sb("pl", [PAIR, 2, W6], F16)
        pss = [pst(f"pss{u}", [P, 512]) for u in range(2)]
        pv = [pst(f"pv{u}", [P, 512]) for u in range(2)]
        pt = [pst(f"pt{u}", [P, 512]) for u in range(2)]
        po = [pst(f"po{u}", [P, 512]) for u in range(2)]
        (p_done, p_out, sq_done, sq_used, ss_done, fold_done, root_done, rn_done, scaled, qk_hi, qk_lo) = (sem(n) for n in (
            "p_done", "p_out", "sq_done", "sq_used", "ss_done", "fold_done", "root_done", "rn_done", "scaled", "qk_hi", "qk_lo"))
        (v_done, v_hi, v_lo, s_done, s_out, mx_done, centred, exp_done, rs_done, prob_done, t_done, t_hi, t_lo, o_done, o_hi, o_lo, rs_inv, rn_ready) = (
            sem(n) for n in ("v_done", "v_hi", "v_lo", "s_done", "s_out", "mx_done", "centred", "exp_done", "rs_done", "prob_done",
                             "t_done", "t_hi", "t_lo", "o_done", "o_hi", "o_lo", "rs_inv", "rn_ready"))
        eps_set, grouped = sem("eps_set"), sem("grouped")
        NP = 4 * NM
        block = ctx.enter_context(nc.Block())
        tiles = lambda x, c, lo, n, p, np_: x[:, c, lo:lo + n, bass.ds(p, np_)]
        head = lambda hd: ((hd % 2) * DH, hd // 2)

        @block.tensor
        def _(pe):
            with pe.Fori(0, NPG) as g:
                for n in range(NP):
                    m, hf = n // 2, n % 2
                    pe.wait_ge(p_out, g * NP + n + 1)
                    c = slice(m * P, (m + 1) * P)
                    if n == 0:
                        pe.wait_ge(grouped, g + 1)
                    xs = [x[:, :, hf * HG:(hf + 1) * HG] for x in (xgh, xgl)]
                    five_t(nc, pv[n % 2][:, 0:HG], wqh[:, c], wql[:, c], wqb[:, c], *xs).then_inc(p_done, 1)
                for n in range(4):
                    pe.wait_ge(ss_done, g * 4 + n + 1)
                    pe.wait_ge(root_done, g * 4 + n + 1)
                    nc.tensor.matmul(pt[n % 2][:, 0:HG], fold[:], ss[:, n // 2, n % 2, :], start=True, stop=True).then_inc(fold_done, 1)
                pe.wait_ge(qk_lo, g * 2 * NM + 2 * NM + 1)

                def scores(j):
                    pe.wait_ge(v_lo, g * GP + j + 1)
                    for half in range(2):
                        ins = None
                        xs = [x[:, :, j * PAIR:(j + 1) * PAIR] for x in (xgh, xgl)]
                        c = slice(2 * INNER + half * (INNER // 2), 2 * INNER + (half + 1) * (INNER // 2))
                        ins = five(nc, pv[half][0:PAIR, 0:INNER // 2], *xs, wqh[:, c], wql[:, c], wqb[:, c])
                    ins.then_inc(v_done, 1)
                    pe.wait_ge(s_out, g * GP + j + 1)
                    for hd in range(H1):
                        o, m = head(hd)
                        out = pss[hd % 2][0:PAIR, m * PAIR:(m + 1) * PAIR]
                        part = lambda t, mm: t[o:o + DH, mm, j * PAIR:(j + 1) * PAIR]
                        for k, (a, b) in enumerate(((qkh, qkh), (qkl, qkh), (qkh, qkl))):
                            ins = nc.tensor.matmul(out, part(a, m), part(b, NM + m), start=(k == 0), stop=(k == 2))
                    ins.then_inc(s_done, 1)

                def mix(j):
                    pe.wait_ge(prob_done, g * GP + j + 1)
                    pe.wait_ge(t_lo, g * GP + j + 1)
                    for hd in range(H1):
                        ins = nc.tensor.transpose(pt[hd % 2][0:PAIR, hd // 2 * PAIR:(hd // 2 + 1) * PAIR],
                                                  sm[j % 2][:, hd % 2, hd // 2 * PAIR:(hd // 2 + 1) * PAIR], ident[0:PAIR, 0:PAIR])
                    ins.then_inc(t_done, 1)
                    pe.wait_ge(t_lo, g * GP + j + 2)
                    pe.wait_ge(o_lo, g * GP + j + 1)
                    for hd in range(H1):
                        o, m = head(hd)
                        out = po[0][o:o + DH, m * PAIR:(m + 1) * PAIR]
                        for k, (a, b) in enumerate(((vh, ph), (vl, ph), (vh, pl))):
                            ins = nc.tensor.matmul(out, a[:, j % 2, hd * DH:(hd + 1) * DH], b[:, hd % 2, m * PAIR:(m + 1) * PAIR],
                                                   start=(k == 0), stop=(k == 2))
                    ins.then_inc(o_done, 1)

                scores(0)
                for j in range(GP):
                    if j + 1 < GP:
                        scores(j + 1)
                    mix(j)
            pe.wait_ge(o_hi, NPG * GP)
            pe.wait_ge(o_lo, NPG * GP + 1)

            def project(t, u, i):
                pe.wait_ge(p_out, NPG * NP + t + 1)
                for k, (a, b) in enumerate(((oh, woh), (ol, woh), (oh, wol))):
                    for m in range(NM):
                        ins = nc.tensor.matmul(pv[u][:, 0:D], a[:, m, t, :], b[:, m * D:(m + 1) * D], start=(k == m == 0), stop=(k == 2 and m == NM - 1))
                ins.then_inc(p_done, 1)

            pairs(pe, NT, project)

        @block.scalar
        def _(act):
            act.sem_inc(p_out, AHEAD)
            act.sem_inc(root_done, AHEAD)
            with act.Fori(0, NPG) as g:
                for n in range(NP):
                    m, hf = n // 2, n % 2
                    act.wait_ge(p_done, g * NP + n + 1)
                    act.wait_ge(sq_used, g * NP + n + 1)
                    if n == 0:
                        act.wait_ge(qk_lo, g * 2 * NM + 1)
                        act.wait_ge(scaled, g * 2 * NM + 1)
                    to = ss[:, m // NM, hf, :] if m % NM == 0 else sq[n % 2][:]
                    nc.scalar.activation(to, pv[n % 2][:, 0:HG], ACT.Square, scale=1.0 / WS).then_inc(sq_done, 1)
                    nc.scalar.activation(qk[:, m, hf * HG:(hf + 1) * HG], pv[n % 2][:, 0:HG], ACT.Copy, scale=1.0 / WS).then_inc(p_out, 1)
                for n in range(4):
                    act.wait_ge(fold_done, g * 4 + n + 1)
                    nc.scalar.activation(ss[:, n // 2, n % 2, :], pt[n % 2][:, 0:HG], ACT.Sqrt).then_inc(root_done, 1)
                act.wait_ge(root_done, g * 4 + 4 + AHEAD)
                act.wait_ge(eps_set, 1)
                nc.scalar.activation(ss[:], ss[:], ACT.Sqrt, bias=eps[:]).then_inc(rn_done, 1)
                for m in range(2 * NM):
                    act.wait_ge(scaled, g * 2 * NM + m + 2)
                    if m == 0:
                        act.wait_ge(s_done, g * GP + 1)
                    nc.scalar.activation(qkh[:, m, :], qk[:, m, :], ACT.Copy).then_inc(qk_hi, 1)

                def values(j):
                    n = g * GP + j
                    act.wait_ge(v_done, n + 2)
                    act.wait_ge(o_done, n + 1)
                    for half in range(2):
                        ins = nc.scalar.activation(vh[:, j % 2, half * (INNER // 2):(half + 1) * (INNER // 2)], pv[half][0:PAIR, 0:INNER // 2], ACT.Copy, scale=1.0 / WS)
                    ins.then_inc(v_hi, 1)

                def probabilities(j):
                    n = g * GP + j
                    act.wait_ge(centred, n + 1)
                    nc.scalar.activation(sm[j % 2][:], sm[j % 2][:], ACT.Exp).then_inc(exp_done, 1)

                def transposed(j):
                    n = g * GP + j
                    act.wait_ge(t_done, n + 1 + AHEAD)
                    act.wait_ge(o_done, n + AHEAD)
                    for par in range(2):
                        ins = nc.scalar.activation(ph[:, par, :], pt[par][0:PAIR, 0:W6], ACT.Copy)
                    ins.then_inc(t_hi, 1)
                    act.wait_ge(o_done, n + 1 + AHEAD)
                    nc.scalar.activation(oh[:, :, :, bass.ds(g * PG + 4 * j, 4)], po[0][:, 0:W6].rearrange("p (m t q) -> p m t q", m=NM, q=4), ACT.Copy).then_inc(o_hi, 1)

                values(0)
                probabilities(0)
                for j in range(GP):
                    if j + 1 < GP:
                        values(j + 1)
                        probabilities(j + 1)
                    transposed(j)

        @block.vector
        def _(dve):
            nc.vector.memset(eps[:], 1e-8).then_inc(eps_set, 1)
            with dve.Fori(0, NPG) as g:
                dve.wait_ge(v_done, g * GP + 1)
                for a, b in ((xgh, xh), (xgl, xl)):
                    for c in range(2):
                        ins = nc.vector.tensor_copy(a[:, c, :].rearrange("f (j t q) -> f j t q", t=NT, q=4),
                                                    b[:, c, :, bass.ds(g * PG, PG)].rearrange("f t (j q) -> f j t q", q=4))
                ins.then_inc(grouped, 1)
                dve.wait_ge(rn_done, g + 1)
                nc.vector.reciprocal(ss[:], ss[:]).then_inc(rn_ready, 1)
                dve.wait_ge(rn_ready, g + 1)
                for m in range(2 * NM):
                    w = qk[:, m, :].rearrange("p (a n) -> p a n", a=2)
                    if m < NM:
                        ins = nc.vector.scalar_tensor_tensor(w, w, isc[:, m:m + 1], ss[:, 0], ALU.mult, ALU.mult)
                    else:
                        ins = nc.vector.tensor_tensor(w, w, ss[:, 1], ALU.mult)
                    ins.then_inc(scaled, 1)

                def scores(j):
                    n = g * GP + j
                    s = sm[j % 2]
                    dve.wait_ge(v_hi, n + 1)
                    for half in range(2):
                        c = slice(half * (INNER // 2), (half + 1) * (INNER // 2))
                        ins = nc.vector.scalar_tensor_tensor(vl[:, j % 2, c], pv[half][0:PAIR, 0:INNER // 2], 1.0 / WS, vh[:, j % 2, c], ALU.mult, ALU.subtract)
                    ins.then_inc(v_lo, 1)
                    dve.wait_ge(s_done, n + 2)
                    dve.wait_ge(t_done, n + 1)
                    mk = mask[:].rearrange("p (a n) -> p a n", a=1).to_broadcast([PAIR, NH, PAIR])
                    for par in range(2):
                        ins = nc.vector.tensor_tensor(s[:, par, :].rearrange("p (m n) -> p m n", m=NH), pss[par][0:PAIR, 0:W6].rearrange("p (m n) -> p m n", m=NH), mk, ALU.add)
                    ins.then_inc(s_out, 1)
                    dve.wait_ge(s_out, n + 2)
                    nc.vector.tensor_reduce(mx[j % 2][:], s[:].rearrange("p a (m n) -> p (a m) n", n=PAIR), AX, ALU.max).then_inc(mx_done, 1)
                    dve.wait_ge(mx_done, n + 1)
                    s3 = s[:].rearrange("p a (m n) -> p (a m) n", n=PAIR)
                    nc.vector.tensor_tensor(s3, s3, mx[j % 2][:].rearrange("p (n a) -> p n a", a=1).to_broadcast([PAIR, H1, PAIR]), ALU.subtract).then_inc(centred, 1)

                def sums(j):
                    n = g * GP + j
                    dve.wait_ge(exp_done, n + 1)
                    nc.vector.tensor_reduce(rs[j % 2][:], sm[j % 2][:].rearrange("p a (m n) -> p (a m) n", n=PAIR), AX, ALU.add).then_inc(rs_done, 1)
                    dve.wait_ge(rs_done, n + 1)
                    nc.vector.reciprocal(rs[j % 2][:], rs[j % 2][:]).then_inc(rs_inv, 1)

                def transposed(j):
                    n = g * GP + j
                    dve.wait_ge(t_hi, n + 1)
                    for par in range(2):
                        ins = nc.vector.tensor_tensor(pl[:, par, :], pt[par][0:PAIR, 0:W6], ph[:, par, :], ALU.subtract)
                    ins.then_inc(t_lo, 1)
                    dve.wait_ge(o_hi, n + 1)
                    at = bass.ds(g * PG + 4 * j, 4)
                    nc.vector.tensor_tensor(ol[:, :, :, at], po[0][:, 0:W6].rearrange("p (m t q) -> p m t q", m=NM, q=4), oh[:, :, :, at], ALU.subtract).then_inc(o_lo, 1)

                scores(0)
                sums(0)
                for j in range(GP):
                    if j + 1 < GP:
                        scores(j + 1)
                        sums(j + 1)
                    transposed(j)

            def project(t, u, i):
                dve.wait_ge(p_done, NPG * NP + t + 1)
                nc.vector.scalar_tensor_tensor(h[:, t, :], pv[u][:, 0:D], 1.0 / WS, h[:, t, :], ALU.mult, ALU.add).then_inc(p_out, 1)

            pairs(dve, NT, project)

        @block.gpsimd
        def _(pool):
            pool.sem_inc(sq_used, AHEAD)
            pool.sem_inc(t_done, AHEAD)
            pool.sem_inc(o_done, AHEAD)
            for one in (v_lo, s_out, t_lo, o_lo, qk_lo, scaled, s_done, v_done):
                pool.sem_inc(one, 1)
            with pool.Fori(0, NPG) as g:
                for n in range(NP):
                    m, hf = n // 2, n % 2
                    to = ss[:, m // NM, hf, :]
                    pool.wait_ge(sq_done, g * NP + n + 1)
                    if m % NM == 0:
                        pool.sem_inc(sq_used, 1)
                        continue
                    nc.gpsimd.tensor_tensor(to, to, sq[n % 2][:], ALU.add).then_inc(sq_used, 1)
                    if m % NM == NM - 1:
                        pool.wait_ge(sq_used, g * NP + n + 1 + AHEAD)
                        pool.sem_inc(ss_done, 1)
                for m in range(2 * NM):
                    pool.wait_ge(qk_hi, g * 2 * NM + m + 1)
                    nc.gpsimd.tensor_tensor(qkl[:, m, :], qk[:, m, :], qkh[:, m, :], ALU.subtract).then_inc(qk_lo, 1)

                def scale(j):
                    pool.wait_ge(rs_inv, g * GP + j + 1)
                    s3 = sm[j % 2][:].rearrange("p a (m n) -> p (a m) n", n=PAIR)
                    nc.gpsimd.tensor_tensor(s3, s3, rs[j % 2][:].rearrange("p (n a) -> p n a", a=1).to_broadcast([PAIR, H1, PAIR]), ALU.mult).then_inc(prob_done, 1)

                for j in range(GP):
                    scale(j)


def constants(nc, ident, ident16, tri, ones16):
    with nc.semaphore("const_set") as const_set, nc.Block() as block:
        @block.gpsimd
        def _(pool):
            nc.gpsimd.memset(ident[:], 0.0).then_inc(const_set, 1)
            nc.gpsimd.memset(ident16[:], 0.0).then_inc(const_set, 1)
            nc.gpsimd.memset(ones16[:], 1.0).then_inc(const_set, 1)
            pool.wait_ge(const_set, 3)
            for m in (ident, ident16):
                nc.gpsimd.affine_select(out=m[:], in_=m[:], compare_op=ALU.not_equal, fill=1.0, base=0,
                                        pattern=[[-1, P]], channel_multiplier=1)
            nc.gpsimd.affine_select(out=tri[:], in_=ones16[:], compare_op=ALU.is_gt, fill=0.0, base=0,
                                    pattern=[[1, P]], channel_multiplier=-1)


def recycle_semaphores(nc):
    nc.clear_and_free_semaphores(SPENT)
    SPENT.clear()
    nc.all_engine_barrier()


def build(nc, dr, out, stage):
    SPENT.clear()
    with (nc.sbuf_tensor("h", [P, NT, D], F32) as h, nc.sbuf_tensor("ident", [P, P], F32) as ident,
          nc.sbuf_tensor("ident16", [P, P], F16) as ident16, ExitStack() as stack):
        tri = stack.enter_context(nc.sbuf_tensor("tri", [P, P], F16))
        ones16 = stack.enter_context(nc.sbuf_tensor("ones16", [P, P], F16))
        constants(nc, ident, ident16, tri, ones16)
        slots = nc.dram_tensor("slots", [NB * P, ROW], F32, kind="Internal").ap()
        sums = nc.dram_tensor("sums", [2 * T + RING * P, D], F32, kind="Internal").ap()
        xh = stack.enter_context(nc.sbuf_tensor("xh", [P, 2, NT, P], F16))
        xl = stack.enter_context(nc.sbuf_tensor("xl", [P, 2, NT, P], F16))
        patch_projection(nc, dr, h, ident)
        if stage >= 1:
            normalise(nc, None, h, xh, xl, ident16, "n0_")
            dynamic_convolution(nc, dr, h, xh, xl)
            normalise(nc, h, h, xh, xl, ident16, "n1_")
        if stage >= 2:
            experts(nc, dr, h, h, xh, xl, (ident, tri, ones16), slots, sums, "f0_", HID0, True, 1)
            normalise(nc, h, h, xh, xl, ident16, "n2_")
        if stage >= 3:
            recycle_semaphores(nc)
            attention(nc, dr, h, xh, xl, ident)
            h2 = stack.enter_context(nc.sbuf_tensor("h2", [P, NT, D], F32))
            normalise(nc, h, h, xh, xl, ident16, "n3_")
        if stage >= 4:
            recycle_semaphores(nc)
            normalise(nc, h, h2, xh, xl, ident16, "n4_", affine=(dr["f1_gamma"], dr["f1_beta"]))
            experts(nc, dr, h2, h, xh, xl, (ident, tri, ones16), slots, sums, "f1_", HID1, False, 0)
            normalise(nc, h, h, xh, xl, ident16, "n5_")
        with nc.semaphore("out_done") as out_done, nc.Block() as block:
            @block.sync
            def _(sp):
                sp.dma_start(out, h[:]).then_inc(out_done, 16)
                sp.wait_ge(out_done, 16)


def pixel_rows():
    pix = []
    for c in range(C):
        for y in range(-1, PATCH + 1):
            for x in range(-1, PATCH + 1):
                if not (0 <= y < PATCH or 0 <= x < PATCH):
                    continue
                fs = []
                for s, (dy, dx) in enumerate(((0, 0), (0, 1), (0, -1), (1, 0), (-1, 0))):
                    py, px = y + dy, x + dx
                    inside = 0 <= py < PATCH and 0 <= px < PATCH
                    fs.append((py * PATCH + px) * SHIFTS * C + s * C + c if inside else PD)
                pix.append((sum(f < PD for f in fs), c, y, x, fs))
    pix.sort(key=lambda p: -p[0])
    return [p[1:4] for p in pix], np.array([p[4] for p in pix]).T, np.array([p[0] for p in pix])


def lay_out(inp):
    f = {k: np.asarray(v) for k, v in inp.items()}
    pix, feats, count = pixel_rows()
    assert [tuple(c) for c in CLASSES if c[0] < 5] == [(n, int((count == n).sum())) for n in (4, 3, 1)]
    xp = np.pad(f["x"], ((0, 0), (0, 0), (1, 1), (1, 1)))
    cols = np.empty((B, GRID, GRID, KR), np.float32)
    for r, (c, y, x) in enumerate(pix):
        cols[..., r] = xp[:, c, y + 1:y + 2 + IMG - PATCH:PATCH, x + 1:x + 2 + IMG - PATCH:PATCH]
    d = {"x": cols.reshape(P, NT, KR).transpose(1, 0, 2)}
    none = lambda a: np.concatenate([a, np.zeros(a.shape[:-1] + (1,), a.dtype)], -1)
    wt = none(f["L0_tok_proj_weight"])[:, feats]
    d["tok_w"] = wt.reshape(D, SHIFTS, NK, KC).transpose(3, 1, 2, 0)
    by_row = lambda a: none(a)[feats].reshape(SHIFTS * NK, KC).T
    d["tok_lnw"] = by_row(f["L0_tok_ln_weight"])
    d["tok_lnb"] = by_row(f["L0_tok_ln_bias"])
    d["tok_negmult"] = (-count / PD).astype(np.float32).reshape(NK, KC).T
    d["tok_class"] = np.array([[n, 1, n] * 2 for n, _ in CLASSES], np.float32).ravel()
    d["tok_b"] = f["L0_tok_proj_bias"]
    dw = f["L0_attn_dw_w"][:, 0]
    twice = lambda a: np.concatenate([a[P:], a[P:]])
    d["dc_dw"] = np.stack([dw[:P], twice(dw)], 1)
    d["dc_pwb"] = np.stack([f["L0_attn_pw_b"][:P], twice(f["L0_attn_pw_b"])], 1)
    d["dc_akb"], d["dc_ptb"] = f["L0_attn_ak_b"], f["L0_attn_pt_b"]
    pw, ak, pt = f["L0_attn_pw_w"], f["L0_attn_ak_w"], f["L0_attn_pt_w"].T
    w = np.zeros((P, 2 * P + 2 * HA * K + 2 * D), np.float32)
    heads_b = list(range(HA, H)) * 2
    for n in range(HA):
        r = slice(n * IPG, (n + 1) * IPG)
        for g, head in ((0, n), (1, heads_b[n])):
            w[r, g * P + n * IPG:g * P + (n + 1) * IPG] = pw[head].T
            w[r, 2 * P + (g * HA + n) * K:2 * P + (g * HA + n + 1) * K] = ak[head].T
    w[:, 2 * P + 2 * HA * K:2 * P + 2 * HA * K + D] = pt[:P]
    w[:, 2 * P + 2 * HA * K + D:] = np.concatenate([pt[P:], pt[P:]])
    d["dc_w"] = w
    wq = f["L1_attn_w_qkv"].T
    d["at_wqkv"] = np.stack([wq[:P], twice(wq)], 1)
    d["at_wout"] = f["L1_attn_w_out"].T.reshape(NM, P, D).transpose(1, 0, 2).reshape(P, NM * D)
    d["at_bout"] = f["L1_attn_b_out"]
    d["at_scale"] = np.repeat(f["L1_attn_scale"].reshape(NM, 2).T, DH, 0)
    d["at_fold"] = np.tile(np.eye(DH, dtype=np.float32), (2, 2))
    image = np.arange(PAIR) % 4 // 2
    d["at_mask"] = np.where(image[:, None] == image, 0, NEG).astype(np.float32)
    d["f1_gamma"], d["f1_beta"] = f["L1_ffn_ln_gamma"], f["L1_ffn_ln_beta"]
    d["consts"] = np.concatenate([np.arange(E, 0, -1), P * np.arange(NT), np.arange(NB)]).astype(np.float32)

    def router(r):
        return np.stack([r[:P], twice(r)], 1)

    def pack(first, second):
        return np.concatenate([first[:P], twice(first), second.reshape(-1, P, D).transpose(1, 0, 2).reshape(P, -1)], 1)

    d["f0_router"] = router(f["L0_ffn_gate_w"].T)
    d["f0_w"] = np.stack([pack(np.concatenate([a.T, c.T], 1), b.T) for a, b, c in
                          [(f["L0_ffn_w1"][e], f["L0_ffn_w2"][e], f["L0_ffn_w3"][e]) for e in range(E)]
                          + [(f["L0_ffn_ws1"], f["L0_ffn_ws2"], f["L0_ffn_ws3"])]])
    d["f1_router"] = router(f["L1_ffn_router_w"])
    d["f1_w"] = np.stack([pack(f["L1_ffn_w1"][e], f["L1_ffn_w2"][e]) for e in range(E)])
    return {k: np.ascontiguousarray(v) for k, v in d.items()}


STAGE = 9


def kernel(**inputs):
    import concourse.bacc as bacc
    from concourse.bass_utils import run_bass_kernel_spmd as run

    d = lay_out(inputs)
    nc = bacc.Bacc("TRN2", target_bir_lowering=False, num_devices=1)
    dr = {k: nc.dram_tensor("in_" + k, v.shape, mybir.dt.from_np(v.dtype), kind="ExternalInput").ap() for k, v in d.items()}
    out = nc.dram_tensor("out_h", [P, NT, D], F32, kind="ExternalOutput").ap()
    build(nc, dr, out, STAGE)
    r = run(nc, [{"in_" + k: v for k, v in d.items()}], core_ids=[0])
    return np.asarray(r.results[0]["out_h"]).reshape(B, L, D)
```

```python
import numpy as np
from contextlib import ExitStack

import concourse.bass as bass
from concourse import mybir

F32 = mybir.dt.float32
F16 = mybir.dt.float16
BF16 = mybir.dt.bfloat16
I32 = mybir.dt.int32
ALU = mybir.AluOpType
ACT = mybir.ActivationFunctionType
AX = mybir.AxisListType.X

P = 128
B, C, IMG, PATCH = 64, 3, 96, 16
GRID = IMG // PATCH
L = GRID * GRID
T = B * L
NT = T // P
D = 192
DB = D - P
WS = 256.0
SHIFTS = 5
PD = PATCH * PATCH * SHIFTS * C
CLASSES = ((5, 294), (5, 294), (4, 168), (3, 12), (1, 192))
KR = sum(n for _, n in CLASSES)
KC, NK = 120, KR // 120
EPS = 1e-5
H, K, IPG = 12, 9, 16
PAD = (K - 1) // 2
NTP = NT + 2 * PAD
HT = NT // 2
HTP = HT + 2 * PAD
HA = P // IPG
E = 8
HID0, HID1 = 512, 768
H1, DH = 12, 64
INNER = H1 * DH
NM = INNER // P
PAIR = 2 * L
PAIRS = B // 2
GP = 4
NEG = -1e30
NB = 2 * T // P + E - 1
RING = 6
ROW = D + 2
AHEAD = 2


class Chain:

    def __init__(self, eng, sem):
        self.eng, self.sem, self.n = eng, sem, 0

    def link(self, ins):
        self.n += 1
        ins.then_inc(self.sem, 1)
        self.eng.wait_ge(self.sem, self.n)


def rows(ap, n):
    return ap.rearrange("(a n) -> a n", a=1).to_broadcast([n, ap.shape[0]])


def five(nc, out, xh, xl, ah, al, b, start=True):
    nc.tensor.matmul(out, xh[:, 0], ah, start=start, stop=False)
    nc.tensor.matmul(out, xl[:, 0], ah, start=False, stop=False)
    nc.tensor.matmul(out, xh[:, 0], al, start=False, stop=False)
    nc.tensor.matmul(out, xh[:, 1], b, start=False, stop=False)
    return nc.tensor.matmul(out, xl[0:DB, 1], b[0:DB], start=False, stop=True)


def five_t(nc, out, ah, al, b, xh, xl):
    nc.tensor.matmul(out, ah, xh[:, 0], start=True, stop=False)
    nc.tensor.matmul(out, ah, xl[:, 0], start=False, stop=False)
    nc.tensor.matmul(out, al, xh[:, 0], start=False, stop=False)
    nc.tensor.matmul(out, b, xh[:, 1], start=False, stop=False)
    return nc.tensor.matmul(out, b[0:DB], xl[0:DB, 1], start=False, stop=True)


def skewed(eng, n, ahead, behind):
    ahead(0, 0, 0)
    with eng.Fori(0, (n - 2) // 2) as i:
        for u in range(2):
            ahead(2 * i + u + 1, 1 - u, i + u)
            behind(2 * i + u, u, i)
    ahead(n - 1, 1, n // 2 - 1)
    behind(n - 2, 0, n // 2 - 1)
    behind(n - 1, 1, n // 2 - 1)


def pairs(eng, n, step):
    with eng.Fori(0, n // 2) as i:
        for u in range(2):
            step(2 * i + u, u, i)


SPENT = []


def pipelined(eng, n, r, *stages):
    lead = max(a for a, _ in stages)

    def peeled(i):
        for a, f in stages:
            if 0 <= i + a < n:
                f(i + a, (i + a) % r, (i + a) // r)

    for i in range(-lead, 0):
        peeled(i)
    with eng.Fori(0, (n - lead) // r) as q:
        for u in range(r):
            for a, f in stages:
                f(r * q + u + a, (u + a) % r, q + (u + a) // r)
    for i in range((n - lead) // r * r, n):
        peeled(i)


def scope(nc, ctx, tag):
    sb = lambda n, s, d=F32: ctx.enter_context(nc.sbuf_tensor(tag + n, s, d))
    ps = lambda n, s, d=F32: ctx.enter_context(nc.psum_tensor(tag + n, s, d))

    def sem(n):
        SPENT.append(nc.alloc_semaphore(tag + n))
        return SPENT[-1]

    return sb, ps, sem


def patch_projection(nc, dr, h, ident):
    ctx = ExitStack()
    with ctx:
        sb, pst, sem = scope(nc, ctx, "pp_")
        x = [sb(f"x{u}", [P, KR]) for u in range(2)]
        xh, xl = sb("xh", [KC, 2, NK, P], F16), sb("xl", [KC, 2, NK, P], F16)
        wl = sb("wl", [KC, SHIFTS, NK, D])
        lnw, lnb = sb("lnw", [KC, SHIFTS * NK]), sb("lnb", [KC, SHIFTS * NK])
        negmult = sb("negmult", [KC, NK])
        wsum = sb("wsum", [KC, NK, D])
        wh, wlo = sb("wh", [KC, NK, D], F16), sb("wlo", [KC, NK, D], F16)
        scaled = [sb(f"scaled{u}", [KC, NK, D]) for u in range(2)]
        pbias = sb("pbias", [1, D])
        ones = sb("ones", [KC, P])
        colsum, bias = sb("colsum", [P, D]), sb("bias", [P, D])
        cw = sb("cw", [P, len(CLASSES) * 6])
        st = sb("st", [P, NT, len(CLASSES) * 6])
        mv = sb("mv", [P, NT, 2])
        rstd = sb("rstd", [P, NT])
        xt = [pst(f"xt{u}", [KC, NK * P]) for u in range(2)]
        acc = [pst(f"acc{u}", [P, 512]) for u in range(2)]
        ps, ps2 = pst("ps", [P, 512]), pst("ps2", [P, 512])
        w_in, small_in = [sem(f"w_in{s}") for s in range(SHIFTS)], sem("small_in")
        x_in = [sem(f"x_in{u}") for u in range(2)]
        link = sem("link")
        bias_done = sem("bias_done")
        pool_link, ones_set, wsum_done, sums_done, centred, w_hi, w_ready = (
            sem(n) for n in ("pool_link", "ones_set", "wsum_done", "sums_done", "centred", "w_hi", "w_ready"))
        x_transposed, x_counted, hi_done, lo_done, mm_done, acc_free = (
            sem(n) for n in ("x_transposed", "x_counted", "hi_done", "lo_done", "mm_done", "acc_free"))
        var_done, std_done = sem("var_done"), sem("std_done")
        NV = 5 * NK // 8
        lnw_of = lambda s: lnw[:, s * NK:(s + 1) * NK].rearrange("p (k a) -> p k a", a=1).to_broadcast([KC, NK, D])
        block = ctx.enter_context(nc.Block())

        @block.sync
        def _(sp):
            for s in range(SHIFTS):
                sp.dma_start(wl[:, s], dr["tok_w"][:, s]).then_inc(w_in[s], 16)
            for u in range(2):
                sp.dma_start(x[u][:], dr["x"][u]).then_inc(x_in[u], 16)

            def load(t, u, i):
                sp.wait_ge(x_transposed, t + 1)
                sp.wait_ge(x_counted, t + 1)
                sp.dma_start(x[u][:], dr["x"][t + 2]).then_inc(x_in[u], 16)

            pairs(sp, NT - 2, load)

        @block.gpsimd
        def _(pool):
            ch = Chain(pool, pool_link)
            nc.gpsimd.memset(ones[:], 1.0).then_inc(ones_set, 1)
            pool.wait_ge(small_in, 80)
            for s in range(SHIFTS):
                pool.wait_ge(w_in[s], 16)
                to = scaled[s % 2] if s else wsum
                ch.link(nc.gpsimd.tensor_tensor(to[:, NV:], wl[:, s, NV:], lnw_of(s)[:, NV:], ALU.mult))
                if s:
                    ch.link(nc.gpsimd.tensor_tensor(wsum[:, NV:], wsum[:, NV:], to[:, NV:], ALU.add))
            pool.sem_inc(wsum_done, 1)

        @block.scalar
        def _(act):
            act.sem_inc(acc_free, AHEAD)
            for dst, name in ((lnw, "tok_lnw"), (lnb, "tok_lnb"), (negmult, "tok_negmult")):
                act.dma_start(dst[:], dr[name]).then_inc(small_in, 16)
            act.dma_start(pbias[:], dr["tok_b"].rearrange("(a n) -> a n", a=1)).then_inc(small_in, 16)
            act.dma_start(cw[:], rows(dr["tok_class"], P)).then_inc(small_in, 16)
            act.wait_ge(centred, 1)
            nc.scalar.activation(wh[:], wsum[:], ACT.Copy, scale=WS).then_inc(w_hi, 1)
            def split_hi(t, u, i):
                act.wait_ge(x_transposed, t + 1)
                act.wait_ge(mm_done, t + 1)
                nc.scalar.activation(xh[:, u], xt[u][:].rearrange("p (k q) -> p k q", k=NK), ACT.Copy).then_inc(hi_done, 1)

            def evacuate(t, u, i):
                act.wait_ge(mm_done, t + 1 + AHEAD)
                nc.scalar.activation(h[:, t, 0:D], acc[u][:, 0:D], ACT.Copy, scale=1.0 / WS).then_inc(acc_free, 1)

            skewed(act, NT, split_hi, evacuate)
            act.wait_ge(var_done, 1)
            nc.scalar.activation(rstd[:], rstd[:], ACT.Sqrt).then_inc(std_done, 1)

        @block.vector
        def _(dve):
            ch = Chain(dve, link)
            dve.sem_inc(lo_done, AHEAD)
            dve.wait_ge(small_in, 80)
            for s in range(SHIFTS):
                dve.wait_ge(w_in[s], 16)
                to = scaled[s % 2] if s else wsum
                ch.link(nc.vector.tensor_tensor(to[:, 0:NV], wl[:, s, 0:NV], lnw_of(s)[:, 0:NV], ALU.mult))
                if s:
                    ch.link(nc.vector.tensor_tensor(wsum[:, 0:NV], wsum[:, 0:NV], to[:, 0:NV], ALU.add))
            nc.vector.engine_nop().then_inc(wsum_done, 1)
            dve.wait_ge(sums_done, 1)
            ch.link(nc.vector.tensor_copy(colsum[:], ps[:, 0:D]))
            for k in range(NK):
                ins = nc.vector.scalar_tensor_tensor(wsum[:, k, :], colsum[0:KC, :], negmult[:, k:k + 1],
                                                     wsum[:, k, :], ALU.mult, ALU.add)
            ins.then_inc(centred, 1)
            dve.wait_ge(w_hi, 1)
            nc.vector.scalar_tensor_tensor(wlo[:], wsum[:], WS, wh[:], ALU.mult, ALU.subtract).then_inc(w_ready, 1)

            def count(t, u, i):
                dve.wait_ge(x_in[u], 16 * (i + 1))
                at = 0
                for c, (_, n) in enumerate(CLASSES):
                    ins = nc.vector.bn_stats(st[:, t, 6 * c:6 * c + 6], x[u][:, at:at + n])
                    at += n
                ins.then_inc(x_counted, 1)
                dve.wait_ge(hi_done, t + 1)
                dve.wait_ge(mm_done, t + 1)
                nc.vector.tensor_tensor(xl[:, u], xt[u][:].rearrange("p (k q) -> p k q", k=NK), xh[:, u],
                                        ALU.subtract).then_inc(lo_done, 1)

            pairs(dve, NT, count)
            dve.wait_ge(bias_done, 1)
            nc.vector.tensor_copy(bias[:], ps2[:, 0:D])
            dve.wait_ge(lo_done, NT + AHEAD)
            ch.link(nc.vector.tensor_tensor(st[:], st[:], cw[:].rearrange("p (a n) -> p a n", a=1).to_broadcast([P, NT, len(CLASSES) * 6]), ALU.mult))
            for t in range(NT):
                ins = nc.vector.bn_aggr(mv[:, t, :], st[:, t, :])
            ch.link(ins)
            nc.vector.tensor_scalar(rstd[:], mv[:, :, 1], EPS, None, ALU.add).then_inc(var_done, 1)
            dve.wait_ge(std_done, 1)
            dve.wait_ge(acc_free, NT + AHEAD)
            ch.link(nc.vector.reciprocal(rstd[:], rstd[:]))
            for t in range(NT):
                nc.vector.scalar_tensor_tensor(h[:, t, 0:D], h[:, t, 0:D], rstd[:, t:t + 1], bias[:], ALU.mult, ALU.add)

        @block.tensor
        def _(pe):
            pe.sem_inc(mm_done, AHEAD)
            pe.wait_ge(ones_set, 1)
            pe.wait_ge(small_in, 80)
            def biases(s):
                pe.wait_ge(w_in[s], 16)
                for k in range(NK):
                    j = s * NK + k
                    nc.tensor.matmul(ps2[:, 0:D], lnb[:, j:j + 1].to_broadcast([KC, P]), wl[:, s, k, :], start=(j == 0), stop=False)

            for s in range(SHIFTS - 2):
                biases(s)
            pe.wait_ge(wsum_done, 2)
            for k in range(NK):
                ins = nc.tensor.matmul(ps[:, 0:D], ones[:], wsum[:, k, :], start=(k == 0), stop=(k == NK - 1))
            ins.then_inc(sums_done, 1)
            for s in range(SHIFTS - 2, SHIFTS):
                biases(s)
            nc.tensor.matmul(ps2[:, 0:D], ones[0:1, :], pbias[:], start=False, stop=True).then_inc(bias_done, 1)
            pe.wait_ge(w_ready, 1)

            def transpose(t, u, i):
                pe.wait_ge(x_in[u], 16 * (i + 1))
                pe.wait_ge(lo_done, t + 1)
                for k in range(NK):
                    ins = nc.tensor.transpose(xt[u][:, k * P:(k + 1) * P], x[u][:, k * KC:(k + 1) * KC], ident[:])
                ins.then_inc(x_transposed, 1)

            def project(t, u, i):
                pe.wait_ge(lo_done, t + 1 + AHEAD)
                pe.wait_ge(acc_free, t + 1)
                for a, b in ((xh, wh), (xl, wh), (xh, wlo)):
                    for k in range(NK):
                        ins = nc.tensor.matmul(acc[u][:, 0:D], a[:, u, k, :], b[:, k, :],
                                               start=(a is xh and b is wh and k == 0), stop=(b is wlo and k == NK - 1))
                ins.then_inc(mm_done, 1)

            skewed(pe, NT, transpose, project)


def normalise(nc, z, h, tag, split=None, affine=None, out=None, room=None, beside=None):
    beside = beside or {}
    ctx = ExitStack()
    with ctx:
        sb, pst, sem = scope(nc, ctx, tag)
        parts, n = range(3), NT // 3
        part = lambda c: slice(c * n, (c + 1) * n)
        st, mv, rstd, shift = sb("st", [P, NT, 6]), sb("mv", [P, NT, 2]), sb("rstd", [P, NT]), sb("shift", [P, NT])
        gb = sb("gb", [P, 2, D])
        BY_ACT = 2
        stats_done, var_done, std_done, inv_done, shift_done, last_done, link, h_done, gb_in, out_done = (sem(n) for n in (
            "stats_done", "var_done", "std_done", "inv_done", "shift_done", "last_done", "link", "h_done", "gb_in", "out_done"))
        if split is not None:
            xh, xl, ident16 = split
            if room is None:
                room = sb("room", [P, 2 * NT * 2 * P], F16)[:]
            sh, sl = (room[:, i * NT * 2 * P:(i + 1) * NT * 2 * P].rearrange("p (t f) -> p t f", t=NT) for i in range(2))
            th, tl = ([pst(f"{s}{u}", [P, 4, 2, P], F16) for u in range(n // 2)] for s in ("th", "tl"))
            hi_done, lo_done, lo_done_1, t_done, xh_used, xl_used = (
                sem(n) for n in ("hi_done", "lo_done", "lo_done_1", "t_done", "xh_used", "xl_used"))
            halves = ((slice(0, P), slice(0, P)), (slice(P, P + DB), slice(P, D)), (slice(P + DB, 2 * P), slice(P, D)))
        block = ctx.enter_context(nc.Block())

        @block.sync
        def _(sp):
            if "sync" in beside:
                beside["sync"](sp)
            if affine is not None:
                for j in range(2):
                    sp.dma_start(gb[:, j, :], rows(affine[j], P)).then_inc(gb_in, 16)
            if out is not None:
                for c in parts:
                    sp.wait_ge(h_done, c + 1)
                    sp.wait_ge(last_done, c + 1)
                    sp.dma_start(out[:, part(c), :], h[:, part(c), :]).then_inc(out_done, 16)
                sp.wait_ge(out_done, 16 * len(parts))

        @block.vector
        def _(dve):
            ch = Chain(dve, link)

            def split_lo(c):
                if split is not None and c >= 0:
                    dve.wait_ge(hi_done, c + 1)
                    a, b = halves[0]
                    nc.vector.tensor_tensor(sl[:, part(c), a], h[:, part(c), b], sh[:, part(c), a], ALU.subtract).then_inc(lo_done_1, 1)

            if z is not None:
                for c in parts:
                    for t in range(NT)[part(c)]:
                        ins = nc.vector.bn_stats(st[:, t, :], z[:, t, :])
                    ins.then_inc(stats_done, 1)
                    dve.wait_ge(stats_done, c + 1)
                    for t in range(NT)[part(c)]:
                        ins = nc.vector.bn_aggr(mv[:, t, :], st[:, t, :])
                    ch.link(ins)
                    nc.vector.tensor_scalar(rstd[:, part(c)], mv[:, part(c), 1], EPS, None, ALU.add).then_inc(var_done, 1)
                for c in parts:
                    dve.wait_ge(std_done, c + 1)
                    nc.vector.reciprocal(rstd[:, part(c)], rstd[:, part(c)]).then_inc(inv_done, 1)
                    dve.wait_ge(inv_done, c + 1)
                    nc.vector.scalar_tensor_tensor(shift[:, part(c)], mv[:, part(c), 0], -1.0, rstd[:, part(c)], ALU.mult, ALU.mult).then_inc(shift_done, 1)
                    for t in range(NT)[part(c)][:-BY_ACT]:
                        ins = nc.vector.tensor_scalar(h[:, t, :], z[:, t, :], mv[:, t, 0:1], rstd[:, t:t + 1], ALU.subtract, ALU.mult)
                    if affine is not None:
                        ch.link(ins)
                        dve.wait_ge(last_done, c + 1)
                        dve.wait_ge(gb_in, 32)
                        for j, op in ((0, ALU.mult), (1, ALU.add)):
                            ins = nc.vector.tensor_tensor(h[:, part(c), :], h[:, part(c), :], gb[:, j:j + 1, :].to_broadcast([P, n, D]), op)
                            if j == 0:
                                ch.link(ins)
                    ins.then_inc(h_done, 1)
                    if c < 2:
                        split_lo(c - 1)
                split_lo(1)
                split_lo(2)
            else:
                for c in parts:
                    split_lo(c)
            if split is not None:
                for k in range(NT // 2):
                    dve.wait_ge(t_done, k + 1)
                    nc.vector.tensor_copy(xl[:, :, 2 * k:2 * k + 2, :], tl[k % (n // 2)][:, 0:2].rearrange("p t c q -> p c t q")).then_inc(xl_used, 1)
            if "vector" in beside:
                beside["vector"](dve)

        @block.scalar
        def _(act):
            if z is not None:
                for c in parts:
                    act.wait_ge(var_done, c + 1)
                    nc.scalar.activation(rstd[:, part(c)], rstd[:, part(c)], ACT.Sqrt).then_inc(std_done, 1)

            def last_tiles(c):
                if z is not None:
                    act.wait_ge(shift_done, c + 1)
                    for t in range(NT)[part(c)][-BY_ACT:]:
                        ins = nc.scalar.activation(h[:, t, :], z[:, t, :], ACT.Identity, scale=rstd[:, t:t + 1], bias=shift[:, t:t + 1])
                    ins.then_inc(last_done, 1)

            def split_hi(c):
                if z is not None:
                    act.wait_ge(h_done, c + 1)
                    act.wait_ge(last_done, c + 1)
                for a, b in halves:
                    ins = nc.scalar.activation(sh[:, part(c), a], h[:, part(c), b], ACT.Copy)
                ins.then_inc(hi_done, 1)

            def unload(c):
                for k in range(NT // 2)[c * n // 2:(c + 1) * n // 2]:
                    act.wait_ge(t_done, k + 1)
                    nc.scalar.activation(xh[:, :, 2 * k:2 * k + 2, :], th[k % (n // 2)][:, 0:2].rearrange("p t c q -> p c t q"), ACT.Copy).then_inc(xh_used, 1)

            if split is None:
                for c in parts:
                    last_tiles(c)
            else:
                last_tiles(0)
                last_tiles(1)
                split_hi(0)
                last_tiles(2)
                split_hi(1)
                unload(0)
                split_hi(2)
                unload(1)
                unload(2)
            if "scalar" in beside:
                beside["scalar"](act)

        @block.gpsimd
        def _(pool):
            if split is not None:
                for c in parts:
                    pool.wait_ge(hi_done, c + 1)
                    for a, b in halves[1:]:
                        ins = nc.gpsimd.tensor_tensor(sl[:, part(c), a], h[:, part(c), b], sh[:, part(c), a], ALU.subtract)
                    ins.then_inc(lo_done, 1)
            if "gpsimd" in beside:
                beside["gpsimd"](pool, lo_done, lo_done_1)

        @block.tensor
        def _(pe):
            if split is not None:
                for k in range(NT // 2):
                    pe.wait_ge(lo_done, 2 * k // n + 1)
                    pe.wait_ge(lo_done_1, 2 * k // n + 1)
                    if k >= n // 2:
                        pe.wait_ge(xh_used, k - n // 2 + 1)
                        pe.wait_ge(xl_used, k - n // 2 + 1)
                    for i in range(2):
                        for to, s in ((th, sh), (tl, sl)):
                            for m in range(2):
                                ins = nc.tensor.transpose(to[k % (n // 2)][:, i, m, :], s[:, 2 * k + i, m * P:(m + 1) * P], ident16[:])
                    ins.then_inc(t_done, 1)


def dynamic_convolution(nc, dr, h, xh, xl, ident, ones16, slots, fill):
    ctx = ExitStack()
    with ctx:
        sb, pst, sem = scope(nc, ctx, "dc_")
        xa, xb = sb("xa", [P, NTP, P]), sb("xb", [P, HTP, P])
        ca, cb = sb("ca", [P, NT, P]), sb("cb", [P, HT, P])
        csh, csl = sb("csh", [P, NT + HT, P], F16), sb("csl", [P, NT + HT, P], F16)
        wdw, wpb = sb("wdw", [P, 2, K]), sb("wpb", [P, 2])
        wst = sb("wst", [P, 2 * P + 2 * HA * K + 2 * D])
        wh, wl = (sb(n, [P, 2 * P + 2 * HA * K + 2 * D], F16) for n in ("wh", "wl"))
        akb, ptb, pth, ptl = sb("akb", [P, H * K]), sb("ptb", [1, D]), sb("pth", [1, D], F16), sb("ptl", [1, D], F16)
        kern = sb("kern", [P, NT, H * K])
        mx, rs = sb("mx", [P, NT * H]), sb("rs", [P, NT * H])
        v = sb("v", [P, NTP, D])
        prod = [sb(f"prod{u}", [P, NT, D]) for u in range(2)]
        banks = pst("banks", [P, 7, 512])
        pw, pk, pv = ([banks[:, b] for b in bs] for bs in ((0, 1), (2, 3, 4), (5, 6)))
        TS = 2 * NT // 3
        w_in, bias_in, w_hi, w_ready, link, plink = (sem(n) for n in ("w_in", "bias_in", "w_hi", "w_ready", "link", "plink"))
        filled = sem("filled")
        edges, conv_a, conv_b, pw_done, ca_done, c_hi, c_lo, xb_done, prod_summed = (
            sem(n) for n in ("edges", "conv_a", "conv_b", "pw_done", "ca_done", "c_hi", "c_lo", "xb_done", "prod_summed"))
        k_done, k_out, v_done, v_out, centred, exp_done, halo, prod_done, prod_used = (
            sem(n) for n in ("k_done", "k_out", "v_done", "v_out", "centred", "exp_done", "halo", "prod_done", "prod_used"))
        O_AK, O_PT = 2 * P, 2 * P + 2 * HA * K
        NAK = HA * K
        CH = [(0, 3 * c) for c in range(NT // 3)] + [(1, 3 * c) for c in range(HT // 3)]
        block = ctx.enter_context(nc.Block())

        @block.sync
        def _(sp):
            sp.dma_start(wst[:], dr["dc_w"]).then_inc(w_in, 16)
            sp.dma_start(wdw[:], dr["dc_dw"]).then_inc(bias_in, 16)
            sp.dma_start(wpb[:], dr["dc_pwb"]).then_inc(bias_in, 16)
            sp.dma_start(akb[:], rows(dr["dc_akb"], P)).then_inc(bias_in, 16)
            sp.dma_start(ptb[:], rows(dr["dc_ptb"], 1)).then_inc(bias_in, 16)
            clear_slots(sp, slots, fill, filled)
            sp.wait_ge(v_out, NT + AHEAD)
            sp.wait_ge(edges, 1)
            with nc.allow_non_contiguous_dma(reason="rows of other partitions"):
                sp.dma_start(v[1:P:2, 0:PAD, :], v[0:P:2, NT:NT + PAD, :]).then_inc(halo, 16)
                sp.dma_start(v[0:P:2, NT + PAD:NTP, :], v[1:P:2, PAD:2 * PAD, :]).then_inc(halo, 16)
            sp.wait_ge(filled, 16 * RING)

        @block.gpsimd
        def _(pool):
            ch = Chain(pool, plink)
            nc.gpsimd.memset(xa[:, 0:PAD, :], 0.0)
            nc.gpsimd.memset(xa[:, NT + PAD:NTP, :], 0.0)
            nc.gpsimd.memset(v[:, 0:PAD, :], 0.0)
            nc.gpsimd.memset(v[:, NT + PAD:NTP, :], 0.0).then_inc(edges, 1)
            nc.gpsimd.memset(xb[:, 0:PAD, :], 0.0)
            ch.link(nc.gpsimd.memset(xb[:, HT + PAD:HTP, :], 0.0))
            ch.link(nc.gpsimd.tensor_tensor(xb[0:DB, PAD:HTP, :], xh[0:DB, 1, 0:HT + PAD], xl[0:DB, 1, 0:HT + PAD], ALU.add))
            ch.link(nc.gpsimd.tensor_tensor(xb[DB:P, 0:HT + PAD, :], xh[DB:P, 1, HT - PAD:NT], xl[DB:P, 1, HT - PAD:NT], ALU.add))
            odd, even = slice(1, P, 2), slice(0, P, 2)
            ch.link(nc.gpsimd.tensor_tensor(xb[0:DB, 0:PAD, odd], xh[0:DB, 1, NT - PAD:NT, even], xl[0:DB, 1, NT - PAD:NT, even], ALU.add))
            ch.link(nc.gpsimd.tensor_tensor(xb[DB:P, HT + PAD:HTP, even], xh[DB:P, 1, 0:PAD, odd], xl[DB:P, 1, 0:PAD, odd], ALU.add))
            nc.gpsimd.sem_inc(xb_done, 1)
            for n, (g, t0) in enumerate(CH):
                pool.wait_ge(c_hi, n + 1)
                c = (ca, cb)[g]
                o = NT * g + t0
                nc.gpsimd.tensor_tensor(csl[:, o:o + 3, :], c[:, t0:t0 + 3, :], csh[:, o:o + 3, :], ALU.subtract).then_inc(c_lo, 1)
            for k in range(K):
                pool.wait_ge(prod_done, k + 1)
                if k:
                    pool.wait_ge(prod_used, k)
                nc.gpsimd.tensor_tensor(h[:, TS:], h[:, TS:], prod[k % 2][:, TS:], ALU.add).then_inc(prod_used, 1)

        @block.scalar
        def _(act):
            act.sem_inc(v_out, AHEAD)
            act.wait_ge(w_in, 16)
            nc.scalar.activation(wh[:], wst[:], ACT.Copy, scale=WS).then_inc(w_hi, 1)

            def values(t, u, i):
                act.wait_ge(v_done, t + 1)
                nc.scalar.activation(v[:, PAD + t, :], pv[u][:, 0:D], ACT.Copy, scale=1.0 / WS).then_inc(v_out, 1)

            for t in range(NT):
                values(t, t % 2, t // 2)
            for n, (g, t0) in enumerate(CH):
                act.wait_ge(ca_done, n + 1)
                c = (ca, cb)[g]
                o = NT * g + t0
                nc.scalar.activation(csh[:, o:o + 3, :], c[:, t0:t0 + 3, :], ACT.Copy).then_inc(c_hi, 1)
            act.wait_ge(centred, 1)
            nc.scalar.activation(kern[:], kern[:], ACT.Exp).then_inc(exp_done, 1)

        @block.vector
        def _(dve):
            ch = Chain(dve, link)
            dve.sem_inc(k_out, 3)
            dve.wait_ge(bias_in, 64)
            dve.wait_ge(w_hi, 1)
            ch.link(nc.vector.scalar_tensor_tensor(wl[:], wst[:], WS, wh[:], ALU.mult, ALU.subtract))
            ch.link(nc.vector.tensor_scalar(pth[:], ptb[:], WS, None, ALU.mult))
            nc.vector.scalar_tensor_tensor(ptl[:], ptb[:], WS, pth[:], ALU.mult, ALU.subtract)
            nc.vector.tensor_copy(wh[DB:P, O_PT + D:], wl[DB:P, O_PT + D:]).then_inc(w_ready, 1)

            dve.wait_ge(edges, 1)
            odd, even = slice(1, P, 2), slice(0, P, 2)
            ch.link(nc.vector.tensor_tensor(xa[:, PAD:PAD + NT, :], xh[:, 0], xl[:, 0], ALU.add))
            ch.link(nc.vector.tensor_copy(xa[:, 0:PAD, odd], xa[:, NT:NT + PAD, even]))
            ch.link(nc.vector.tensor_copy(xa[:, NT + PAD:NTP, even], xa[:, PAD:2 * PAD, odd]))
            for x, c, n, g, done in ((xa, ca, NT, 0, conv_a), (xb, cb, HT, 1, conv_b)):
                if g:
                    dve.wait_ge(xb_done, 1)
                ch.link(nc.vector.tensor_scalar(c[:], x[:, 0:n, :], wdw[:, g, 0:1], None, ALU.mult))
                for k in range(1, K):
                    ch.link(nc.vector.scalar_tensor_tensor(c[:], x[:, k:k + n, :], wdw[:, g, k:k + 1], c[:], ALU.mult, ALU.add))
                nc.vector.engine_nop().then_inc(done, 1)
            for n, (g, t0) in enumerate(CH):
                x, c = ((xa, ca), (xb, cb))[g]
                dve.wait_ge(pw_done, n + 1)
                nc.vector.scalar_tensor_tensor(c[:, t0:t0 + 3, :], pw[n % 2][:, 0:3 * P].rearrange("p (t q) -> p t q", t=3), wpb[:, g:g + 1],
                                               x[:, PAD + t0:PAD + t0 + 3, :], ALU.add, ALU.mult).then_inc(ca_done, 1)
            with dve.Fori(0, HT // 3) as i:
                for j in range(3):
                    t = 3 * i + j
                    dve.wait_ge(k_done, t + 1)
                    nc.vector.scalar_tensor_tensor(kern[:].rearrange("p (a t) k -> p a t k", a=2)[:, :, bass.ds(t, 1), :].rearrange("p a b k -> p a (b k)"),
                                                   pk[j][:, 0:2 * H * K].rearrange("p (a k) -> p a k", a=2), 1.0 / WS,
                                                   akb[:].rearrange("p (a k) -> p a k", a=1).to_broadcast([P, 2, H * K]), ALU.mult, ALU.add).then_inc(k_out, 1)
            dve.wait_ge(k_out, HT + 3)
            k3 = kern[:].rearrange("p t (h k) -> p (t h) k", k=K)
            wide = lambda a: a[:].rearrange("p (n a) -> p n a", a=1).to_broadcast([P, NT * H, K])
            ch.link(nc.vector.tensor_reduce(mx[:], k3, AX, ALU.max))
            nc.vector.tensor_tensor(k3, k3, wide(mx), ALU.subtract).then_inc(centred, 1)
            dve.wait_ge(exp_done, 1)
            ch.link(nc.vector.tensor_reduce(rs[:], k3, AX, ALU.add))
            ch.link(nc.vector.reciprocal(rs[:], rs[:]))
            ch.link(nc.vector.tensor_tensor(k3, k3, wide(rs), ALU.mult))
            dve.wait_ge(halo, 32)
            for k in range(K):
                if k >= 2:
                    dve.wait_ge(prod_used, k - 1)
                    dve.wait_ge(prod_summed, k - 1)
                nc.vector.tensor_tensor(prod[k % 2][:].rearrange("p t (h d) -> p (t h) d", d=IPG),
                                        v[:, k:k + NT, :].rearrange("p t (h d) -> p (t h) d", d=IPG),
                                        k3[:, :, k:k + 1].to_broadcast([P, NT * H, IPG]), ALU.mult).then_inc(prod_done, 1)
            dve.wait_ge(prod_summed, K)
            two = h[:, 0:TS].rearrange("p (b t) d -> p b (t d)", t=2)
            nc.vector.tensor_tensor(two, two, banks[:, 0:TS // 2, 0:2 * D], ALU.add)

        @block.tensor
        def _(pe):
            pe.wait_ge(w_ready, 1)

            def values(t, u, i):
                pe.wait_ge(v_out, t + 1)
                nc.tensor.matmul(pv[u][:, 0:D], ones16[0:1, :], pth[:], start=True, stop=False)
                nc.tensor.matmul(pv[u][:, 0:D], ones16[0:1, :], ptl[:], start=False, stop=False)
                five(nc, pv[u][:, 0:D], xh[:, :, t, :], xl[:, :, t, :], wh[:, O_PT:O_PT + D], wl[:, O_PT:O_PT + D],
                     wh[:, O_PT + D:], start=False).then_inc(v_done, 1)

            pe.wait_ge(edges, 1)
            for t in range(NT):
                values(t, t % 2, t // 2)
            for n, (g, t0) in enumerate(CH):
                pe.wait_ge((conv_a, conv_b)[g], 1)
                if n >= 2:
                    pe.wait_ge(ca_done, n - 1)
                c = (ca, cb)[g]
                nc.tensor.matmul(pw[n % 2][:, 0:3 * P], wst[:, g * P:(g + 1) * P], c[:, t0:t0 + 3, :], start=True, stop=True).then_inc(pw_done, 1)
            pe.wait_ge(c_lo, len(CH))
            with pe.Fori(0, HT // 3) as i:
                for b in range(3):
                    t = 3 * i + b
                    pe.wait_ge(k_out, t + 1)
                    for j, (o, n) in enumerate(((t, 0), (t + HT, 0), (t + NT, 1))):
                        if n == 0:
                            to = pk[b][:, j * H * K:j * H * K + NAK]
                        else:
                            to = pk[b][:, 0:2 * H * K].rearrange("p (a k) -> p a k", a=2)[:, :, NAK:H * K]
                        w = slice(O_AK + n * NAK, O_AK + (n + 1) * NAK)
                        nc.tensor.matmul(to, csh[:, o, :], wh[:, w], start=True, stop=False)
                        nc.tensor.matmul(to, csl[:, o, :], wh[:, w], start=False, stop=False)
                        ins = nc.tensor.matmul(to, csh[:, o, :], wl[:, w], start=False, stop=True)
                    ins.then_inc(k_done, 1)
            for k in range(K):
                pe.wait_ge(prod_done, k + 1)
                for b in range(TS // 2):
                    ins = nc.tensor.matmul(banks[:, b, 0:2 * D], ident[:], prod[k % 2][:, 2 * b:2 * b + 2, :], start=(k == 0), stop=(k == K - 1))
                ins.then_inc(prod_summed, 1)


def clear_slots(sp, slots, fill, filled):
    for u in range(RING):
        sp.dma_start(slots.rearrange("(b p) c -> p b c", p=P)[:, u:NB:RING, :],
                     fill[:, u:u + 1, :].to_broadcast([P, len(range(u, NB, RING)), ROW])).then_inc(filled, 16)


def experts(nc, dr, x, h, xh, xl, idents, slots, sums, tag, hid, gated, shared, prepare):
    ident, tri, ones16 = idents
    ne = E + shared
    nm = hid // P
    nw = 2 * hid if gated else hid
    wcol = nw // 2
    n2 = nm * D
    O_B, O_AL, O_2H, O_2L, COLS = nw, 2 * nw, 3 * nw, 3 * nw + n2, 3 * nw + 2 * n2
    NS = NT * shared
    R = RING
    ctx = ExitStack()
    with ctx:
        sb, pst, sem = scope(nc, ctx, tag)
        w = sb("w", [P, ne, COLS], F16)
        wst = [sb(f"wst{u}", [P, 2 * nw + n2]) for u in range(2)]
        rst, rh, rl = sb("rst", [P, 2, E]), sb("rh", [P, 2, E], F16), sb("rl", [P, 2, E], F16)
        lg, pr, sel1, sel2, tmp = (sb(n, [P, NT, E]) for n in ("lg", "pr", "sel1", "sel2", "tmp"))
        both = sb("both", [P, E, NT], F16)
        rank, tot, incl, ones = (sb(n, [P, E, NT]) for n in ("rank", "tot", "incl", "ones"))
        consts = sb("consts", [P, E + NT + NB])
        cnt, nblk, iblk, start = (sb(n, [P, E]) for n in ("cnt", "nblk", "iblk", "start"))
        m, m1, m2, rd = (sb(n, [P, NT]) for n in ("m", "m1", "m2", "rd"))
        pos = sb("pos", [P, 2, NT], I32)
        ebt, ebf, eb = sb("ebt", [1, NB, E]), sb("ebf", [1, NB]), sb("eb", [1, NB], I32)
        xr = sb("xr", [P, 2, NT, ROW])
        z = xr[:].rearrange("p a t c -> p (a t c)")[:, 0:2 * NT * D].rearrange("p (t a c) -> p t a c", a=2, c=D)
        xb = [sb(f"xb{u}", [P, ROW + DB]) for u in range(R)]
        xsh, xsl = sb("xsh", [P, 2, 2, P], F16), sb("xsl", [P, 2, 2, P], F16)
        act_out = [sb(f"act{u}", [P, hid]) for u in range(2)] if gated else None
        g = [sb(f"g{u}", [P, hid]) for u in range(2)]
        gh, gl = sb("gh", [P, 2, nm, P], F16), sb("gl", [P, 2, nm, P], F16)
        ys = [sb(f"ys{u}", [P, D]) for u in range(R)]
        w_in = [sem(f"w_in{u}") for u in range(2)]
        (w_split, w_hi, r_in, r_hi, r_ready, l_done, l_out, link, centred, exp_done, both_done, rank_done, consts_in) = (
            sem(n) for n in ("w_split", "w_hi", "r_in", "r_hi", "r_ready", "l_done", "l_out", "link", "centred", "exp_done",
                             "both_done", "rank_done", "consts_in"))
        rows_copied, rows_marked, routed, table_done, scattered, y_seen = (
            sem(n) for n in ("rows_copied", "rows_marked", "routed", "table_done", "scattered", "y_seen"))
        sums_in = [sem(f"sums_in{c}") for c in range(3)]
        h_done, g_done, t_done, y_done = (sem(n) for n in ("h_done", "g_done", "t_done", "y_done"))
        xl_done, gl_done, y_out = (sem(n) for n in ("xl_done", "gl_done", "y_out"))
        xt_done, xh_done, silu_done, gh_done = (sem(n) for n in ("xt_done", "xh_done", "silu_done", "gh_done"))
        x_in, y_sent = ([sem(f"{n}{u}") for u in range(R)] for n in ("x_in", "y_sent"))

        def load_weights(sp, e):
            e_ = (e - shared) % ne
            sp.dma_start(wst[e % 2][:], dr[tag + "w"][e_]).then_inc(w_in[e % 2], 16)

        def first_loads(sp):
            sp.dma_start(rst[:], dr[tag + "router"]).then_inc(r_in, 16)
            sp.dma_start(consts[:], rows(dr["consts"], P)).then_inc(consts_in, 16)
            load_weights(sp, 0)
            load_weights(sp, 1)

        prepare(w[:].rearrange("p e c -> p (e c)")[:, 0:2 * NT * 2 * P], {"sync": first_loads})
        ph = [[pst(f"ph{u}{k}", [P, 512]) for k in range(2)] for u in range(2)]
        px = pst("px", [P, 512])
        pt = pst("pt", [P, nm * P])
        py = pst("py", [P, 512])
        block = ctx.enter_context(nc.Block())

        @block.sync
        def _(sp):
            for e in range(2, ne):
                sp.wait_ge(w_split, e - 1)
                load_weights(sp, e)
            sp.wait_ge(scattered, 16 * 2 * NT)

            def load(n, u, q):
                at = bass.ds(n * P, P)
                sp.dma_start(xb[u][:, 0:D], slots[at, 0:D]).then_inc(x_in[u], 16)
                sp.dma_start(xb[u][:, D:D + ROW - P], slots[at, P:ROW]).then_inc(x_in[u], 16)

            for n in range(R):
                load(n, n, 0)

            def reload(n, u, q):
                sp.wait_ge(y_sent[u], 16 * (q + 1))
                load(n + R, u, q + 1)

            pipelined(sp, NB - R, R, (0, reload))
            for u in range(R):
                sp.wait_ge(y_sent[u], 16 * len(range(u, NB, R)))
            for c in range(3):
                part = slice(c * NT // 3, (c + 1) * NT // 3)
                sp.dma_start(z[:, part], sums[0:2 * T, :].rearrange("(p t a) c -> p t a c", t=NT, a=2)[:, part]).then_inc(sums_in[c], 16)

        @block.gpsimd
        def _(pool):
            nc.gpsimd.memset(ones[:], 1.0)
            for a in range(2):
                nc.gpsimd.iota(xr[:, a, :, ROW - 1:ROW].bitcast(I32), pattern=[[2, NT]], base=a, channel_multiplier=2 * NT)
            nc.gpsimd.tensor_copy(xr[:, 1, :, 0:D], x[:]).then_inc(rows_marked, 1)
            pool.wait_ge(rows_copied, 1)
            pool.wait_ge(rows_marked, 1)
            pool.wait_ge(routed, 1)
            for t in range(NT):
                for a in range(2):
                    nc.gpsimd.indirect_dma_start(out=slots, out_offset=bass.IndirectOffsetOnAxis(ap=pos[:, a, t:t + 1], axis=0),
                                                 in_=xr[:, a, t, :], in_offset=None).then_inc(scattered, 16)

            def send(n, u, q):
                pool.wait_ge(y_out, NS + n + 2)
                pool.sem_inc(y_seen, 1)
                nc.gpsimd.indirect_dma_start(out=sums, out_offset=bass.IndirectOffsetOnAxis(ap=xb[u][:, ROW + DB - 1:ROW + DB].bitcast(I32), axis=0),
                                             in_=ys[u][:], in_offset=None).then_inc(y_sent[u], 16)

            pipelined(pool, NB, R, (0, send))

        @block.scalar
        def _(act):
            act.wait_ge(r_in, 16)
            nc.scalar.activation(rh[:], rst[:], ACT.Copy, scale=WS).then_inc(r_hi, 1)

            def split_weights(v, i):
                e_ = E * shared if type(i) is int and v + 2 * i == 0 else v + 2 * i - shared
                act.wait_ge(w_in[v], 16 * (i + 1))
                nc.scalar.activation(w[:, e_, 0:2 * nw], wst[v][:, 0:2 * nw], ACT.Copy, scale=WS)
                nc.scalar.activation(w[:, e_, O_2H:O_2L], wst[v][:, 2 * nw:], ACT.Copy, scale=WS).then_inc(w_hi, 1)

            def more_weights(n, u, q):
                if u % 2 and not (type(q) is int and q > 0):
                    split_weights(*((1, q) if u == 1 else (0, q + 1)))

            split_weights(0, 0)
            act.wait_ge(centred, 1)
            nc.scalar.activation(pr[:], lg[:], ACT.Exp).then_inc(exp_done, 1)
            nc.scalar.activation(xr[:, 0, :, 0:D], x[:], ACT.Copy).then_inc(rows_copied, 1)
            if not shared:
                for e in range(1, ne):
                    split_weights(e % 2, e // 2)

            def rows_hi(n, u, q):
                act.wait_ge(xt_done, n + 1)
                act.wait_ge(h_done, NS + n + 1)
                nc.scalar.activation(xsh[:, u % 2], px[:, 0:2 * P].rearrange("p (c q) -> p c q", c=2), ACT.Copy).then_inc(xh_done, 1)

            def silu_of(base):
                def silu(n, u, q):
                    v = u % 2
                    act.wait_ge(h_done, base + n + 1 + AHEAD)
                    if gated:
                        act.wait_ge(g_done, base + n + 1)
                        nc.scalar.activation(act_out[v][:], ph[v][0][:, 0:hid], ACT.Silu, scale=1.0 / WS).then_inc(silu_done, 1)
                    else:
                        act.wait_ge(t_done, base + n + 1)
                        nc.scalar.activation(g[v][:, 0:wcol], ph[v][0][:, 0:wcol], ACT.Silu, scale=1.0 / WS)
                        nc.scalar.activation(g[v][:, wcol:], ph[v][1][:, 0:wcol], ACT.Silu, scale=1.0 / WS).then_inc(g_done, 1)
                return silu

            def hidden_hi_of(base):
                def hidden_hi(n, u, q):
                    act.wait_ge(t_done, base + n + 1 + AHEAD)
                    act.wait_ge(y_done, base + n + 1)
                    nc.scalar.activation(gh[:, u % 2], pt[:].rearrange("p (m q) -> p m q", m=nm), ACT.Copy).then_inc(gh_done, 1)
                return hidden_hi

            if shared:
                pipelined(act, NS, 4, (2, silu_of(0)), (1, hidden_hi_of(0)), (0, more_weights))
            pipelined(act, NB, R, (3, rows_hi), (2, silu_of(NS)), (1, hidden_hi_of(NS)))

        @block.vector
        def _(dve):
            ch = Chain(dve, link)
            dve.sem_inc(g_done, AHEAD)
            for one in (y_out, gl_done, xl_done):
                dve.sem_inc(one, 1)
            dve.wait_ge(r_hi, 1)
            ch.link(nc.vector.scalar_tensor_tensor(rl[:], rst[:], WS, rh[:], ALU.mult, ALU.subtract))
            nc.vector.tensor_copy(rh[DB:P, 1, :], rl[DB:P, 1, :]).then_inc(r_ready, 1)

            def split_weights(v, i):
                e_ = E * shared if type(i) is int and v + 2 * i == 0 else v + 2 * i - shared
                dve.wait_ge(w_hi, v + 2 * i + 1)
                st = wst[v]
                nc.vector.scalar_tensor_tensor(w[:, e_, O_AL:O_2H], st[:, 0:nw], WS, w[:, e_, 0:nw], ALU.mult, ALU.subtract)
                nc.vector.scalar_tensor_tensor(w[DB:P, e_, O_B:O_AL], st[DB:P, nw:2 * nw], WS, w[DB:P, e_, O_B:O_AL], ALU.mult, ALU.subtract)
                nc.vector.scalar_tensor_tensor(w[:, e_, O_2L:COLS], st[:, 2 * nw:], WS, w[:, e_, O_2H:O_2L], ALU.mult, ALU.subtract).then_inc(w_split, 1)

            def more_weights(n, u, q):
                if u % 2 and not (type(q) is int and q > 0):
                    split_weights(*((1, q) if u == 1 else (0, q + 1)))

            split_weights(0, 0)
            dve.wait_ge(l_done, NT)
            nc.vector.tensor_scalar(lg[:].rearrange("p t e -> p (t e)"), ph[0][0][:, 0:NT * E], 1.0 / WS, None, ALU.mult).then_inc(l_out, 1)
            dve.wait_ge(l_out, 1)
            over = lambda a, n: a.rearrange("p (n a) -> p n a", a=1).to_broadcast([a.shape[0], a.shape[1], n])
            each = lambda a, n: a.rearrange("p (a n) -> p a n", a=1).to_broadcast([a.shape[0], n, a.shape[1]])
            TT, TR = nc.vector.tensor_tensor, nc.vector.tensor_reduce
            ch.link(TR(m[:], lg[:], AX, ALU.max))
            TT(lg[:], lg[:], over(m[:], E), ALU.subtract).then_inc(centred, 1)
            dve.wait_ge(exp_done, 1)
            ch.link(TR(m[:], pr[:], AX, ALU.add))
            ch.link(nc.vector.reciprocal(m[:], m[:]))
            ch.link(TT(pr[:], pr[:], over(m[:], E), ALU.mult))
            dve.wait_ge(consts_in, 16)
            order, blocks_of, block_no = consts[:, 0:E], consts[:, E:E + NT], consts[:, E + NT:]
            for mk, sel in ((m1, sel1), (m2, sel2)):
                ch.link(TR(mk[:], pr[:], AX, ALU.max))
                ch.link(TT(sel[:], pr[:], over(mk[:], E), ALU.is_ge))
                ch.link(TT(sel[:], sel[:], each(order, NT), ALU.mult))
                ch.link(TR(m[:], sel[:], AX, ALU.max))
                ch.link(TT(sel[:], sel[:], over(m[:], E), ALU.is_equal))
                if mk is m1:
                    ch.link(nc.vector.scalar_tensor_tensor(pr[:], sel[:], -2.0, pr[:], ALU.mult, ALU.add))
            TT(both[:].rearrange("p e t -> p t e"), sel1[:], sel2[:], ALU.add).then_inc(both_done, 1)
            ch.link(TT(rd[:], m1[:], m2[:], ALU.add))
            if shared:
                ch.link(nc.vector.tensor_scalar(rd[:], rd[:], 1e-20, None, ALU.add))
            ch.link(nc.vector.reciprocal(rd[:], rd[:]))
            dve.wait_ge(rows_marked, 1)
            for a, mk in ((0, m1), (1, m2)):
                nc.vector.scalar_tensor_tensor(xr[:, a, :, D], mk[:], 1.0 / WS, rd[:], ALU.mult, ALU.mult)
            dve.wait_ge(rank_done, 1)
            flat = lambda a: a[:].rearrange("p e t -> p (e t)")
            ch.link(nc.vector.tensor_copy(flat(tot), ph[0][1][:, 0:E * NT]))
            ch.link(nc.vector.tensor_tensor_scan(flat(incl), flat(ones), flat(tot), 0.0, ALU.mult, ALU.add))
            ch.link(TT(tot[:], incl[:], tot[:], ALU.subtract))
            ch.link(TT(cnt[:], incl[:, :, NT - 1], tot[:, :, 0], ALU.subtract))
            ch.link(TT(incl[:], over(cnt[:], NT), each(blocks_of, E), ALU.is_gt))
            ch.link(TR(nblk[:], incl[:], AX, ALU.add))
            ch.link(nc.vector.tensor_tensor_scan(iblk[:], ones[:, 0, 0:E], nblk[:], 0.0, ALU.mult, ALU.add))
            ch.link(TT(start[:], iblk[:], nblk[:], ALU.subtract))
            ch.link(nc.vector.scalar_tensor_tensor(start[:], start[:], float(P), tot[:, :, 0], ALU.mult, ALU.subtract))
            ch.link(TT(flat(rank), ph[0][0][:, 0:E * NT], flat(tot), ALU.add))
            ch.link(TT(rank[:], rank[:], over(start[:], NT), ALU.add))
            for a, sel in ((0, sel1), (1, sel2)):
                ch.link(TT(tmp[:], sel[:], rank[:].rearrange("p e t -> p t e"), ALU.mult))
                ch.link(TR(m[:], tmp[:], AX, ALU.add))
                ch.link(nc.vector.tensor_copy(pos[:, a, :], m[:]))
            nc.vector.engine_nop().then_inc(routed, 1)
            ch.link(TT(ebt[:], over(block_no[0:1], E), each(iblk[0:1, :], NB), ALU.is_ge))
            ch.link(TR(ebf[:], ebt[:], AX, ALU.add))
            ch.link(nc.vector.tensor_scalar(ebf[:], ebf[:], float(E - 1), None, ALU.min))
            nc.vector.tensor_copy(eb[:], ebf[:]).then_inc(table_done, 1)
            dve.wait_ge(rows_copied, 1)
            if not shared:
                for e in range(1, ne):
                    split_weights(e % 2, e // 2)

            def rows_lo(n, u, q):
                dve.wait_ge(xh_done, n + 1)
                dve.wait_ge(h_done, NS + n + 1)
                TT(xsl[:, u % 2], px[:, 0:2 * P].rearrange("p (c q) -> p c q", c=2), xsh[:, u % 2], ALU.subtract).then_inc(xl_done, 1)

            def gate_of(base):
                def gate(n, u, q):
                    v = u % 2
                    if gated:
                        dve.wait_ge(silu_done, base + n + 1)
                        dve.wait_ge(t_done, base + n + 1)
                        nc.vector.scalar_tensor_tensor(g[v][:], ph[v][1][:, 0:hid], 1.0 / WS, act_out[v][:], ALU.mult, ALU.mult).then_inc(g_done, 1)
                return gate

            def hidden_lo_of(base):
                def hidden_lo(n, u, q):
                    dve.wait_ge(gh_done, base + n + 1)
                    TT(gl[:, u % 2], pt[:].rearrange("p (m q) -> p m q", m=nm), gh[:, u % 2], ALU.subtract).then_inc(gl_done, 1)
                return hidden_lo

            def add_shared(n, u, q):
                dve.wait_ge(y_done, n + 1 + AHEAD)
                nc.vector.scalar_tensor_tensor(h[:, n, :], py[:, 0:D], 1.0 / WS, h[:, n, :], ALU.mult, ALU.add).then_inc(y_out, 1)

            def share(n, u, q):
                dve.wait_ge(y_done, NS + n + 1 + AHEAD)
                nc.vector.tensor_scalar(ys[u][:], py[:, 0:D], xb[u][:, ROW + DB - 2:ROW + DB - 1], None, ALU.mult).then_inc(y_out, 1)

            if shared:
                pipelined(dve, NS, 4, (2, gate_of(0)), (1, hidden_lo_of(0)), (0, add_shared), (0, more_weights))
            pipelined(dve, NB, R, (3, rows_lo), (2, gate_of(NS)), (1, hidden_lo_of(NS)), (0, share))
            for c in range(3):
                dve.wait_ge(sums_in[c], 16)
                part = slice(c * NT // 3, (c + 1) * NT // 3)
                ch.link(nc.vector.scalar_tensor_tensor(h[:, part, :], h[:, part, :], 1.0 if shared else 2.0, z[:, part, 0, :], ALU.mult, ALU.add))
                ch.link(TT(h[:, part, :], h[:, part, :], z[:, part, 1, :], ALU.add))

        @block.tensor
        def _(pe):
            for two in (h_done, t_done, y_done):
                pe.sem_inc(two, AHEAD)
            pe.wait_ge(r_ready, 1)

            for t in range(NT):
                five(nc, ph[0][0][:, t * E:(t + 1) * E], xh[:, :, t, :], xl[:, :, t, :], rh[:, 0, :], rl[:, 0, :], rh[:, 1, :]).then_inc(l_done, 1)
            pe.wait_ge(both_done, 1)
            cols = both[:].rearrange("p e t -> p (e t)")
            nc.tensor.matmul(ph[0][0][:, 0:E * NT], tri[:], cols, start=True, stop=True)
            nc.tensor.matmul(ph[0][1][:, 0:E * NT], ones16[:], cols, start=True, stop=True).then_inc(rank_done, 1)
            pe.wait_ge(routed, 1)

            sorted_rows = lambda n, v: (xsh[:, v], xsl[:, v])

            def first_of(base, parts, expert):
                def first(n, u, q):
                    v = u % 2
                    e = expert(n)
                    if parts is sorted_rows:
                        pe.wait_ge(xl_done, n + 2)
                    pe.wait_ge(g_done, base + n + 1)
                    for k in range(2):
                        c = k * wcol
                        ins = five(nc, ph[v][k][:, 0:wcol], *parts(n, v), w[:, e, c:c + wcol],
                                   w[:, e, O_AL + c:O_AL + c + wcol], w[:, e, O_B + c:O_B + c + wcol])
                    ins.then_inc(h_done, 1)
                return first

            def second_of(base, expert):
                def second(n, u, q):
                    v = u % 2
                    e = expert(n)
                    pe.wait_ge(gl_done, base + n + 2)
                    pe.wait_ge(y_out, base + n + 1)
                    for j, (a, o) in enumerate(((gh, O_2H), (gl, O_2H), (gh, O_2L))):
                        for k in range(nm):
                            ins = nc.tensor.matmul(py[:, 0:D], a[:, v, k, :], w[:, e, o + k * D:o + (k + 1) * D],
                                                   start=(j == 0 and k == 0), stop=(j == 2 and k == nm - 1))
                    ins.then_inc(y_done, 1)
                return second

            def turn_of(base):
                def turn(n, u, q):
                    v = u % 2
                    pe.wait_ge(g_done, base + n + 1 + AHEAD)
                    pe.wait_ge(gl_done, base + n + 1)
                    for k in range(nm):
                        ins = nc.tensor.transpose(pt[:, k * P:(k + 1) * P], g[v][:, k * P:(k + 1) * P], ident[:])
                    ins.then_inc(t_done, 1)
                return turn

            def rows_in(n, u, q):
                pe.wait_ge(x_in[u], 32 * (q + 1))
                pe.wait_ge(xl_done, n + 1)
                nc.tensor.transpose(px[:, 0:P], xb[u][:, 0:P], ident[:])
                nc.tensor.transpose(px[:, P:2 * P], xb[u][:, P:2 * P], ident[:]).then_inc(xt_done, 1)

            if shared:
                pe.wait_ge(w_split, 1)
                own = lambda n: E
                pipelined(pe, NS, 4, (2, first_of(0, lambda n, v: (xh[:, :, n, :], xl[:, :, n, :]), own)), (1, turn_of(0)), (0, second_of(0, own)))
            pe.wait_ge(w_split, ne)
            pe.wait_ge(table_done, 1)
            by_block = lambda n: pe.value_load(eb[0:1, bass.ds(n, 1)], min_val=0, max_val=E - 1)
            pipelined(pe, NB, R, (3, rows_in), (2, first_of(NS, sorted_rows, by_block)), (1, turn_of(NS)), (0, second_of(NS, by_block)))


def attention_weights(nc, dr, h, w, small, prepare):
    wqh, wql, wqb, woh, wol = w
    mask, isc, fold = small
    ctx = ExitStack()
    with ctx:
        sb, pst, sem = scope(nc, ctx, "aw_")
        wst, wost = sb("wst", [P, 2, 3 * INNER]), sb("wost", [P, NM * D])
        bout, mst = sb("bout", [P, D]), sb("mst", [2, (1 + H1 // 2) * PAIR])
        w_in, small_in, w_hi, isc_inv = (sem(n) for n in ("w_in", "small_in", "w_hi", "isc_inv"))

        def load(sp):
            sp.dma_start(bout[:], rows(dr["at_bout"], P)).then_inc(small_in, 16)
            sp.dma_start(mst[:], dr["at_mask"]).then_inc(small_in, 16)
            sp.dma_start(isc[:], dr["at_scale"]).then_inc(small_in, 16)
            sp.dma_start(fold[:], dr["at_fold"]).then_inc(small_in, 16)
            sp.dma_start(wst[:], dr["at_wqkv"]).then_inc(w_in, 16)
            sp.dma_start(wost[:], dr["at_wout"]).then_inc(w_in, 16)

        def hi(act):
            act.wait_ge(w_in, 32)
            nc.scalar.activation(wqh[:], wst[:, 0], ACT.Copy, scale=WS)
            nc.scalar.activation(wqb[:], wst[:, 1], ACT.Copy, scale=WS)
            nc.scalar.activation(woh[:], wost[:], ACT.Copy, scale=WS).then_inc(w_hi, 1)

        def lo(dve):
            dve.wait_ge(small_in, 64)
            nc.vector.tensor_copy(mask[:], mst[:])
            nc.vector.reciprocal(isc[:], isc[:]).then_inc(isc_inv, 1)
            dve.wait_ge(isc_inv, 1)
            nc.vector.tensor_scalar(isc[:], isc[:], 1.0 / WS, None, ALU.mult)
            dve.wait_ge(w_hi, 1)
            nc.vector.scalar_tensor_tensor(wql[:], wst[:, 0], WS, wqh[:], ALU.mult, ALU.subtract)
            nc.vector.scalar_tensor_tensor(wqb[DB:P], wst[DB:P, 1], WS, wqb[DB:P], ALU.mult, ALU.subtract)
            nc.vector.scalar_tensor_tensor(wol[:], wost[:], WS, woh[:], ALU.mult, ALU.subtract)

        def bias(pool, lo_done, lo_done_1):
            pool.wait_ge(small_in, 64)
            pool.wait_ge(lo_done, 3)
            pool.wait_ge(lo_done_1, 3)
            nc.gpsimd.tensor_tensor(h[:], h[:], bout[:].rearrange("p (a n) -> p a n", a=1).to_broadcast([P, NT, D]), ALU.add)

        prepare(None, {"sync": load, "scalar": hi, "vector": lo, "gpsimd": bias})


def attention(nc, dr, h, xh, xl, ident, slots, fill, prepare):
    ctx = ExitStack()
    with ctx:
        sb, pst, sem = scope(nc, ctx, "at_")
        GT = GP * PAIR
        NH = H1 // 2
        W6 = NH * PAIR
        HALF = INNER // 2
        wqh, wql, wqb = (sb(n, [P, 3 * INNER], F16) for n in ("wqh", "wql", "wqb"))
        woh, wol = sb("woh", [P, NM * D], F16), sb("wol", [P, NM * D], F16)
        mask, isc, fold = sb("mask", [2, PAIR + W6], BF16), sb("isc", [P, NM]), sb("fold", [P, P])
        attention_weights(nc, dr, h, (wqh, wql, wqb, woh, wol), (mask, isc, fold), prepare)
        oh, ol = sb("oh", [P, NM, NT, P], F16), sb("ol", [P, NM, NT, P], F16)
        xgh, xgl = sb("xgh", [P, 2, T], F16), sb("xgl", [P, 2, T], F16)
        qk = [sb(f"qk{u}", [P, 2 * NM, GT]) for u in range(2)]
        ss = [sb(f"ss{u}", [P, 2, GT]) for u in range(2)]
        sq = [sb(f"sq{u}", [P, GT]) for u in range(1, NM)]
        eps = sb("eps", [P, 1])
        qs = [sb(f"qs{u}", [P, 2 * NM, PAIR]) for u in range(2)]
        qsh, qsl = sb("qsh", [P, 2, 2 * NM, PAIR], F16), sb("qsl", [P, 2, 2 * NM, PAIR], F16)
        vh, vl = sb("vh", [PAIR, 2, INNER], F16), sb("vl", [PAIR, 2, INNER], F16)
        sm = [sb(f"sm{u}", [PAIR, 2, W6]) for u in range(2)]
        mx, rs = [[sb(f"{n}{u}", [PAIR, H1]) for u in range(2)] for n in ("mx", "rs")]
        ph, pl = sb("ph", [PAIR, 2, 2, W6], F16), sb("pl", [PAIR, 2, 2, W6], F16)
        pq = pst("pq", [P, 512])
        pss = pst("pss", [P, 2, 512])
        pv = pst("pv", [P, 2, 512])
        pt = pst("pt", [P, 2, 512])
        po = pst("po", [P, 512])
        pq_done, pq_out, sq_done, sq_used, root_done, rn_done, rn_ready = (sem(n) for n in (
            "pq_done", "pq_out", "sq_done", "sq_used", "root_done", "rn_done", "rn_ready"))
        USES = 2 * NM + 2
        qk_lo, s_done, t_done, o_done = (sem(n) for n in ("qk_lo", "s_done", "t_done", "o_done"))
        centred, v_lo, t_lo, o_lo = (sem(n) for n in ("centred", "v_lo", "t_lo", "o_lo"))
        scaled, qk_hi, mx_done, exp_done, rs_done, rs_inv, prob_done, v_done, v_hi, t_hi, o_hi = (sem(n) for n in (
            "scaled", "qk_hi", "mx_done", "exp_done", "rs_done", "rs_inv", "prob_done", "v_done", "v_hi", "t_hi", "o_hi"))
        eps_set, grouped, p_done, p_out, filled = (sem(n) for n in ("eps_set", "grouped", "p_done", "p_out", "filled"))
        block = ctx.enter_context(nc.Block())
        head = lambda hd: ((hd % 2) * DH, hd // 2)
        heads = lambda a: a.rearrange("p a (m n) -> p (a m) n", n=PAIR)
        over = lambda a: a[:].rearrange("p (n a) -> p n a", a=1).to_broadcast([PAIR, H1, PAIR])

        def use_of(u, place):
            k = 5 * (u % GP) + place
            return {12: 12, 14: 13}.get(k) if k >= 2 * NM else k

        first_group = lambda n: type(n) is int and n < GP

        def bank_of(n, k):
            return (pq, pss[:, 0], pv[:, 0], pt[:, 0])[k % 4] if first_group(n) else pq

        @block.sync
        def _(sp):
            clear_slots(sp, slots, fill, filled)
            sp.wait_ge(filled, 16 * RING)

        @block.tensor
        def _(pe):
            pe.wait_ge(grouped, 1)

            def ahead(place):
                def step(n, u, q):
                    k, g, v = use_of(u, place), 2 * q + u // GP, u // GP
                    if k is None:
                        return
                    to = bank_of(n, k)
                    if not first_group(n):
                        pe.wait_ge(pq_out, g * USES + k + 1)
                    elif k >= 4:
                        pe.wait_ge(pq_out, k - 2)
                    if k < 2 * NM:
                        c = slice(k * P, (k + 1) * P)
                        xs = [x[:, :, bass.ds(g * GT, GT)] for x in (xgh, xgl)]
                        five_t(nc, to[:, 0:GT], wqh[:, c], wql[:, c], wqb[:, c], *xs).then_inc(pq_done, 1)
                    else:
                        i = k - 2 * NM
                        pe.wait_ge(sq_used, g * 2 * NM + (i + 1) * NM + NM)
                        nc.tensor.matmul(to[:, 0:GT], fold[:], ss[v][:, i, :], start=True, stop=True).then_inc(pq_done, 1)
                return (7, step)

            def scores(n, u, q):
                v = u % 2
                pe.wait_ge(qk_lo, n + 1 + AHEAD)
                pe.wait_ge(centred, n + 1)
                for par in range(2):
                    nc.tensor.matmul(pss[0:PAIR, par, 0:W6], mask[:, 0:PAIR], mask[:, PAIR:], start=True, stop=False)
                for hd in range(H1):
                    o, m = head(hd)
                    for k, (a, b) in enumerate(((qsh, qsh), (qsl, qsh), (qsh, qsl))):
                        ins = nc.tensor.matmul(pss[0:PAIR, hd % 2, m * PAIR:(m + 1) * PAIR], a[o:o + DH, v, m, :], b[o:o + DH, v, NM + m, :],
                                               start=False, stop=(k == 2 and hd >= H1 - 2))
                ins.then_inc(s_done, 1)

            def values(half):
                def step(n, u, q):
                    if half == 0:
                        pe.wait_ge(v_lo, n + 1)
                    xs = [x[:, :, bass.ds(n * PAIR, PAIR)] for x in (xgh, xgl)]
                    c = slice(2 * INNER + half * HALF, 2 * INNER + (half + 1) * HALF)
                    ins = five(nc, pv[0:PAIR, half, 0:HALF], *xs, wqh[:, c], wql[:, c], wqb[:, c])
                    if half == 1:
                        ins.then_inc(v_done, 1)
                return (1, step)

            def turn(n, u, q):
                pe.wait_ge(prob_done, n + 1)
                pe.wait_ge(t_lo, n + 1)
                for hd in range(H1):
                    c = slice(hd // 2 * PAIR, (hd // 2 + 1) * PAIR)
                    ins = nc.tensor.transpose(pt[0:PAIR, hd % 2, c], sm[u % 2][:, hd % 2, c], ident[0:PAIR, 0:PAIR])
                ins.then_inc(t_done, 1)

            def mix(n, u, q):
                v = u % 2
                pe.wait_ge(t_lo, n + 2)
                pe.wait_ge(v_lo, n + 2)
                pe.wait_ge(o_lo, n + 1)
                for hd in range(H1):
                    o, m = head(hd)
                    for k, (a, b) in enumerate(((vh, ph), (vl, ph), (vh, pl))):
                        ins = nc.tensor.matmul(po[o:o + DH, m * PAIR:(m + 1) * PAIR], a[:, v, hd * DH:(hd + 1) * DH],
                                               b[:, v, hd % 2, m * PAIR:(m + 1) * PAIR], start=(k == 0), stop=(k == 2))
                ins.then_inc(o_done, 1)

            pipelined(pe, PAIRS, 2 * GP, ahead(0), (2, scores), ahead(1), values(0), ahead(2), values(1), ahead(3),
                      (1, turn), ahead(4), (0, mix))
            pe.wait_ge(o_hi, PAIRS)
            pe.wait_ge(o_lo, PAIRS + 1)

            def project(t, u, i):
                pe.wait_ge(p_out, t + 1)
                for k, (a, b) in enumerate(((oh, woh), (ol, woh), (oh, wol))):
                    for m in range(NM):
                        ins = nc.tensor.matmul(pv[:, u, 0:D], a[:, m, t, :], b[:, m * D:(m + 1) * D], start=(k == m == 0), stop=(k == 2 and m == NM - 1))
                ins.then_inc(p_done, 1)

            pairs(pe, NT, project)

        @block.scalar
        def _(act):
            act.sem_inc(pq_out, 1)

            def ahead(place):
                def step(n, u, q):
                    k, g, v = use_of(u, place), 2 * q + u // GP, u // GP
                    if k is None:
                        return
                    act.wait_ge(pq_done, g * USES + k + 1)
                    use = bank_of(n, k)[:, 0:GT]
                    if k < 2 * NM:
                        act.wait_ge(sq_used, g * 2 * NM + k + 1)
                        to = ss[v][:, k // NM, :] if k % NM == 0 else sq[k % NM - 1][:]
                        nc.scalar.activation(to, use, ACT.Square, scale=1.0 / WS).then_inc(sq_done, 1)
                        nc.scalar.activation(qk[v][:, k, :], use, ACT.Copy, scale=isc[:, k:k + 1] if k < NM else 1.0 / WS).then_inc(pq_out, 1)
                    else:
                        nc.scalar.activation(ss[v][:, k - 2 * NM, :], use, ACT.Copy).then_inc(pq_out, 1)
                return (7, step)

            def roots(n, u, q):
                if u % GP == GP - 1:
                    g, v = 2 * q + u // GP, u // GP
                    act.wait_ge(pq_out, (g + 1) * USES + 1)
                    nc.scalar.activation(ss[v][:], ss[v][:], ACT.Sqrt).then_inc(root_done, 1)
                    act.wait_ge(root_done, g + 1)
                    nc.scalar.activation(ss[v][:], ss[v][:], ACT.Sqrt, bias=eps[:]).then_inc(rn_done, 1)

            def scaled_hi(n, u, q):
                act.wait_ge(scaled, n + 1)
                act.wait_ge(s_done, n + 1)
                nc.scalar.activation(qsh[:, u % 2], qs[u % 2][:], ACT.Copy).then_inc(qk_hi, 1)

            def values_hi(n, u, q):
                act.wait_ge(v_done, n + 1)
                act.wait_ge(o_done, n + 1)
                nc.scalar.activation(vh[:, u % 2].rearrange("p (a n) -> p a n", a=2), pv[0:PAIR, :, 0:HALF], ACT.Copy, scale=1.0 / WS).then_inc(v_hi, 1)

            def exponentials(n, u, q):
                act.wait_ge(centred, n + 2)
                nc.scalar.activation(sm[u % 2][:], sm[u % 2][:], ACT.Exp).then_inc(exp_done, 1)

            def turned_hi(n, u, q):
                act.wait_ge(t_done, n + 1 + AHEAD)
                act.wait_ge(o_done, n + 1)
                nc.scalar.activation(ph[:, u % 2], pt[0:PAIR, :, 0:W6], ACT.Copy).then_inc(t_hi, 1)

            def mixed_hi(n, u, q):
                act.wait_ge(o_done, n + 1 + AHEAD)
                nc.scalar.activation(oh[:, :, :, bass.ds(n * 4, 4)], po[:, 0:W6].rearrange("p (m t q) -> p m t q", m=NM, q=4), ACT.Copy).then_inc(o_hi, 1)

            act.wait_ge(eps_set, 1)
            pipelined(act, PAIRS, 2 * GP, ahead(0), ahead(1), (7, roots), (3, scaled_hi), ahead(2),
                      (1, values_hi), ahead(3), (2, exponentials), (1, turned_hi), ahead(4), (0, mixed_hi))

        @block.vector
        def _(dve):
            dve.sem_inc(p_out, AHEAD)
            for one in (centred, v_lo, t_lo, o_lo):
                dve.sem_inc(one, 1)
            nc.vector.memset(eps[:], 1e-8).then_inc(eps_set, 1)
            for a, b in ((xgh, xh), (xgl, xl)):
                for c in range(2):
                    ins = nc.vector.tensor_copy(a[:, c, :].rearrange("f (s t q) -> f s t q", t=NT, q=4),
                                                b[:, c].rearrange("f t (s q) -> f s t q", q=4))
            ins.then_inc(grouped, 1)

            def roots(n, u, q):
                if u % GP == GP - 1:
                    g, v = 2 * q + u // GP, u // GP
                    dve.wait_ge(rn_done, g + 1)
                    nc.vector.reciprocal(ss[v][:], ss[v][:]).then_inc(rn_ready, 1)

            def scale(n, u, q):
                g, v, j = 2 * q + u // GP, u // GP, u % GP
                c = slice(j * PAIR, (j + 1) * PAIR)
                if j == 0:
                    dve.wait_ge(rn_ready, g + 1)
                dve.wait_ge(qk_lo, n + 1)
                for i in range(2):
                    m = slice(i * NM, (i + 1) * NM)
                    ins = nc.vector.tensor_tensor(qs[u % 2][:, m, :], qk[v][:, m, c], ss[v][:, i:i + 1, c].to_broadcast([P, NM, PAIR]), ALU.mult)
                ins.then_inc(scaled, 1)

            def centre(n, u, q):
                v = u % 2
                s = pss[0:PAIR, :, 0:W6].rearrange("p a (m n) -> p a m n", n=PAIR)
                dve.wait_ge(s_done, n + 1 + AHEAD)
                nc.vector.tensor_reduce(mx[v][:].rearrange("p (a m) -> p a m", a=2), s, AX, ALU.max).then_inc(mx_done, 1)
                dve.wait_ge(mx_done, n + 1)
                dve.wait_ge(t_done, n + 1)
                nc.vector.tensor_tensor(sm[v][:].rearrange("p a (m n) -> p a m n", n=PAIR), s,
                                        mx[v][:].rearrange("p (a m n) -> p a m n", a=2, n=1).to_broadcast([PAIR, 2, NH, PAIR]), ALU.subtract).then_inc(centred, 1)

            def values_lo(n, u, q):
                dve.wait_ge(v_hi, n + 1)
                two = lambda a: a.rearrange("p (a n) -> p a n", a=2)
                nc.vector.scalar_tensor_tensor(two(vl[:, u % 2]), pv[0:PAIR, :, 0:HALF], 1.0 / WS, two(vh[:, u % 2]), ALU.mult, ALU.subtract).then_inc(v_lo, 1)

            def sums(n, u, q):
                v = u % 2
                dve.wait_ge(exp_done, n + 1)
                nc.vector.tensor_reduce(rs[v][:], heads(sm[v][:]), AX, ALU.add).then_inc(rs_done, 1)
                dve.wait_ge(rs_done, n + 1)
                nc.vector.reciprocal(rs[v][:], rs[v][:]).then_inc(rs_inv, 1)

            def turned_lo(n, u, q):
                dve.wait_ge(t_hi, n + 1)
                nc.vector.tensor_tensor(pl[:, u % 2], pt[0:PAIR, :, 0:W6], ph[:, u % 2], ALU.subtract).then_inc(t_lo, 1)

            def mixed_lo(n, u, q):
                dve.wait_ge(o_hi, n + 1)
                at = bass.ds(n * 4, 4)
                nc.vector.tensor_tensor(ol[:, :, :, at], po[:, 0:W6].rearrange("p (m t q) -> p m t q", m=NM, q=4), oh[:, :, :, at], ALU.subtract).then_inc(o_lo, 1)

            pipelined(dve, PAIRS, 2 * GP, (3, scale), (2, centre), (7, roots), (1, values_lo), (2, sums), (1, turned_lo), (0, mixed_lo))

            def project(t, u, i):
                dve.wait_ge(p_done, t + 1)
                nc.vector.scalar_tensor_tensor(h[:, t, :], pv[:, u, 0:D], 1.0 / WS, h[:, t, :], ALU.mult, ALU.add).then_inc(p_out, 1)

            pairs(dve, NT, project)

        @block.gpsimd
        def _(pool):
            pool.sem_inc(sq_used, NM)
            for two in (qk_lo, s_done, t_done, o_done):
                pool.sem_inc(two, AHEAD)

            def ahead(n, u, q):
                g, v = 2 * q + u // GP, u // GP
                for k in range(5 * (u % GP), min(5 * (u % GP) + 5, 2 * NM)):
                    pool.wait_ge(sq_done, g * 2 * NM + k + 1)
                    pool.wait_ge(sq_used, g * 2 * NM + k + NM)
                    if k % NM == 0:
                        pool.sem_inc(sq_used, 1)
                    else:
                        to = ss[v][:, k // NM, :]
                        nc.gpsimd.tensor_tensor(to, to, sq[k % NM - 1][:], ALU.add).then_inc(sq_used, 1)

            def scaled_lo(n, u, q):
                pool.wait_ge(qk_hi, n + 1)
                nc.gpsimd.tensor_tensor(qsl[:, u % 2], qs[u % 2][:], qsh[:, u % 2], ALU.subtract).then_inc(qk_lo, 1)

            def probabilities(n, u, q):
                pool.wait_ge(rs_inv, n + 1)
                nc.gpsimd.tensor_tensor(heads(sm[u % 2][:]), heads(sm[u % 2][:]), over(rs[u % 2]), ALU.mult).then_inc(prob_done, 1)

            pipelined(pool, PAIRS, 2 * GP, (3, scaled_lo), (7, ahead), (2, probabilities))


def constants(nc, ident, ident16, tri, ones16, fill):
    with nc.semaphore("const_set") as const_set, nc.Block() as block:
        @block.gpsimd
        def _(pool):
            nc.gpsimd.memset(fill[:, :, 0:ROW - 1], 0.0)
            nc.gpsimd.iota(fill[:, :, ROW - 1:ROW].bitcast(I32), pattern=[[P, RING]], base=2 * T, channel_multiplier=1)
            nc.gpsimd.memset(ident[:], 0.0).then_inc(const_set, 1)
            nc.gpsimd.memset(ident16[:], 0.0).then_inc(const_set, 1)
            nc.gpsimd.memset(ones16[:], 1.0).then_inc(const_set, 1)
            pool.wait_ge(const_set, 3)
            for m in (ident, ident16):
                nc.gpsimd.affine_select(out=m[:], in_=m[:], compare_op=ALU.not_equal, fill=1.0, base=0,
                                        pattern=[[-1, P]], channel_multiplier=1)
            nc.gpsimd.affine_select(out=tri[:], in_=ones16[:], compare_op=ALU.is_gt, fill=0.0, base=0,
                                    pattern=[[1, P]], channel_multiplier=-1)


def recycle_semaphores(nc):
    nc.clear_and_free_semaphores(SPENT)
    SPENT.clear()
    nc.all_engine_barrier()


def build(nc, dr, out):
    SPENT.clear()
    with (nc.sbuf_tensor("h", [P, NT, D], F32) as h, nc.sbuf_tensor("ident", [P, P], F32) as ident,
          nc.sbuf_tensor("ident16", [P, P], F16) as ident16, ExitStack() as stack):
        tri = stack.enter_context(nc.sbuf_tensor("tri", [P, P], F16))
        ones16 = stack.enter_context(nc.sbuf_tensor("ones16", [P, P], F16))
        fill = stack.enter_context(nc.sbuf_tensor("fill", [P, RING, ROW], F32))
        constants(nc, ident, ident16, tri, ones16, fill)
        slots = nc.dram_tensor("slots", [NB * P, ROW], F32, kind="Internal").ap()
        sums = nc.dram_tensor("sums", [2 * T + RING * P, D], F32, kind="Internal").ap()
        xh = stack.enter_context(nc.sbuf_tensor("xh", [P, 2, NT, P], F16))
        xl = stack.enter_context(nc.sbuf_tensor("xl", [P, 2, NT, P], F16))
        split = xh, xl, ident16

        def ahead(tag, z, to, affine=None):
            return lambda room, beside: normalise(nc, z, to, tag, split, affine, room=room, beside=beside)

        patch_projection(nc, dr, h, ident)
        normalise(nc, None, h, "n0_", split)
        dynamic_convolution(nc, dr, h, xh, xl, ident, ones16, slots, fill)
        experts(nc, dr, h, h, xh, xl, (ident, tri, ones16), slots, sums, "f0_", HID0, True, 1, ahead("n1_", h, h))
        recycle_semaphores(nc)
        attention(nc, dr, h, xh, xl, ident, slots, fill, ahead("n2_", h, h))
        h2 = stack.enter_context(nc.sbuf_tensor("h2", [P, NT, D], F32))
        normalise(nc, h, h, "n3_")
        recycle_semaphores(nc)
        experts(nc, dr, h2, h, xh, xl, (ident, tri, ones16), slots, sums, "f1_", HID1, False, 0,
                ahead("n4_", h, h2, (dr["f1_gamma"], dr["f1_beta"])))
        normalise(nc, h, h, "n5_", out=out)


def pixel_rows():
    pix = []
    for c in range(C):
        for y in range(-1, PATCH + 1):
            for x in range(-1, PATCH + 1):
                if not (0 <= y < PATCH or 0 <= x < PATCH):
                    continue
                fs = []
                for s, (dy, dx) in enumerate(((0, 0), (0, 1), (0, -1), (1, 0), (-1, 0))):
                    py, px = y + dy, x + dx
                    inside = 0 <= py < PATCH and 0 <= px < PATCH
                    fs.append((py * PATCH + px) * SHIFTS * C + s * C + c if inside else PD)
                pix.append((sum(f < PD for f in fs), c, y, x, fs))
    pix.sort(key=lambda p: -p[0])
    return [p[1:4] for p in pix], np.array([p[4] for p in pix]).T, np.array([p[0] for p in pix])


def lay_out(inp):
    f = {k: np.asarray(v) for k, v in inp.items()}
    pix, feats, count = pixel_rows()
    assert [tuple(c) for c in CLASSES if c[0] < 5] == [(n, int((count == n).sum())) for n in (4, 3, 1)]
    xp = np.pad(f["x"], ((0, 0), (0, 0), (1, 1), (1, 1)))
    cols = np.empty((B, GRID, GRID, KR), np.float32)
    for r, (c, y, x) in enumerate(pix):
        cols[..., r] = xp[:, c, y + 1:y + 2 + IMG - PATCH:PATCH, x + 1:x + 2 + IMG - PATCH:PATCH]
    d = {"x": cols.reshape(P, NT, KR).transpose(1, 0, 2)}
    none = lambda a: np.concatenate([a, np.zeros(a.shape[:-1] + (1,), a.dtype)], -1)
    wt = none(f["L0_tok_proj_weight"])[:, feats]
    d["tok_w"] = wt.reshape(D, SHIFTS, NK, KC).transpose(3, 1, 2, 0)
    by_row = lambda a: none(a)[feats].reshape(SHIFTS * NK, KC).T
    d["tok_lnw"] = by_row(f["L0_tok_ln_weight"])
    d["tok_lnb"] = by_row(f["L0_tok_ln_bias"])
    d["tok_negmult"] = (-count / PD).astype(np.float32).reshape(NK, KC).T
    d["tok_class"] = np.array([[n, 1, n] * 2 for n, _ in CLASSES], np.float32).ravel()
    d["tok_b"] = f["L0_tok_proj_bias"]
    dw = f["L0_attn_dw_w"][:, 0]
    twice = lambda a: np.concatenate([a[P:], a[P:]])
    d["dc_dw"] = np.stack([dw[:P], twice(dw)], 1)
    d["dc_pwb"] = np.stack([f["L0_attn_pw_b"][:P], twice(f["L0_attn_pw_b"])], 1)
    d["dc_akb"], d["dc_ptb"] = f["L0_attn_ak_b"], f["L0_attn_pt_b"]
    pw, ak, pt = f["L0_attn_pw_w"], f["L0_attn_ak_w"], f["L0_attn_pt_w"].T
    w = np.zeros((P, 2 * P + 2 * HA * K + 2 * D), np.float32)
    heads_b = list(range(HA, H)) * 2
    for n in range(HA):
        r = slice(n * IPG, (n + 1) * IPG)
        for g, head in ((0, n), (1, heads_b[n])):
            w[r, g * P + n * IPG:g * P + (n + 1) * IPG] = pw[head].T
            w[r, 2 * P + (g * HA + n) * K:2 * P + (g * HA + n + 1) * K] = ak[head].T
    w[:, 2 * P + 2 * HA * K:2 * P + 2 * HA * K + D] = pt[:P]
    w[:, 2 * P + 2 * HA * K + D:] = np.concatenate([pt[P:], pt[P:]])
    d["dc_w"] = w
    wq = f["L1_attn_w_qkv"].T
    d["at_wqkv"] = np.stack([wq[:P], twice(wq)], 1)
    d["at_wout"] = f["L1_attn_w_out"].T.reshape(NM, P, D).transpose(1, 0, 2).reshape(P, NM * D)
    d["at_bout"] = f["L1_attn_b_out"]
    d["at_scale"] = np.repeat(f["L1_attn_scale"].reshape(NM, 2).T, DH, 0)
    d["at_fold"] = np.tile(np.eye(DH, dtype=np.float32), (2, 2))
    image = np.arange(PAIR) % 4 // 2
    own = (image == np.arange(2)[:, None]).astype(np.float32)
    d["at_mask"] = np.concatenate([own, np.tile((1 - own) * NEG, (1, H1 // 2))], 1).astype(np.float32)
    d["f1_gamma"], d["f1_beta"] = f["L1_ffn_ln_gamma"], f["L1_ffn_ln_beta"]
    d["consts"] = np.concatenate([np.arange(E, 0, -1), P * np.arange(NT), np.arange(NB)]).astype(np.float32)

    def router(r):
        return np.stack([r[:P], twice(r)], 1)

    def pack(first, second):
        return np.concatenate([first[:P], twice(first), second.reshape(-1, P, D).transpose(1, 0, 2).reshape(P, -1)], 1)

    d["f0_router"] = router(f["L0_ffn_gate_w"].T)
    d["f0_w"] = np.stack([pack(np.concatenate([a.T, c.T], 1), b.T) for a, b, c in
                          [(f["L0_ffn_w1"][e], f["L0_ffn_w2"][e], f["L0_ffn_w3"][e]) for e in range(E)]
                          + [(f["L0_ffn_ws1"], f["L0_ffn_ws2"], f["L0_ffn_ws3"])]])
    d["f1_router"] = router(f["L1_ffn_router_w"])
    d["f1_w"] = np.stack([pack(f["L1_ffn_w1"][e], f["L1_ffn_w2"][e]) for e in range(E)])
    return {k: np.ascontiguousarray(v) for k, v in d.items()}


def kernel(**inputs):
    import concourse.bacc as bacc
    from concourse.bass_utils import run_bass_kernel_spmd as run

    d = lay_out(inputs)
    nc = bacc.Bacc("TRN2", target_bir_lowering=False, num_devices=1)
    dr = {k: nc.dram_tensor("in_" + k, v.shape, mybir.dt.from_np(v.dtype), kind="ExternalInput").ap() for k, v in d.items()}
    out = nc.dram_tensor("out_h", [P, NT, D], F32, kind="ExternalOutput").ap()
    build(nc, dr, out)
    r = run(nc, [{"in_" + k: v for k, v in d.items()}], core_ids=[0])
    return np.asarray(r.results[0]["out_h"]).reshape(B, L, D)
```
